# Optimizing a Trainium2 kernel written in Bass

```python
import numpy as np
import jax
import jax.numpy as jnp

def _softmax(x, axis=-1):
    return jax.nn.softmax(x, axis=axis)

def _gelu(x):
    return jax.nn.gelu(x, approximate=True)

def _silu(x):
    return jax.nn.silu(x)

def _sigmoid(x):
    return jax.nn.sigmoid(x)

def _layernorm(x, axis=-1, eps=1e-05):
    m = jnp.mean(x, axis=axis, keepdims=True)
    v = jnp.var(x, axis=axis, keepdims=True)
    return (x - m) / jnp.sqrt(v + eps)

def _scatter_add(tgt, idx, src, axis=0):
    return tgt.at[idx].add(src)

def _segment_sum(src, seg, n):
    return jax.ops.segment_sum(src, seg, n)
kernel_name = 'mk_hybrid_d1_jaxref_r8_d302f4'

def setup_inputs(seed: int=0):
    np.random.seed(seed)
    _w = jnp.asarray

    def _L0_attn_a_setup():
        import jax, jax.numpy as jnp
        import numpy as np
        B_, L_, D_MODEL = (2, 256, 256)
        EXPAND = 2
        D_IN = EXPAND * D_MODEL
        HEADS = 64
        HEAD_DIM = D_IN // HEADS
        STATE = 128
        NGROUPS = 1
        K = 4
        CONV_DIM = D_IN + 2 * NGROUPS * STATE
        PROJ = D_IN + CONV_DIM + HEADS
        CHUNK = 32
        EPS = 1e-05

        def _segsum(x):
            T = x.shape[-1]
            c = jnp.cumsum(x, axis=-1)
            seg = c[..., :, None] - c[..., None, :]
            return jnp.where(jnp.tril(jnp.ones((T, T), bool)), seg, -jnp.inf)

        def _ssd(x, dA, Bm, Cm):
            b, l, h, p = x.shape
            n = Bm.shape[-1]
            c = l // CHUNK
            rep = h // Bm.shape[2]
            Bh = jnp.repeat(Bm, rep, axis=2).reshape(b, c, CHUNK, h, n)
            Ch = jnp.repeat(Cm, rep, axis=2).reshape(b, c, CHUNK, h, n)
            x = x.reshape(b, c, CHUNK, h, p)
            dA = dA.reshape(b, c, CHUNK, h).transpose(0, 3, 1, 2)
            dA_cum = jnp.cumsum(dA, axis=-1)
            Lmat = jnp.exp(_segsum(dA))
            Y_diag = jnp.einsum('bcthn,bcshn,bhcts,bcshp->bcthp', Ch, Bh, Lmat, x)
            decay_states = jnp.exp(dA_cum[..., -1:] - dA_cum)
            states = jnp.einsum('bcshn,bhcs,bcshp->bchpn', Bh, decay_states, x)
            chunk_decay = jnp.exp(_segsum(jnp.pad(dA_cum[..., -1], ((0, 0), (0, 0), (1, 0)))))
            states = jnp.concatenate([jnp.zeros_like(states[:, :1]), states], axis=1)
            prev = jnp.einsum('bhzc,bchpn->bzhpn', chunk_decay, states)[:, :-1]
            Y_off = jnp.einsum('bcthn,bchpn,bhct->bcthp', Ch, prev, jnp.exp(dA_cum))
            return (Y_diag + Y_off).reshape(b, l, h, p)
        key = jax.random.key(seed)
        ks = jax.random.split(key, 4)
        return {'hidden_states': jax.random.normal(ks[0], (B_, L_, D_MODEL), jnp.float32), 'in_proj_w': jax.random.normal(ks[1], (PROJ, D_MODEL), jnp.float32) * 0.02, 'conv_w': jax.random.normal(ks[2], (CONV_DIM, K), jnp.float32) * 0.2, 'conv_b': jnp.zeros((CONV_DIM,), jnp.float32), 'dt_bias': jnp.ones((HEADS,), jnp.float32), 'A_log': jnp.log(jnp.arange(1, HEADS + 1, dtype=jnp.float32)), 'D': jnp.ones((HEADS,), jnp.float32), 'norm_w': jnp.ones((D_IN,), jnp.float32), 'out_proj_w': jax.random.normal(ks[3], (D_MODEL, D_IN), jnp.float32) * 0.02}
    _L0_attn_a_in = _L0_attn_a_setup()

    def _L0_attn_b_setup():
        import jax, jax.numpy as jnp
        import numpy as np
        import math
        D = 256
        H = 32
        HKV = 8
        HD = D // H
        ROPE_BASE = 10000.0

        def _rope_cache(T, hd, base=ROPE_BASE):
            theta = 1.0 / base ** (jnp.arange(0, hd, 2, dtype=jnp.float32) / hd)
            t = jnp.arange(T, dtype=jnp.float32)
            freqs = t[:, None] * theta[None, :]
            return (jnp.cos(freqs), jnp.sin(freqs))

        def _apply_rope(x, cos, sin):
            B, Hh, T, hd = x.shape
            x_ = x.reshape(B, Hh, T, hd // 2, 2)
            x1, x2 = (x_[..., 0], x_[..., 1])
            c = cos[None, None, :, :]
            s = sin[None, None, :, :]
            rx1 = x1 * c - x2 * s
            rx2 = x1 * s + x2 * c
            return jnp.stack([rx1, rx2], axis=-1).reshape(B, Hh, T, hd)
        key = jax.random.key(seed)
        ks = jax.random.split(key, 5)
        B, T = (1, 256)
        sc = 0.02
        return {'x': jax.random.normal(ks[0], (B, T, D), dtype=jnp.float32), 'wq': jax.random.normal(ks[1], (D, D), dtype=jnp.float32) * sc, 'wk': jax.random.normal(ks[2], (HKV * HD, D), dtype=jnp.float32) * sc, 'wv': jax.random.normal(ks[3], (HKV * HD, D), dtype=jnp.float32) * sc, 'wo': jax.random.normal(ks[4], (D, D), dtype=jnp.float32) * sc}
    _L0_attn_b_in = _L0_attn_b_setup()

    def _L0_ffn_setup():
        import jax, jax.numpy as jnp
        import numpy as np
        E, H, I = (8, 256, 512)
        TOP_K = 1
        B, S = (1, 256)
        key = jax.random.key(seed)
        ks = jax.random.split(key, 7)
        std = 0.02
        return {'hidden_states': jax.random.normal(ks[0], (B, S, H), dtype=jnp.float32), 'router_w': jax.random.normal(ks[1], (E, H), dtype=jnp.float32) * std, 'gate_up_proj': jax.random.normal(ks[2], (E, H, 2 * I), dtype=jnp.float32) * std, 'down_proj': jax.random.normal(ks[3], (E, I, H), dtype=jnp.float32) * std, 'shared_gate_w': jax.random.normal(ks[4], (H, I), dtype=jnp.float32) * std, 'shared_up_w': jax.random.normal(ks[5], (H, I), dtype=jnp.float32) * std, 'shared_down_w': jax.random.normal(ks[6], (I, H), dtype=jnp.float32) * std}
    _L0_ffn_in = _L0_ffn_setup()
    _d = {'L0_attn_a_hidden_states': _L0_attn_a_in['hidden_states'], 'L0_attn_a_in_proj_w': _L0_attn_a_in['in_proj_w'], 'L0_attn_a_conv_w': _L0_attn_a_in['conv_w'], 'L0_attn_a_conv_b': _L0_attn_a_in['conv_b'], 'L0_attn_a_dt_bias': _L0_attn_a_in['dt_bias'], 'L0_attn_a_A_log': _L0_attn_a_in['A_log'], 'L0_attn_a_D': _L0_attn_a_in['D'], 'L0_attn_a_norm_w': _L0_attn_a_in['norm_w'], 'L0_attn_a_out_proj_w': _L0_attn_a_in['out_proj_w'], 'L0_attn_b_wq': _L0_attn_b_in['wq'], 'L0_attn_b_wk': _L0_attn_b_in['wk'], 'L0_attn_b_wv': _L0_attn_b_in['wv'], 'L0_attn_b_wo': _L0_attn_b_in['wo'], 'L0_ffn_router_w': _L0_ffn_in['router_w'], 'L0_ffn_gate_up_proj': _L0_ffn_in['gate_up_proj'], 'L0_ffn_down_proj': _L0_ffn_in['down_proj'], 'L0_ffn_shared_gate_w': _L0_ffn_in['shared_gate_w'], 'L0_ffn_shared_up_w': _L0_ffn_in['shared_up_w'], 'L0_ffn_shared_down_w': _L0_ffn_in['shared_down_w']}
    _x0 = _d['L0_attn_a_hidden_states']
    _d['L0_attn_a_hidden_states'] = jax.random.normal(jax.random.fold_in(jax.random.key(seed), 1), (4, 256, 256), dtype=_x0.dtype)
    del _x0
    return _d

def reference(L0_attn_a_hidden_states, L0_attn_a_in_proj_w, L0_attn_a_conv_w, L0_attn_a_conv_b, L0_attn_a_dt_bias, L0_attn_a_A_log, L0_attn_a_D, L0_attn_a_norm_w, L0_attn_a_out_proj_w, L0_attn_b_wq, L0_attn_b_wk, L0_attn_b_wv, L0_attn_b_wo, L0_ffn_router_w, L0_ffn_gate_up_proj, L0_ffn_down_proj, L0_ffn_shared_gate_w, L0_ffn_shared_up_w, L0_ffn_shared_down_w):

    def _L0_attn_a_ref(hidden_states, in_proj_w, conv_w, conv_b, dt_bias, A_log, D, norm_w, out_proj_w):
        import jax, jax.numpy as jnp
        import numpy as np
        B_, L_, D_MODEL = (2, 256, 256)
        EXPAND = 2
        D_IN = EXPAND * D_MODEL
        HEADS = 64
        HEAD_DIM = D_IN // HEADS
        STATE = 128
        NGROUPS = 1
        K = 4
        CONV_DIM = D_IN + 2 * NGROUPS * STATE
        PROJ = D_IN + CONV_DIM + HEADS
        CHUNK = 32
        EPS = 1e-05

        def _segsum(x):
            T = x.shape[-1]
            c = jnp.cumsum(x, axis=-1)
            seg = c[..., :, None] - c[..., None, :]
            return jnp.where(jnp.tril(jnp.ones((T, T), bool)), seg, -jnp.inf)

        def _ssd(x, dA, Bm, Cm):
            b, l, h, p = x.shape
            n = Bm.shape[-1]
            c = l // CHUNK
            rep = h // Bm.shape[2]
            Bh = jnp.repeat(Bm, rep, axis=2).reshape(b, c, CHUNK, h, n)
            Ch = jnp.repeat(Cm, rep, axis=2).reshape(b, c, CHUNK, h, n)
            x = x.reshape(b, c, CHUNK, h, p)
            dA = dA.reshape(b, c, CHUNK, h).transpose(0, 3, 1, 2)
            dA_cum = jnp.cumsum(dA, axis=-1)
            Lmat = jnp.exp(_segsum(dA))
            Y_diag = jnp.einsum('bcthn,bcshn,bhcts,bcshp->bcthp', Ch, Bh, Lmat, x)
            decay_states = jnp.exp(dA_cum[..., -1:] - dA_cum)
            states = jnp.einsum('bcshn,bhcs,bcshp->bchpn', Bh, decay_states, x)
            chunk_decay = jnp.exp(_segsum(jnp.pad(dA_cum[..., -1], ((0, 0), (0, 0), (1, 0)))))
            states = jnp.concatenate([jnp.zeros_like(states[:, :1]), states], axis=1)
            prev = jnp.einsum('bhzc,bchpn->bzhpn', chunk_decay, states)[:, :-1]
            Y_off = jnp.einsum('bcthn,bchpn,bhct->bcthp', Ch, prev, jnp.exp(dA_cum))
            return (Y_diag + Y_off).reshape(b, l, h, p)
        b, l, _ = hidden_states.shape
        proj = hidden_states @ in_proj_w.T
        gate = proj[..., :D_IN]
        xBC = proj[..., D_IN:D_IN + CONV_DIM]
        dt = proj[..., D_IN + CONV_DIM:]
        xp = jnp.pad(xBC, ((0, 0), (K - 1, 0), (0, 0)))
        conv = conv_b + sum((conv_w[:, i] * xp[:, i:i + l, :] for i in range(K)))
        xBC = jax.nn.silu(conv)
        x = xBC[..., :D_IN].reshape(b, l, HEADS, HEAD_DIM)
        Bm = xBC[..., D_IN:D_IN + NGROUPS * STATE].reshape(b, l, NGROUPS, STATE)
        Cm = xBC[..., D_IN + NGROUPS * STATE:].reshape(b, l, NGROUPS, STATE)
        dt = jax.nn.softplus(dt + dt_bias)
        A = -jnp.exp(A_log)
        y = _ssd(x * dt[..., None], dt * A, Bm, Cm)
        y = y + D[None, None, :, None] * x
        y = y.reshape(b, l, D_IN)
        hg = y * jax.nn.silu(gate)
        var = jnp.mean(hg * hg, axis=-1, keepdims=True)
        y = hg * jax.lax.rsqrt(var + EPS) * norm_w
        return y @ out_proj_w.T

    def _L0_attn_b_ref(x, wq, wk, wv, wo):
        import jax, jax.numpy as jnp
        import numpy as np
        import math
        D = 256
        H = 32
        HKV = 8
        HD = D // H
        ROPE_BASE = 10000.0

        def _rope_cache(T, hd, base=ROPE_BASE):
            theta = 1.0 / base ** (jnp.arange(0, hd, 2, dtype=jnp.float32) / hd)
            t = jnp.arange(T, dtype=jnp.float32)
            freqs = t[:, None] * theta[None, :]
            return (jnp.cos(freqs), jnp.sin(freqs))

        def _apply_rope(x, cos, sin):
            B, Hh, T, hd = x.shape
            x_ = x.reshape(B, Hh, T, hd // 2, 2)
            x1, x2 = (x_[..., 0], x_[..., 1])
            c = cos[None, None, :, :]
            s = sin[None, None, :, :]
            rx1 = x1 * c - x2 * s
            rx2 = x1 * s + x2 * c
            return jnp.stack([rx1, rx2], axis=-1).reshape(B, Hh, T, hd)
        B, T, _ = x.shape
        q = (x @ wq.T).reshape(B, T, H, HD).transpose(0, 2, 1, 3)
        k = (x @ wk.T).reshape(B, T, HKV, HD).transpose(0, 2, 1, 3)
        v = (x @ wv.T).reshape(B, T, HKV, HD).transpose(0, 2, 1, 3)
        cos, sin = _rope_cache(T, HD)
        q = _apply_rope(q, cos, sin)
        k = _apply_rope(k, cos, sin)
        rep = H // HKV
        k = jnp.repeat(k, rep, axis=1)
        v = jnp.repeat(v, rep, axis=1)
        scores = jnp.einsum('bhtd,bhsd->bhts', q, k) / math.sqrt(HD)
        mask = jnp.triu(jnp.full((T, T), -jnp.inf, dtype=scores.dtype), k=1)
        scores = scores + mask[None, None, :, :]
        attn = jax.nn.softmax(scores, axis=-1)
        y = jnp.einsum('bhts,bhsd->bhtd', attn, v)
        y = y.transpose(0, 2, 1, 3).reshape(B, T, D)
        return y @ wo.T

    def _L0_ffn_ref(hidden_states, router_w, gate_up_proj, down_proj, shared_gate_w, shared_up_w, shared_down_w):
        import jax, jax.numpy as jnp
        import numpy as np
        E, H, I = (8, 256, 512)
        TOP_K = 1
        B, S = (1, 256)
        orig_shape = hidden_states.shape
        x = hidden_states.reshape(-1, H)
        T = x.shape[0]
        logits = x @ router_w.T
        top_vals, top_idx = jax.lax.top_k(logits, TOP_K)
        scores = jnp.full_like(logits, -jnp.inf)
        scores = scores.at[jnp.arange(T)[:, None], top_idx].set(top_vals)
        scores = jax.nn.sigmoid(scores.astype(jnp.float32)).astype(logits.dtype)
        xr = x[None, :, :] * scores.T[:, :, None]
        gate_up = jnp.einsum('eth,ehf->etf', xr, gate_up_proj)
        gate, up = jnp.split(gate_up, 2, axis=-1)
        routed = jnp.einsum('etf,efh->eth', up * jax.nn.silu(gate), down_proj)
        routed_sum = routed.sum(axis=0)
        shared = jax.nn.silu(x @ shared_gate_w) * (x @ shared_up_w) @ shared_down_w
        return (shared + routed_sum).reshape(orig_shape)
    x = L0_attn_a_hidden_states
    x = x + _L0_attn_a_ref(_layernorm(x, axis=-1), L0_attn_a_in_proj_w, L0_attn_a_conv_w, L0_attn_a_conv_b, L0_attn_a_dt_bias, L0_attn_a_A_log, L0_attn_a_D, L0_attn_a_norm_w, L0_attn_a_out_proj_w)
    x = x + _L0_ffn_ref(_layernorm(x, axis=-1), L0_ffn_router_w, L0_ffn_gate_up_proj, L0_ffn_down_proj, L0_ffn_shared_gate_w, L0_ffn_shared_up_w, L0_ffn_shared_down_w)
    x = x + _L0_attn_b_ref(_layernorm(x, axis=-1), L0_attn_b_wq, L0_attn_b_wk, L0_attn_b_wv, L0_attn_b_wo)
    x = x + _L0_ffn_ref(_layernorm(x, axis=-1), L0_ffn_router_w, L0_ffn_gate_up_proj, L0_ffn_down_proj, L0_ffn_shared_gate_w, L0_ffn_shared_up_w, L0_ffn_shared_down_w)
    return x

_drawn_inputs = setup_inputs


def setup_inputs(seed=0):
    import zlib

    import numpy as np

    out = dict(_drawn_inputs(seed))
    spreads = {'L0_attn_a_conv_b': (0.0, 0.1),
     'L0_attn_a_dt_bias': (1.0, 0.6),
     'L0_attn_a_D': (1.0, 0.2),
     'L0_attn_a_norm_w': (1.0, 0.2)}
    factors = {'L0_attn_a_A_log': 8.0,
     'L0_attn_b_wq': 8.0,
     'L0_attn_b_wk': 8.0,
     'L0_attn_b_wv': 3.699,
     'L0_attn_b_wo': 3.74,
     'L0_ffn_router_w': 3.608,
     'L0_ffn_gate_up_proj': 3.375,
     'L0_ffn_down_proj': 3.368}
    for name, (base, spread) in spreads.items():
        noise = np.random.default_rng([zlib.crc32(name.encode()), seed]).standard_normal(out[name].shape)
        drawn = base * np.exp(spread * noise) if base else spread * noise
        out[name] = jnp.asarray(drawn.astype(out[name].dtype))
    for name, factor in factors.items():
        out[name] = (out[name] * factor).astype(out[name].dtype)
    return out
```

```python
from contextlib import ExitStack

import concourse.bass as bass
from concourse import mybir
from concourse.alu_op_type import AluOpType as ALU

F32 = mybir.dt.float32
BF16 = mybir.dt.bfloat16
I32 = mybir.dt.int32
U32 = mybir.dt.uint32
ACT = mybir.ActivationFunctionType
AX = mybir.AxisListType

P = 128
B, L, D = 4, 256, 256
TOK = B * L
NT = TOK // P
KD = D // P
EPS = 1e-5
E, FI = 8, 512
KF = FI // P
SHARED = E
NR = NT + E - 1
NJ = NT + NR


class Steps:

    def __init__(self):
        self.n = 0

    def step(self):
        self.n += 1
        return 1


def ffn_stage(nc, x, W, tag, load_behind=None):
    with ExitStack() as ctx:
        def sb(name, shape, dt=F32):
            return ctx.enter_context(nc.sbuf_tensor(tag + name, shape, dt))

        def ps(name, shape, dt=F32):
            return ctx.enter_context(nc.psum_tensor(tag + name, shape, dt))

        def sem(name):
            return ctx.enter_context(nc.semaphore(tag + name))

        C = W["consts"]
        stats = sb("stats", [P, NT, 6])
        meanvar = sb("meanvar", [P, NT, 2])
        rstd = sb("rstd", [P, NT])
        vareps = sb("vareps", [P, NT])
        xn = sb("xn", [P, NT, D])
        xscaled = sb("xscaled", [P, NT, D])
        xnT = sb("xnT", [P, KD, TOK])
        logitT = sb("logitT", [E, TOK])
        logit = sb("logit", [P, NT, E])
        top = sb("top", [P, NT])
        score = sb("score", [P, NT])
        tmp = sb("tmp", [P, E * E])
        first = sb("first", [P, NT])
        onehot = sb("onehot", [P, NT, E])
        before = sb("before", [P, NT + 1, E])
        counts = sb("counts", [P, NT, E])
        tiles_of = sb("tiles_of", [P, E])
        tile_end = sb("tile_end", [P, E])
        base = sb("base", [P, E])
        rank = sb("rank", [P, NT, E])
        slotf = sb("slotf", [P, NT])
        slot = sb("slot", [P, NT], U32)
        expf = sb("expf", [1, NR])
        expert = sb("expert", [1, NR], I32)
        cmp = sb("cmp", [1, NR, E])
        xg = [sb(f"xg{i}", [P, D]) for i in range(2)]
        xgT = [sb(f"xgT{i}", [P, KD, P]) for i in range(2)]
        sg = [sb(f"sg{i}", [P, FI]) for i in range(2)]
        h = [sb(f"h{i}", [P, FI]) for i in range(2)]
        hT = [sb(f"hT{i}", [P, KF, P]) for i in range(2)]
        yout = [sb(f"yout{i}", [P, D]) for i in range(2)]
        yback = sb("yback", [P, NT, D])

        gu = [ps(f"gu{i}", [P, 2 * FI]) for i in range(2)]
        pt = ps("pt", [P, KF * P])
        pd = [ps(f"pd{i}", [P, 512]) for i in range(2)]
        px = ps("px", [P, 512])

        dve_done = sem("dve_done")
        var_ready = sem("var_ready")
        rstd_ready = sem("rstd_ready")
        xn_ready = sem("xn_ready")
        xnT_in_psum = sem("xnT_in_psum")
        xnT_ready = sem("xnT_ready")
        logitT_in_psum = sem("logitT_in_psum")
        logitT_ready = sem("logitT_ready")
        logit_in_psum = sem("logit_in_psum")
        top_ready = sem("top_ready")
        score_ready = sem("score_ready")
        onehot_ready = sem("onehot_ready")
        ranks_in_psum = sem("ranks_in_psum")
        route_ready = sem("route_ready")
        scattered = sem("scattered")
        gathered = [sem(f"gathered{t}") for t in range(NT)]
        xg_loaded = [sem(f"xg_loaded{i}") for i in range(2)]
        xgT_in_psum = sem("xgT_in_psum")
        xgT_ready = sem("xgT_ready")
        gu_ready = sem("gu_ready")
        silu_ready = sem("silu_ready")
        h_ready = sem("h_ready")
        hT_in_psum = sem("hT_in_psum")
        hT_ready = sem("hT_ready")
        y_in_psum = sem("y_in_psum")
        y_taken = sem("y_taken")
        y_stored = [sem(f"y_stored{i}") for i in range(2)]

        slots_x = W["slots_x"]
        slots_y = W["slots_y"]
        block = ctx.enter_context(nc.Block())

        LOOP = range(NT + 4, NJ - 1)
        assert len(LOOP) % 2 == 0

        def steps(eng, step):
            for j in range(0, LOOP.start):
                step(j, j % 2, j)
            with eng.Fori(0, len(LOOP) // 2) as i:
                for u in range(2):
                    step(2 * i + (LOOP.start + u), u, LOOP.start + u)
            for j in range(LOOP.stop, NJ + 2):
                step(j, j % 2, j)

        @block.sync
        def _(sp):
            def load(r):
                sp.dma_start(xg[r % 2][:, :], slots_x[r * P:(r + 1) * P, :]).then_inc(xg_loaded[r % 2], 16)

            if load_behind:
                load_behind(sp)
            sp.wait_ge(scattered, 16 * NT)
            for r in range(2):
                load(r)
            for r in range(NR + 3):
                if r + 2 < NR:
                    sp.wait_ge(xgT_in_psum, r + 1)
                    load(r + 2)
                if r >= 3:
                    q = r - 3
                    sp.wait_ge(y_taken, NT + q + 1)
                    sp.dma_start(slots_y[q * P:(q + 1) * P, :], yout[q % 2][:, :]).then_inc(y_stored[q % 2], 16)

        @block.gpsimd
        def _(pool):
            pool.wait_ge(var_ready, 1)
            pool.tensor_tensor(rstd[:, :], vareps[:, :], C["minus_half"], ALU.pow).then_inc(rstd_ready, 1)
            for t in range(NT):
                pool.wait_ge(route_ready, 2 + t)
                pool.indirect_dma_start(out=slots_x, out_offset=bass.IndirectOffsetOnAxis(ap=slot[:, t:t + 1], axis=0),
                                        in_=xscaled[:, t, :], in_offset=None).then_inc(scattered, 16)
            pool.wait_ge(y_stored[0], 16 * ((NR + 1) // 2))
            pool.wait_ge(y_stored[1], 16 * (NR // 2))
            for t in range(NT):
                pool.indirect_dma_start(out=yback[:, t, :], out_offset=None, in_=slots_y,
                                        in_offset=bass.IndirectOffsetOnAxis(ap=slot[:, t:t + 1], axis=0)).then_inc(gathered[t], 16)

        @block.vector
        def _(dve):
            own = Steps()
            for t in range(NT):
                dve.bn_stats(stats[:, t, :], x[:, t, :]).then_inc(dve_done, own.step())
            dve.wait_ge(dve_done, own.n)
            for t in range(NT):
                dve.bn_aggr(meanvar[:, t, :], stats[:, t, :]).then_inc(dve_done, own.step())
            dve.wait_ge(dve_done, own.n)
            dve.tensor_scalar(vareps[:, :], meanvar[:, :, 1], EPS, None, ALU.add).then_inc(var_ready, 1)
            dve.wait_ge(rstd_ready, 1)
            for t in range(NT):
                dve.tensor_scalar(xn[:, t, :], x[:, t, :], meanvar[:, t, 0:1], rstd[:, t:t + 1],
                                  ALU.subtract, ALU.mult).then_inc(xn_ready, 1)
            dve.wait_ge(logitT_in_psum, 1)
            dve.tensor_copy(logitT[:, :], gu[1][0:E, :]).then_inc(logitT_ready, 1)
            dve.wait_ge(logit_in_psum, 1)
            dve.tensor_copy(logit[:, :, :], px[:, 0:NT * E].rearrange("p (t e) -> p t e", e=E)).then_inc(dve_done, own.step())
            dve.wait_ge(dve_done, own.n)
            dve.tensor_reduce(top[:, :], logit[:, :, :], AX.X, ALU.max).then_inc(top_ready, 1)
            dve.wait_ge(top_ready, 1)
            t3 = tmp[:, :].rearrange("p (t e) -> p t e", e=E)
            dve.tensor_tensor(onehot[:, :, :], logit[:, :, :], top[:, :].unsqueeze(2).broadcast_to([P, NT, E]), ALU.is_ge).then_inc(dve_done, own.step())
            dve.wait_ge(dve_done, own.n)
            dve.tensor_tensor(t3, onehot[:, :, :], C["weigh"], ALU.mult).then_inc(dve_done, own.step())
            dve.wait_ge(dve_done, own.n)
            dve.tensor_reduce(first[:, :], t3, AX.X, ALU.max).then_inc(dve_done, own.step())
            dve.wait_ge(dve_done, own.n)
            dve.tensor_tensor(onehot[:, :, :], t3, first[:, :].unsqueeze(2).broadcast_to([P, NT, E]), ALU.is_equal).then_inc(onehot_ready, 1)
            dve.wait_ge(onehot_ready, 1)
            dve.wait_ge(ranks_in_psum, 1)
            pr = pd[0]
            dve.tensor_copy(rank[:, :, :], pr[:, 0:NT * E].rearrange("p (t e) -> p t e", e=E)).then_inc(dve_done, own.step())
            dve.tensor_copy(counts[:, :, :], pr[:, NT * E:2 * NT * E].rearrange("p (t e) -> p t e", e=E)).then_inc(dve_done, own.step())
            dve.memset(before[:, 0, :], 0.0).then_inc(dve_done, own.step())
            for t in range(NT):
                dve.wait_ge(dve_done, own.n)
                dve.tensor_tensor(before[:, t + 1, :], before[:, t, :], counts[:, t, :], ALU.add).then_inc(dve_done, own.step())
            dve.wait_ge(dve_done, own.n)
            dve.tensor_tensor(t3, before[:, NT, :].unsqueeze(2).broadcast_to([P, E, NT]), C["steps"], ALU.is_gt).then_inc(dve_done, own.step())
            dve.wait_ge(dve_done, own.n)
            dve.tensor_reduce(tiles_of[:, :], t3, AX.X, ALU.add).then_inc(dve_done, own.step())
            dve.wait_ge(dve_done, own.n)
            dve.tensor_tensor(t3, tiles_of[:, :].unsqueeze(1).broadcast_to([P, E, E]), C["upto"], ALU.mult).then_inc(dve_done, own.step())
            dve.wait_ge(dve_done, own.n)
            dve.tensor_reduce(tile_end[:, :], t3, AX.X, ALU.add).then_inc(dve_done, own.step())
            dve.wait_ge(dve_done, own.n)
            dve.tensor_tensor(base[:, :], tile_end[:, :], tiles_of[:, :], ALU.subtract).then_inc(dve_done, own.step())
            dve.tensor_tensor(rank[:, :, :], rank[:, :, :], before[:, 0:NT, :], ALU.add).then_inc(dve_done, own.step())
            dve.tensor_tensor(cmp[:, :, :], tile_end[0:1, :].unsqueeze(1).broadcast_to([1, NR, E]), C["tile_no"], ALU.is_le).then_inc(dve_done, own.step())
            dve.wait_ge(dve_done, own.n)
            dve.scalar_tensor_tensor(t3, base[:, :].unsqueeze(1).broadcast_to([P, NT, E]), float(P), rank[:, :, :], ALU.mult, ALU.add).then_inc(dve_done, own.step())
            dve.tensor_reduce(expf[:, :], cmp[:, :, :], AX.X, ALU.add).then_inc(dve_done, own.step())
            dve.wait_ge(dve_done, own.n)
            dve.tensor_tensor(rank[:, :, :], t3, onehot[:, :, :], ALU.mult).then_inc(dve_done, own.step())
            dve.tensor_scalar(expert[:, :], expf[:, :], float(E - 1), None, ALU.min).then_inc(dve_done, own.step())
            dve.wait_ge(dve_done, own.n)
            dve.tensor_reduce(slotf[:, :], rank[:, :, :], AX.X, ALU.add).then_inc(dve_done, own.step())
            dve.wait_ge(dve_done, own.n)
            dve.tensor_copy(slot[:, :], slotf[:, :]).then_inc(route_ready, 1)
            dve.wait_ge(score_ready, 1)
            for t in range(NT):
                dve.tensor_scalar(xscaled[:, t, :], xn[:, t, :], score[:, t:t + 1], None, ALU.mult).then_inc(route_ready, 1)

            def step(j, u, jn):
                if NT <= jn + 1 < NJ:
                    r1 = j + 1 - NT
                    dve.wait_ge(xgT_in_psum, r1 + 1)
                    dve.wait_ge(gu_ready, j)
                    dve.tensor_copy(xgT[(u + 1) % 2][:, :, :], px[:, 0:D].rearrange("p (k n) -> p k n", k=KD)).then_inc(xgT_ready, 1)
                if jn < NJ:
                    dve.wait_ge(silu_ready, j + 1)
                    if jn >= 2:
                        dve.wait_ge(hT_in_psum, j - 1)
                    dve.tensor_tensor(h[u][:, :], sg[u][:, :], gu[u][:, FI:], ALU.mult).then_inc(h_ready, 1)
                if jn >= 2:
                    dve.wait_ge(y_in_psum, j - 1)
                    if jn - 2 < NT:
                        dve.tensor_tensor(x[:, jn - 2, :], x[:, jn - 2, :], pd[u][:, 0:D], ALU.add).then_inc(y_taken, 1)
                    else:
                        if jn - 2 >= NT + 2:
                            dve.wait_ge(y_stored[u], 8 * (j - (2 + NT + u)))
                        dve.tensor_copy(yout[u][:, :], pd[u][:, 0:D]).then_inc(y_taken, 1)

            steps(dve, step)
            for t in range(NT):
                dve.wait_ge(gathered[t], 16)
                dve.tensor_tensor(x[:, t, :], x[:, t, :], yback[:, t, :], ALU.add)

        @block.scalar
        def _(act):
            for g in range(NT // 2):
                act.wait_ge(xnT_in_psum, g + 1)
                act.activation(xnT[:, :, 2 * g * P:2 * (g + 1) * P], gu[0][:, (g % 2) * 512:(g % 2) * 512 + 512].rearrange("p (k n) -> p k n", k=KD),
                               ACT.Copy).then_inc(xnT_ready, 1)
            act.wait_ge(top_ready, 1)
            act.activation(score[:, :], top[:, :], ACT.Sigmoid).then_inc(score_ready, 1)

            def step(j, u, jn):
                if jn < NJ:
                    act.wait_ge(gu_ready, j + 1)
                    if jn >= 2:
                        act.wait_ge(h_ready, j - 1)
                    act.activation(sg[u][:, :], gu[u][:, 0:FI], ACT.Silu).then_inc(silu_ready, 1)
                if 1 <= jn <= NJ:
                    act.wait_ge(hT_in_psum, j)
                    if jn >= 3:
                        act.wait_ge(y_in_psum, j - 2)
                    act.activation(hT[(u + 1) % 2][:, :, :], pt[:, :].rearrange("p (k n) -> p k n", k=KF), ACT.Copy).then_inc(hT_ready, 1)

            steps(act, step)

        @block.tensor
        def _(pe):
            ident = C["ident"]
            for t in range(NT):
                g, r = t // 2, t % 2
                if r == 0 and g >= 2:
                    pe.wait_ge(xnT_ready, g - 1)
                pe.wait_ge(xn_ready, t + 1)
                for k in range(KD):
                    mm = pe.transpose(gu[0][:, (g % 2) * 512 + k * 256 + r * P:(g % 2) * 512 + k * 256 + (r + 1) * P], xn[:, t, k * P:(k + 1) * P], ident)
                if r == 1:
                    mm.then_inc(xnT_in_psum, 1)
            for half in range(2):
                pe.wait_ge(xnT_ready, 2 * (half + 1))
                for k in range(KD):
                    mm = pe.matmul(gu[1][0:E, half * 512:(half + 1) * 512], W["router"][:, k, :], xnT[:, k, half * 512:(half + 1) * 512],
                                   start=(k == 0), stop=(k == KD - 1))
            mm.then_inc(logitT_in_psum, 1)
            pe.wait_ge(logitT_ready, 1)
            for t in range(NT):
                mm = pe.transpose(px[:, t * E:(t + 1) * E], logitT[:, t * P:(t + 1) * P], ident[0:E, 0:E])
            mm.then_inc(logit_in_psum, 1)

            def ranks():
                pe.wait_ge(onehot_ready, 1)
                oh = onehot[:, :, :].rearrange("p t e -> p (t e)")
                pe.matmul(pd[0][:, 0:NT * E], C["below"], oh, start=True, stop=True)
                pe.matmul(pd[0][:, NT * E:2 * NT * E], C["ones"], oh, start=True, stop=True).then_inc(ranks_in_psum, 1)

            def step(j, u, jn):
                if NT <= jn + 1 < NJ:
                    v = (u + 1) % 2
                    pe.wait_ge(xg_loaded[v], 8 * (j + (3 - NT - v)))
                    if jn >= NT:
                        pe.wait_ge(xgT_ready, j + 1 - NT)
                    for k in range(KD):
                        mm = pe.transpose(px[:, k * P:(k + 1) * P], xg[v][:, k * P:(k + 1) * P], ident)
                    mm.then_inc(xgT_in_psum, 1)
                if jn < NJ:
                    if jn < NT:
                        e = SHARED
                        pe.wait_ge(xnT_ready, jn // 2 + 1)
                    else:
                        pe.wait_ge(xgT_ready, j - NT + 1)
                        e = pe.value_load(expert[0:1, bass.ds(j - NT, 1)], min_val=0, max_val=E - 1)
                    if jn >= 2:
                        pe.wait_ge(h_ready, j - 1)
                    for half in range(2):
                        for k in range(KD):
                            lhsT = xnT[:, k, jn * P:(jn + 1) * P] if jn < NT else xgT[u][:, k, :]
                            rhs = W["gate_up"][:, bass.ds(e, 1), k, half * FI:(half + 1) * FI]
                            mm = pe.matmul(gu[u][:, half * FI:(half + 1) * FI], lhsT, rhs.rearrange("p a n -> p (a n)"), start=(k == 0), stop=(k == KD - 1))
                    mm.then_inc(gu_ready, 1)
                if jn >= 2:
                    pe.wait_ge(hT_ready, j - 1)
                    if jn == 2 or jn == 2 + NT:
                        pe.wait_ge(W["down_loads"][0 if jn == 2 else 1], 16)
                    if jn >= 4:
                        pe.wait_ge(y_taken, j - 3)
                    e = SHARED if jn - 2 < NT else pe.value_load(expert[0:1, bass.ds(j - 2 - NT, 1)], min_val=0, max_val=E - 1)
                    for k in range(KF):
                        mm = pe.matmul(pd[u][:, 0:D], hT[u][:, k, :], W["down"][:, bass.ds(e, 1), k, :].rearrange("p a n -> p (a n)"),
                                       start=(k == 0), stop=(k == KF - 1))
                    mm.then_inc(y_in_psum, 1)
                if 1 <= jn <= NJ:
                    pe.wait_ge(h_ready, j)
                    for k in range(KF):
                        mm = pe.transpose(pt[:, k * P:(k + 1) * P], h[(u + 1) % 2][:, k * P:(k + 1) * P], ident)
                    mm.then_inc(hT_in_psum, 1)
                if jn == 0:
                    ranks()

            steps(pe, step)



H, HKV, HD = 32, 8, 8
G, HALF, REP = HKV // 2, 2, H // HKV
TS = L // P
ROWS = 64
TYPES = 6
QKV = (H + 2 * HKV) * HD
QK = (H + HKV) * HD


def attention_stage(nc, x, W, tag):
    with ExitStack() as ctx:
        def sb(name, shape, dt=F32):
            return ctx.enter_context(nc.sbuf_tensor(tag + name, shape, dt))

        def ps(name, shape, dt=F32):
            return ctx.enter_context(nc.psum_tensor(tag + name, shape, dt))

        def sem(name):
            return ctx.enter_context(nc.semaphore(tag + name))

        C = W["consts"]
        stats = sb("stats", [P, TS, 6])
        meanvar = sb("meanvar", [P, TS, 2])
        rstd = sb("rstd", [P, TS])
        vareps = sb("vareps", [P, TS])
        xn = sb("xn", [P, TS, D])
        xnT = sb("xnT", [P, KD, L])
        ropeA = sb("ropeA", [P, QK])
        ropeB = sb("ropeB", [P, QK])
        parts = sb("parts", [P, 3, QK], BF16)
        qs = sb("qs", [P, TS, H, ROWS], BF16)
        ks = sb("ks", [P, TS, HKV, ROWS], BF16)
        qTa = sb("qTa", [P, G * REP, L], BF16)
        qTb = [sb(f"qTb{i}", [P, G, REP, L], BF16) for i in range(2)]
        kz = [sb(f"kz{i}", [P, G, HALF, L], BF16) for i in range(2)]
        V = [sb(f"V{i}", [P, TS, HKV, 32]) for i in range(2)]
        top = sb("top", [P, TS, H])
        rest = sb("rest", [P, H])
        probs = [sb(f"probs{i}", [P, 2 * 512]) for i in range(2)]
        oT = sb("oT", [P, REP, P])
        recip = sb("recip", [P, REP, 4])
        y = sb("y", [P, TS, HKV, REP, HD])
        yT = sb("yT", [P, KD, P])
        identb = sb("identb", [P, P], BF16)
        hide = sb("hide", [P, HALF, P], BF16)

        sT = [ps(f"sT{i}", [P, 2 * 512]) for i in range(2)]
        po = ps("po", [P, 512])
        pf = [ps(f"pf{i}", [P, 512]) for i in range(2)]
        ot = ps("ot", [P, 512])

        dve_done = sem("dve_done")
        var_ready = sem("var_ready")
        rstd_ready = sem("rstd_ready")
        xn_ready = sem("xn_ready")
        front_in_psum = sem("front_in_psum")
        front_taken = sem("front_taken")
        parts_ready = sem("parts_ready")
        q1_copied = sem("q1_copied")
        rows_ready = sem("rows_ready")
        max_rows_ready = sem("max_rows_ready")
        scores_ready = sem("scores_ready")
        probs_ready = sem("probs_ready")
        pv_done = sem("pv_done")
        oT_in_psum = sem("oT_in_psum")
        oT_ready = sem("oT_ready")
        o_in_psum = sem("o_in_psum")
        y_ready = sem("y_ready")
        yT_in_psum = sem("yT_in_psum")
        yT_ready = sem("yT_ready")
        wo_in_psum = sem("wo_in_psum")
        x_ready = sem("x_ready")

        FRONT = ([("xnT", t, 0) for t in range(TS)] + [("qkv", t, 0) for t in range(TS)]
                 + [(kind, t, n) for t in range(TS) for kind, n in (("kT", 0), ("qTa", 0), ("qTa", 1))]
                 + [("max0", 0, n) for n in range(G * REP // 2)] + [("max1", 1, n) for n in range(G * REP)]
                 + [("qTb", t, n) for t in range(TS) for n in range(2)])
        NF = len(FRONT)
        UNITS = [(tt, kv) for tt in range(TS) for kv in range(HKV)]
        NU = len(UNITS)
        LAST = 4
        PIECES = [[] for _ in range(NU)]
        for n in range(NF):
            PIECES[min(NU - 1, n * NU // NF)].append(n)

        def slots():
            yield from ((-1, s, PIECES[s]) for s in range(NU))
            for b in range(B):
                for s in range(NU + (LAST if b == B - 1 else 0)):
                    yield b, s, PIECES[s] if b < B - 1 and s < NU else []

        def unit(b, s):
            return b * NU + s

        block = ctx.enter_context(nc.Block())

        @block.gpsimd
        def _(pool):
            for b, s, pieces in slots():
                for n in pieces:
                    if FRONT[n][:2] == ("xnT", 0):
                        pool.wait_ge(var_ready, b + 2)
                        pool.tensor_tensor(rstd[:, :], vareps[:, :], C["minus_half"][:, 0:TS], ALU.pow).then_inc(rstd_ready, 1)

        @block.vector
        def _(dve):
            own = Steps()
            dve.tensor_copy(identb[:, :], C["ident"]).then_inc(dve_done, own.step())
            dve.tensor_copy(hide[:, :, :], C["hide"].unsqueeze(1).broadcast_to([P, HALF, P])).then_inc(dve_done, own.step())
            dve.memset(qs[:, :, :, :], 0.0).then_inc(dve_done, own.step())
            dve.memset(ks[:, :, :, :], 0.0).then_inc(dve_done, own.step())
            for i in range(2):
                dve.memset(kz[i][:, :, :, :], 0.0).then_inc(dve_done, own.step())
                dve.memset(V[i][:, :, :, :], 0.0).then_inc(dve_done, own.step())
            dve.wait_ge(dve_done, own.n)
            dve.memset(ks[:, :, :, TYPES * HD:TYPES * HD + 3], 1.0).then_inc(dve_done, own.step())
            for i in range(2):
                dve.memset(V[i][:, :, :, HD:HD + 1], 1.0).then_inc(dve_done, own.step())
            dve.wait_ge(dve_done, own.n)

            def front(b, n):
                kind, t, m = FRONT[n]
                src = pf[n % 2]
                seen = NF * b + n + 1
                if (kind, t) == ("xnT", 0):
                    for q in range(TS):
                        dve.bn_stats(stats[:, q, :], x[:, TS * b + q, :]).then_inc(dve_done, own.step())
                    dve.wait_ge(dve_done, own.n)
                    for q in range(TS):
                        dve.bn_aggr(meanvar[:, q, :], stats[:, q, :]).then_inc(dve_done, own.step())
                    dve.wait_ge(dve_done, own.n)
                    dve.tensor_scalar(vareps[:, :], meanvar[:, :, 1], EPS, None, ALU.add).then_inc(var_ready, 1)
                    dve.wait_ge(rstd_ready, b + 1)
                    for q in range(TS):
                        dve.tensor_scalar(xn[:, q, :], x[:, TS * b + q, :], meanvar[:, q, 0:1], rstd[:, q:q + 1],
                                          ALU.subtract, ALU.mult).then_inc(xn_ready, 1)
                dve.wait_ge(front_in_psum, seen)
                if kind == "xnT":
                    dve.tensor_copy(xnT[:, :, t * P:(t + 1) * P], src[:, 0:KD * P].rearrange("p (k n) -> p k n", k=KD)).then_inc(front_taken, 1)
                if kind == "qkv":
                    cosT, sinT = C["cos"][:, t, :], C["sin"][:, t, :]
                    qk = src[:, 0:QK].rearrange("p (h j) -> p h j", j=2)
                    sn = sinT.rearrange("p (h j) -> p h j", j=2)
                    rb = ropeB[:, :].rearrange("p (h j) -> p h j", j=2)
                    dve.tensor_tensor(ropeA[:, :], src[:, 0:QK], cosT, ALU.mult).then_inc(dve_done, own.step())
                    dve.tensor_tensor(rb[:, :, 0], qk[:, :, 1], sn[:, :, 0], ALU.mult).then_inc(dve_done, own.step())
                    dve.tensor_tensor(rb[:, :, 1], qk[:, :, 0], sn[:, :, 1], ALU.mult).then_inc(dve_done, own.step())
                    if b >= 2:
                        dve.wait_ge(pv_done, unit(b - 1, 0))
                    dve.wait_ge(dve_done, own.n)
                    dve.tensor_copy(V[b % 2][:, t, :, 0:HD], src[:, QK:QKV].rearrange("p (h d) -> p h d", d=HD)).then_inc(front_taken, 1)
                    dve.tensor_tensor(ropeA[:, :], ropeA[:, :], ropeB[:, :], ALU.add).then_inc(dve_done, own.step())
                    dve.wait_ge(dve_done, own.n)
                    if TS * b + t >= 1:
                        dve.wait_ge(q1_copied, TS * b + t)
                    dve.tensor_copy(parts[:, 0, :], ropeA[:, :]).then_inc(dve_done, own.step())
                    dve.wait_ge(dve_done, own.n)
                    dve.tensor_tensor(ropeB[:, :], ropeA[:, :], parts[:, 0, :], ALU.subtract).then_inc(dve_done, own.step())
                    dve.wait_ge(dve_done, own.n)
                    dve.tensor_copy(parts[:, 1, :], ropeB[:, :]).then_inc(dve_done, own.step())
                    dve.wait_ge(dve_done, own.n)
                    dve.tensor_tensor(parts[:, 2, :], ropeB[:, :], parts[:, 1, :], ALU.subtract).then_inc(parts_ready, 1)
                    dve.wait_ge(parts_ready, TS * b + t + 1)
                    q2 = parts[:, 1, 0:H * HD].rearrange("p (h d) -> p h d", d=HD).unsqueeze(2).broadcast_to([P, H, 2, HD])
                    dve.tensor_copy(qs[:, t, :, 3 * HD:5 * HD].rearrange("p h (r d) -> p h r d", d=HD), q2).then_inc(dve_done, own.step())
                    dve.tensor_copy(qs[:, t, :, 5 * HD:6 * HD], parts[:, 2, 0:H * HD].rearrange("p (h d) -> p h d", d=HD)).then_inc(dve_done, own.step())
                    dve.memset(qs[:, t, :, TYPES * HD:TYPES * HD + 3], 0.0).then_inc(dve_done, own.step())
                    kp = parts[:, :, H * HD:QK].rearrange("p r (h d) -> p h r d", d=HD)
                    dve.tensor_copy(ks[:, t, :, 0:3 * HD].rearrange("p h (r d) -> p h r d", d=HD), kp).then_inc(dve_done, own.step())
                    dve.tensor_copy(ks[:, t, :, 3 * HD:5 * HD].rearrange("p h (r d) -> p h r d", d=HD), kp[:, :, 0:2, :]).then_inc(dve_done, own.step())
                    dve.tensor_copy(ks[:, t, :, 5 * HD:6 * HD], kp[:, :, 0, :]).then_inc(rows_ready, 1)
                if kind == "kT":
                    if b >= 2:
                        dve.wait_ge(scores_ready, unit(b - 1, 0))
                    kT = src[:, 0:G * P // 2].bitcast(BF16).rearrange("p (g n) -> p g n", g=G)
                    dve.tensor_copy(kz[b % 2][0:ROWS, :, 0, t * P:(t + 1) * P], kT[0:ROWS]).then_inc(dve_done, own.step())
                    dve.tensor_copy(kz[b % 2][ROWS:P, :, 1, t * P:(t + 1) * P], kT[ROWS:P]).then_inc(front_taken, 1)
                if kind in ("qTa", "qTb"):
                    if kind == "qTb" and b >= 2:
                        dve.wait_ge(scores_ready, unit(b - 1, 0))
                    dst = qTa if kind == "qTa" else qTb[b % 2][:, :, :, :].rearrange("p g i n -> p (g i) n")
                    dve.tensor_copy(dst[:, 8 * m:8 * m + 8, t * P:(t + 1) * P], src[:, :].bitcast(BF16).rearrange("p (g n) -> p g n", g=8)).then_inc(front_taken, 1)
                if kind == "max0":
                    dve.tensor_reduce(top[:, 0, 4 * m:4 * m + 4], src[:, :].rearrange("p (h s) -> p h s", h=4), AX.X, ALU.max).then_inc(front_taken, 1)
                if kind == "max1":
                    dve.tensor_reduce(top[:, 1, 2 * m:2 * m + 2], src[:, :].rearrange("p (h s) -> p h s", h=2), AX.X, ALU.max).then_inc(front_taken, 1)
                if (kind == "max0" and m == G * REP // 2 - 1) or (kind == "max1" and m == G * REP - 1):
                    at = TYPES * HD
                    dve.wait_ge(front_taken, seen)
                    dve.tensor_scalar(qs[:, t, :, at], top[:, t, :], -1.0, None, ALU.mult).then_inc(dve_done, own.step())
                    dve.wait_ge(dve_done, own.n)
                    dve.scalar_tensor_tensor(rest[:, :], top[:, t, :], -1.0, qs[:, t, :, at], ALU.mult, ALU.subtract).then_inc(dve_done, own.step())
                    dve.wait_ge(dve_done, own.n)
                    dve.tensor_copy(qs[:, t, :, at + 1], rest[:, :]).then_inc(dve_done, own.step())
                    dve.wait_ge(dve_done, own.n)
                    dve.tensor_tensor(qs[:, t, :, at + 2], rest[:, :], qs[:, t, :, at + 1], ALU.subtract).then_inc(max_rows_ready, 1)

            def tail(u):
                if u % 4 == 1 and u >= 5:
                    q = u // 4 - 1
                    t = q // 2
                    pot = ot[:, :].rearrange("p (i k r) -> p i k r", i=REP, k=4)
                    dve.wait_ge(o_in_psum, q + 1)
                    dve.reciprocal(recip[:, :, :], pot[:, :, :, HD]).then_inc(dve_done, own.step())
                    dve.wait_ge(dve_done, own.n)
                    for k in range(4):
                        ins = dve.tensor_tensor(y[:, t % TS, 4 * (q % 2) + k, :, :], pot[:, :, k, 0:HD],
                                                recip[:, :, k].unsqueeze(2).broadcast_to([P, REP, HD]), ALU.mult)
                        if k < 3:
                            ins.then_inc(dve_done, own.step())
                    ins.then_inc(y_ready, 1)
                if u % 8 == 2 and u >= 10:
                    t = u // 8 - 1
                    dve.wait_ge(yT_in_psum, t + 1)
                    dve.tensor_copy(yT[:, :, :], ot[:, 0:KD * P].rearrange("p (k n) -> p k n", k=KD)).then_inc(yT_ready, 1)
                if u % 8 == 3 and u >= 11:
                    t = u // 8 - 1
                    dve.wait_ge(wo_in_psum, t + 1)
                    dve.tensor_tensor(x[:, t, :], x[:, t, :], ot[:, 0:D], ALU.add).then_inc(x_ready, 1)

            for b, s, pieces in slots():
                for n in pieces:
                    front(b + 1, n)
                if b >= 0:
                    tail(unit(b, s))

        @block.scalar
        def _(act):
            for b, s, pieces in slots():
                if b >= 0 and s < NU:
                    u = unit(b, s)
                    tt = UNITS[s][0]
                    act.wait_ge(scores_ready, u + 1)
                    if u >= 2:
                        act.wait_ge(pv_done, u - 1)
                    act.activation(probs[u % 2][:, 0:(tt + 1) * 512], sT[u % 2][:, 0:(tt + 1) * 512], ACT.Exp).then_inc(probs_ready, 1)
                for n in pieces:
                    kind, t, m = FRONT[n]
                    if kind == "qkv":
                        act.wait_ge(parts_ready, TS * (b + 1) + t + 1)
                        if b + 1 >= 1:
                            act.wait_ge(front_in_psum, NF * (b + 1))
                        q1 = parts[:, 0, 0:H * HD].rearrange("p (h d) -> p h d", d=HD).unsqueeze(2).broadcast_to([P, H, 3, HD])
                        act.activation(qs[:, t, :, 0:3 * HD].rearrange("p h (r d) -> p h r d", d=HD), q1, ACT.Copy).then_inc(q1_copied, 1)
                u = unit(b, s)
                if b >= 0 and u % 4 == 0 and u >= 4:
                    q = u // 4 - 1
                    act.wait_ge(pv_done, u)
                    if q >= 1:
                        act.wait_ge(o_in_psum, q)
                    act.activation(oT[:, :, :], po[:, :].rearrange("p (i t) -> p i t", i=REP), ACT.Copy).then_inc(oT_ready, 1)

        @block.tensor
        def _(pe):
            ident = C["ident"]
            pe.wait_ge(dve_done, 11)

            def front(b, n):
                kind, t, m = FRONT[n]
                dst = pf[n % 2]
                seen = NF * b + n
                if seen >= 2:
                    pe.wait_ge(front_taken, seen - 1)
                if kind == "xnT":
                    pe.wait_ge(xn_ready, TS * b + t + 1)
                    for k in range(KD):
                        mm = pe.transpose(dst[:, k * P:(k + 1) * P], xn[:, t, k * P:(k + 1) * P], ident)
                if kind == "qkv":
                    pe.wait_ge(front_taken, NF * b + t + 1)
                    for k in range(KD):
                        mm = pe.matmul(dst[:, 0:QKV], xnT[:, k, t * P:(t + 1) * P], W["qkv"][:, k, :], start=(k == 0), stop=(k == KD - 1))
                if kind == "kT":
                    pe.wait_ge(rows_ready, TS * b + t + 1)
                    out = dst[:, 0:G * P // 2].bitcast(BF16)
                    for g in range(G):
                        mm = pe.transpose(out[:, g * P:(g + 1) * P], ks[:, t, 2 * g:2 * g + 2, :].rearrange("p h r -> p (h r)"), identb[:, :])
                if kind in ("qTa", "qTb"):
                    if kind == "qTa":
                        pe.wait_ge(rows_ready, TS * b + t + 1)
                        pe.wait_ge(q1_copied, TS * b + t + 1)
                    else:
                        pe.wait_ge(max_rows_ready, TS * b + t + 1)
                    out = dst[:, :].bitcast(BF16)
                    for g in range(8):
                        w = 8 * m + g
                        mm = pe.transpose(out[:, g * P:(g + 1) * P], qs[:, t, 2 * w:2 * w + 2, :].rearrange("p h r -> p (h r)"), identb[:, :])
                if kind == "max0":
                    if m == 0:
                        pe.wait_ge(front_taken, NF * b + FRONT.index(("qTa", 1, 1)) + 1)
                    for w in range(2):
                        pair = 2 * m + w
                        out = dst[:, w * 256:(w + 1) * 256]
                        pe.matmul(out, qTa[:, pair, 0:P], kz[b % 2][:, pair // REP, :, 0:P], start=True, stop=False)
                        mm = pe.matmul(out, identb[:, :], hide[:, :, :], start=False, stop=True)
                if kind == "max1":
                    pe.matmul(dst[:, :], qTa[:, m, P:2 * P], kz[b % 2][:, m // REP, :, :], start=True, stop=False)
                    mm = pe.matmul(dst[:, :].rearrange("p (h s) -> p h s", h=2)[:, :, P:2 * P], identb[:, :], hide[:, :, :], start=False, stop=True)
                mm.then_inc(front_in_psum, 1)

            def scores(b, s):
                u = unit(b, s)
                tt, kv = UNITS[s]
                if s == 0:
                    pe.wait_ge(front_taken, NF * (b + 1))
                if u >= 2:
                    pe.wait_ge(probs_ready, u - 1)
                for sbk in range(tt + 1):
                    pe.matmul(sT[u % 2][:, sbk * 512:(sbk + 1) * 512], kz[b % 2][:, kv // 2, kv % 2, sbk * P:(sbk + 1) * P],
                                   qTb[b % 2][:, kv // 2, :, tt * P:(tt + 1) * P], start=True, stop=(sbk < tt))
                pe.matmul(sT[u % 2][:, tt * 512:(tt + 1) * 512], hide[:, 0, :], identb[:, :].unsqueeze(1).broadcast_to([P, REP, P]),
                          start=False, stop=True).then_inc(scores_ready, 1)

            def weigh(u):
                b, s = u // NU, u % NU
                tt, kv = UNITS[s]
                pe.wait_ge(probs_ready, u + 1)
                if u % 4 == 0 and u >= 4:
                    pe.wait_ge(oT_ready, u // 4)
                rows = po[32 * (kv % 4):32 * (kv % 4) + 32, :]
                for sbk in range(tt + 1):
                    mm = pe.matmul(rows, V[b % 2][:, sbk, kv, :], probs[u % 2][:, sbk * 512:(sbk + 1) * 512], start=(sbk == 0), stop=(sbk == tt))
                mm.then_inc(pv_done, 1)

            def tail(u):
                if u % 4 == 1 and u >= 5:
                    q = u // 4 - 1
                    pe.wait_ge(oT_ready, q + 1)
                    if q >= 2 and q % 2 == 0:
                        pe.wait_ge(x_ready, q // 2)
                    if q % 2 == 1:
                        pe.wait_ge(y_ready, q)
                    for i in range(REP):
                        mm = pe.transpose(ot[:, i * P:(i + 1) * P], oT[:, i, :], ident)
                    mm.then_inc(o_in_psum, 1)
                if u % 8 == 2 and u >= 10:
                    t = u // 8 - 1
                    pe.wait_ge(y_ready, 2 * t + 2)
                    flat = y[:, t % TS, :, :, :].rearrange("p h i d -> p (h i d)")
                    for k in range(KD):
                        mm = pe.transpose(ot[:, k * P:(k + 1) * P], flat[:, k * P:(k + 1) * P], ident)
                    mm.then_inc(yT_in_psum, 1)
                if u % 8 == 3 and u >= 11:
                    t = u // 8 - 1
                    pe.wait_ge(yT_ready, t + 1)
                    for k in range(KD):
                        mm = pe.matmul(ot[:, 0:D], yT[:, k, :], W["wo"][:, k, :], start=(k == 0), stop=(k == KD - 1))
                    mm.then_inc(wo_in_psum, 1)

            for b, s, pieces in slots():
                if b >= 0 and s < NU:
                    scores(b, s)
                for n in pieces:
                    front(b + 1, n)
                if b >= 0:
                    u = unit(b, s)
                    if 1 <= u <= B * NU:
                        weigh(u - 1)
                    tail(u)



D_IN, HEADS, PD, NS, TAPS = 512, 64, 8, 128, 4
Q = 32
CB_ = D_IN // P
NB = CB_ + 2
NCH = L // Q
CPT = P // Q
HG = HEADS // CPT
PAD = TAPS - 1


def ssd_stage(nc, x, W, tag):
    with ExitStack() as ctx:
        def sb(name, shape, dt=F32):
            return ctx.enter_context(nc.sbuf_tensor(tag + name, shape, dt))

        def ps(name, shape, dt=F32):
            return ctx.enter_context(nc.psum_tensor(tag + name, shape, dt))

        def sem(name):
            return ctx.enter_context(nc.semaphore(tag + name))

        C = W["consts"]
        stats = sb("stats", [P, TS, 6])
        meanvar = sb("meanvar", [P, TS, 2])
        rstd = sb("rstd", [P, TS])
        vareps = sb("vareps", [P, TS])
        xn = sb("xn", [P, TS, D])
        xnT = sb("xnT", [P, KD, L])
        raw = sb("raw", [P, NB, PAD + L])
        conv = sb("conv", [P, NB, L])
        xT, BT = conv[:, 0:CB_, :], conv[:, CB_, :]
        CT = [sb(f"CT{i}", [P, L]) for i in range(2)]
        gate = [sb(f"gate{i}", [P, TS, D_IN]) for i in range(2)]
        dtabs = sb("dtabs", [HEADS, L])
        dtpos = sb("dtpos", [HEADS, L])
        dtT = sb("dtT", [HEADS, L])
        dt = sb("dt", [P, TS, HEADS])
        dA = sb("dA", [P, TS, HEADS])
        dAq = [sb(f"dAq{i}", [P, NCH, HG]) for i in range(2)]
        decays = [sb(f"decays{i}", [P, 2, TS, HEADS]) for i in range(2)]
        chdec = [sb(f"chdec{i}", [P, CPT, TS, HEADS]) for i in range(2)]
        cbm = [sb(f"cbm{i}", [P, NCH, Q]) for i in range(2)]
        xdt = sb("xdt", [P, D_IN])
        xdec = [sb(f"xdec{i}", [P, D_IN]) for i in range(3)]
        xD = [sb(f"xD{i}", [P, D_IN]) for i in range(3)]
        xbd = [sb(f"xbd{i}", [P, CPT, HG, CPT, PD]) for i in range(3)]
        Bz = [sb(f"Bz{i}", [P, CPT, NS]) for i in range(3)]
        spread = [sb(f"spread{i}", [P, HG, Q]) for i in range(2)]
        mix = [sb(f"mix{i}", [P, HG, Q]) for i in range(2)]
        S = [sb(f"S{i}", [P, D_IN]) for i in range(2)]
        Sd = sb("Sd", [P, D_IN])
        y1 = sb("y1", [P, D_IN])
        y2 = sb("y2", [P, D_IN])
        sq = sb("sq", [P, 1])
        msq = sb("msq", [P, 1])
        rms = sb("rms", [P, 1])
        yT = sb("yT", [P, CB_, P])
        Arow = sb("Arow", [P, HEADS])
        negA = sb("negA", [P, HEADS])
        wo = W["ssd_out"]
        zerob = sb("zerob", [P, 512], BF16)

        pf = [ps(f"pf{i}", [P, 512]) for i in range(2)]
        pseg = [ps(f"pseg{i}", [P, 512]) for i in range(2)]
        pst = ps("pst", [P, 512])
        pyd = ps("pyd", [P, 512])
        pyo = ps("pyo", [P, 512])
        pz = ps("pz", [P, 512])

        dve_done = sem("dve_done")
        act_done = sem("act_done")
        prepared = sem("prepared")
        var_ready = sem("var_ready")
        rstd_ready = sem("rstd_ready")
        xn_ready = sem("xn_ready")
        front_in_psum = sem("front_in_psum")
        taken = {"act": sem("taken_by_act"), "dve": sem("taken_by_dve")}
        conv_ready = sem("conv_ready")
        channels_ready = sem("channels_ready")
        soft_ready = sem("soft_ready")
        dtT_ready = sem("dtT_ready")
        dA_ready = sem("dA_ready")
        dAq_ready = sem("dAq_ready")
        xbd_ready = sem("xbd_ready")
        xdt_ready = sem("xdt_ready")
        spread_ready = sem("spread_ready")
        seg_ready = sem("seg_ready")
        exp_ready = sem("exp_ready")
        mix_ready = sem("mix_ready")
        state_in_psum = sem("state_in_psum")
        decayed = sem("decayed")
        state_ready = sem("state_ready")
        yoff_done = sem("yoff_done")
        ydiag_done = sem("ydiag_done")
        y_ready = sem("y_ready")
        sq_ready = sem("sq_ready")
        msq_ready = sem("msq_ready")
        rms_ready = sem("rms_ready")
        yT_in_psum = sem("yT_in_psum")
        yT_ready = sem("yT_ready")
        out_in_psum = sem("out_in_psum")
        x_ready = sem("x_ready")

        FRONT = [("xnT", 0, "act", 0), ("xnT", 1, "act", 0),
                 ("conv", 0, "act", 1), ("conv", 1, "act", 1), ("conv", 2, "act", 2),
                 ("gate", 0, "act", 2), ("gate", 1, "act", 3), ("dtT", 0, "act", 4),
                 ("dt", 0, "dve", 4), ("decays", 0, "act", 5), ("chdec", 0, "act", 5),
                 ("cb", 0, "dve", 6), ("xtok", 0, "dve", 6), ("btok", 0, "act", 6),
                 ("xtok", 1, "dve", 7), ("btok", 1, "act", 7)]
        NF = len(FRONT)
        NTK = {e: sum(f[2] == e for f in FRONT) for e in taken}

        def take_no(b, n):
            e = FRONT[n][2]
            return taken[e], b * NTK[e] + sum(f[2] == e for f in FRONT[:n + 1])

        def place(kind, t=0):
            return next(n for n, f in enumerate(FRONT) if f[:2] == (kind, t))

        NG = B * NCH
        LAST = 3

        def slots():
            yield from ((g - NCH, [n for n in range(NF) if FRONT[n][3] == g], 0) for g in range(NCH))
            for g in range(NG + LAST):
                b = g // NCH
                yield g, [n for n in range(NF) if FRONT[n][3] == g % NCH] if b < B - 1 else [], b + 1

        block = ctx.enter_context(nc.Block())

        @block.gpsimd
        def _(pool):
            pool.memset(zerob[:, :], 0.0).then_inc(prepared, 1)
            for i in range(3):
                pool.memset(xbd[i][:, :, :, :, :], 0.0).then_inc(prepared, 1)
                pool.memset(Bz[i][:, :, :], 0.0).then_inc(prepared, 1)
            pool.memset(raw[:, :, 0:PAD], 0.0).then_inc(prepared, 1)

            def front(b, n):
                kind, t = FRONT[n][:2]
                if (kind, t) == ("xnT", 0):
                    pool.wait_ge(var_ready, b + 1)
                    pool.tensor_tensor(rstd[:, :], vareps[:, :], C["minus_half"][:, 0:TS], ALU.pow).then_inc(rstd_ready, 1)

            for g, pieces, nb in slots():
                for n in pieces:
                    front(nb, n)
                if 0 <= g < NG:
                    b, c = g // NCH, g % NCH
                    pool.wait_ge(dAq_ready, b + 1)
                    if g >= 2:
                        pool.wait_ge(seg_ready, g - 1)
                    pool.tensor_tensor(spread[g % 2][:, :, :], dAq[b % 2][:, c, :].unsqueeze(2).broadcast_to([P, HG, Q]),
                                       C["tri"].unsqueeze(1).broadcast_to([P, HG, Q]), ALU.mult).then_inc(spread_ready, 1)
                g1 = g - 1
                if 0 <= g1 < NG and 1 <= g1 % NCH < NCH - 1:
                    b, c = g1 // NCH, g1 % NCH
                    pool.wait_ge(state_ready, b * (NCH - 1) + c)
                    dec = chdec[b % 2][:, c % CPT, c // CPT, :].unsqueeze(2).broadcast_to([P, HEADS, PD])
                    pool.tensor_tensor(Sd[:, :].rearrange("p (h d) -> p h d", d=PD), S[c % 2][:, :].rearrange("p (h d) -> p h d", d=PD),
                                       dec, ALU.mult).then_inc(decayed, 1)
                if g >= 5 and g % CPT == 1 and g // CPT <= NG // CPT:
                    T = g // CPT - 1
                    pool.wait_ge(msq_ready, T + 1)
                    pool.tensor_tensor(rms[:, :], msq[:, :], C["minus_half"][:, 0:1], ALU.pow).then_inc(rms_ready, 1)

        @block.vector
        def _(dve):
            own = Steps()
            for k in range(CB_):
                dve.tensor_scalar(wo[:, k, :], wo[:, k, :], C["norm_w"][:, k:k + 1], None, ALU.mult).then_inc(dve_done, own.step())
            dve.wait_ge(act_done, 1)
            dve.tensor_scalar(negA[:, :], Arow[:, :], -1.0, None, ALU.mult).then_inc(dve_done, own.step())
            dve.wait_ge(dve_done, own.n)
            dve.wait_ge(prepared, 8)

            def front(b, n):
                kind, t = FRONT[n][:2]
                src = pf[n % 2]
                seen = NF * b + n + 1
                if (kind, t) == ("xnT", 0):
                    for q in range(TS):
                        dve.bn_stats(stats[:, q, :], x[:, TS * b + q, :]).then_inc(dve_done, own.step())
                    dve.wait_ge(dve_done, own.n)
                    for q in range(TS):
                        dve.bn_aggr(meanvar[:, q, :], stats[:, q, :]).then_inc(dve_done, own.step())
                    dve.wait_ge(dve_done, own.n)
                    dve.tensor_scalar(vareps[:, :], meanvar[:, :, 1], EPS, None, ALU.add).then_inc(var_ready, 1)
                    dve.wait_ge(rstd_ready, b + 1)
                    for q in range(TS):
                        dve.tensor_scalar(xn[:, q, :], x[:, TS * b + q, :], meanvar[:, q, 0:1], rstd[:, q:q + 1],
                                          ALU.subtract, ALU.mult).then_inc(xn_ready, 1)
                if kind == "conv":
                    dve.wait_ge(*take_no(b, n))
                    for i in range(PAD):
                        for m in (2 * t, 2 * t + 1):
                            ins = dve.scalar_tensor_tensor(conv[:, m, :], raw[:, m, i:i + L], C["conv_w"][:, m * TAPS + i:m * TAPS + i + 1],
                                                           conv[:, m, :], ALU.mult, ALU.add)
                            if i < PAD - 1:
                                ins.then_inc(dve_done, own.step())
                            else:
                                ins.then_inc(conv_ready, 1)
                        if i < PAD - 1:
                            dve.wait_ge(dve_done, own.n)
                if kind == "dtT":
                    dve.wait_ge(soft_ready, b + 1)
                    dve.tensor_tensor(dtT[:, :], dtT[:, :], dtpos[:, :], ALU.add).then_inc(dtT_ready, 1)
                if kind == "dt":
                    dve.wait_ge(front_in_psum, seen)
                    tk, no = take_no(b, n)
                    dve.tensor_copy(dt[:, :, :], src[:, 0:TS * HEADS].rearrange("p (t h) -> p t h", h=HEADS)).then_inc(tk, 1)
                    dve.wait_ge(tk, no)
                    dve.tensor_tensor(dA[:, :, :], dt[:, :, :], negA[:, :].unsqueeze(1).broadcast_to([P, TS, HEADS]), ALU.mult).then_inc(dA_ready, 1)
                    dve.wait_ge(dA_ready, b + 1)
                    for c4 in range(CPT):
                        for h4 in range(CPT):
                            ins = dve.tensor_copy(dAq[b % 2][Q * h4:Q * h4 + Q, c4::CPT, :],
                                                  dA[Q * c4:Q * c4 + Q, :, h4::CPT])
                            if (c4, h4) != (CPT - 1, CPT - 1):
                                ins.then_inc(dve_done, own.step())
                    ins.then_inc(dAq_ready, 1)
                if kind == "cb":
                    dve.wait_ge(front_in_psum, seen)
                    for c4 in range(CPT):
                        for h4 in range(CPT):
                            ins = dve.tensor_tensor(cbm[b % 2][Q * h4:Q * h4 + Q, c4::CPT, :],
                                                    src[Q * c4:Q * c4 + Q, 0:L].rearrange("p (t n) -> p t n", n=P)[:, :, Q * c4:Q * c4 + Q],
                                                    C["tri"][Q * c4:Q * c4 + Q, :].unsqueeze(1).broadcast_to([Q, TS, Q]), ALU.mult)
                            if (c4, h4) != (CPT - 1, CPT - 1):
                                ins.then_inc(dve_done, own.step())
                    ins.then_inc(take_no(b, n)[0], 1)
                if kind == "xtok":
                    T = TS * b + t
                    dve.wait_ge(front_in_psum, seen)
                    xt = src[:, :].rearrange("p (h d) -> p h d", d=PD)
                    if T >= 1:
                        dve.wait_ge(xbd_ready, T)
                    dve.tensor_tensor(xdt[:, :].rearrange("p (h d) -> p h d", d=PD), xt, dt[:, t, :].unsqueeze(2).broadcast_to([P, HEADS, PD]),
                                      ALU.mult).then_inc(xdt_ready, 1)
                    dve.tensor_tensor(xD[T % 3][:, :].rearrange("p (h d) -> p h d", d=PD), xt, C["D"].unsqueeze(2).broadcast_to([P, HEADS, PD]),
                                      ALU.mult).then_inc(take_no(b, n)[0], 1)
                    dve.wait_ge(xdt_ready, T + 1)
                    dve.wait_ge(*take_no(b, place("decays")))
                    dve.tensor_tensor(xdec[T % 3][:, :].rearrange("p (h d) -> p h d", d=PD), xdt[:, :].rearrange("p (h d) -> p h d", d=PD),
                                      decays[b % 2][:, 1, t, :].unsqueeze(2).broadcast_to([P, HEADS, PD]), ALU.mult).then_inc(dve_done, own.step())
                    src4 = xdt[:, :].rearrange("p (g f d) -> p g f d", f=CPT, d=PD)
                    for c4 in range(CPT):
                        for h4 in range(CPT):
                            ins = dve.tensor_copy(xbd[T % 3][Q * h4:Q * h4 + Q, c4, :, h4, :], src4[Q * c4:Q * c4 + Q, :, h4, :])
                            if (c4, h4) != (CPT - 1, CPT - 1):
                                ins.then_inc(dve_done, own.step())
                    ins.then_inc(xbd_ready, 1)

            for g, pieces, nb in slots():
                for n in pieces:
                    front(nb, n)
                if 0 <= g < NG:
                    b, c = g // NCH, g % NCH
                    dve.wait_ge(exp_ready, g + 1)
                    dve.tensor_tensor(mix[g % 2][:, :, :], mix[g % 2][:, :, :], cbm[b % 2][:, c, :].unsqueeze(1).broadcast_to([P, HG, Q]),
                                      ALU.mult).then_inc(mix_ready, 1)
                g1 = g - 1
                if 0 <= g1 < NG and g1 % NCH < NCH - 1:
                    b, c = g1 // NCH, g1 % NCH
                    no = b * (NCH - 1) + c + 1
                    dve.wait_ge(state_in_psum, no)
                    if g1 >= 1:
                        dve.wait_ge(yoff_done, g1)
                    if c == 0:
                        if b >= 1:
                            dve.wait_ge(decayed, b * (NCH - 2))
                        dve.tensor_copy(S[1][:, :], pst[:, :]).then_inc(state_ready, 1)
                    else:
                        dve.wait_ge(decayed, b * (NCH - 2) + c)
                        dve.tensor_tensor(S[(c + 1) % 2][:, :], Sd[:, :], pst[:, :], ALU.add).then_inc(state_ready, 1)
                if g >= CPT and g % CPT == 0 and g // CPT <= NG // CPT:
                    T = g // CPT - 1
                    b, t = T // TS, T % TS
                    dve.wait_ge(ydiag_done, CPT * (T + 1))
                    if T >= 1:
                        dve.wait_ge(yT_in_psum, T)
                    dve.tensor_tensor(y1[:, :].rearrange("p (h d) -> p h d", d=PD), pyo[:, :].rearrange("p (h d) -> p h d", d=PD),
                                      decays[b % 2][:, 0, t, :].unsqueeze(2).broadcast_to([P, HEADS, PD]), ALU.mult).then_inc(dve_done, own.step())
                    if T >= 1:
                        dve.wait_ge(sq_ready, T)
                    dve.tensor_tensor(y2[:, :], xD[T % 3][:, :], pyd[:, :], ALU.add).then_inc(dve_done, own.step())
                    dve.wait_ge(dve_done, own.n)
                    dve.tensor_tensor(y1[:, :], y1[:, :], y2[:, :], ALU.add).then_inc(dve_done, own.step())
                    dve.wait_ge(dve_done, own.n)
                    dve.tensor_tensor(y1[:, :], y1[:, :], gate[b % 2][:, t, :], ALU.mult).then_inc(y_ready, 1)
                if g >= CPT and g % CPT == 1 and g // CPT <= NG // CPT:
                    T = g // CPT - 1
                    dve.wait_ge(sq_ready, T + 1)
                    dve.tensor_scalar(msq[:, :], sq[:, :], 1.0 / D_IN, EPS, ALU.mult, ALU.add).then_inc(msq_ready, 1)
                if g >= CPT and g % CPT == 2 and g // CPT <= NG // CPT:
                    T = g // CPT - 1
                    dve.wait_ge(out_in_psum, T + 1)
                    dve.wait_ge(rms_ready, T + 1)
                    dve.scalar_tensor_tensor(x[:, T, :], pz[:, 0:D], rms[:, 0:1], x[:, T, :], ALU.mult, ALU.add).then_inc(x_ready, 1)

        @block.scalar
        def _(act):
            own = Steps()
            act.activation(Arow[:, :], C["A_log"], ACT.Exp).then_inc(act_done, own.step())
            act.wait_ge(prepared, 8)

            def front(b, n):
                kind, t, who, _ = FRONT[n]
                src = pf[n % 2]
                if who == "act":
                    act.wait_ge(front_in_psum, NF * b + n + 1)
                    tk = take_no(b, n)[0]
                if kind == "xnT":
                    act.activation(xnT[:, :, t * P:(t + 1) * P], src[:, 0:KD * P].rearrange("p (k n) -> p k n", k=KD), ACT.Copy).then_inc(tk, 1)
                if kind == "conv":
                    s3 = src[:, :].rearrange("p (m n) -> p m n", m=2)
                    if b >= 1:
                        act.wait_ge(conv_ready, NB * b)
                        act.wait_ge(channels_ready, NB * b)
                        act.wait_ge(front_in_psum, NF * b)
                    for i in range(2):
                        m = 2 * t + i
                        act.activation(conv[:, m, :], s3[:, i, :], ACT.Identity, bias=C["conv_b"][:, m:m + 1],
                                       scale=C["conv_w"][:, m * TAPS + PAD:m * TAPS + PAD + 1]).then_inc(act_done, own.step())
                    act.activation(raw[:, 2 * t:2 * t + 2, PAD:], s3, ACT.Copy).then_inc(tk, 1)
                if kind == "gate":
                    act.activation(gate[b % 2][:, t, :], src[:, :], ACT.Silu).then_inc(tk, 1)
                    if t == 1:
                        for m in range(NB):
                            act.wait_ge(conv_ready, NB * b + m + 1)
                            dst = xT[:, m, :] if m < CB_ else BT if m == CB_ else CT[b % 2][:, :]
                            act.activation(dst, conv[:, m, :], ACT.Silu).then_inc(channels_ready, 1)
                if kind == "dtT":
                    z = src[0:HEADS, 0:L]
                    bias = C["dt_bias"][0:HEADS, :]
                    if b >= 1:
                        act.wait_ge(front_in_psum, NF * (b - 1) + place("dt") + 1)
                    act.activation(dtabs[:, :], z, ACT.Abs, bias=bias).then_inc(act_done, own.step())
                    act.activation(dtpos[:, :], z, ACT.Relu, bias=bias).then_inc(tk, 1)
                    act.wait_ge(act_done, own.n)
                    act.activation(dtabs[:, :], dtabs[:, :], ACT.Exp, scale=-1.0).then_inc(act_done, own.step())
                    act.wait_ge(act_done, own.n)
                    act.activation(dtT[:, :], dtabs[:, :], ACT.Ln, bias=1.0).then_inc(soft_ready, 1)
                if kind == "decays":
                    act.activation(decays[b % 2][:, :, :, :], src[:, 0:2 * TS * HEADS].rearrange("p (w t h) -> p w t h", w=2, t=TS), ACT.Exp).then_inc(tk, 1)
                if kind == "chdec":
                    act.activation(chdec[b % 2][:, :, :, :], src[:, :].rearrange("p (c t h) -> p c t h", c=CPT, t=TS), ACT.Exp).then_inc(tk, 1)
                if kind == "btok":
                    T = TS * b + t
                    for c4 in range(CPT):
                        rows = slice(Q * c4, Q * c4 + Q)
                        ins = act.activation(Bz[T % 3][rows, c4, :], src[rows, 0:NS], ACT.Copy)
                        if c4 < CPT - 1:
                            ins.then_inc(act_done, own.step())
                    ins.then_inc(tk, 1)

            for g, pieces, nb in slots():
                if 0 <= g < NG:
                    act.wait_ge(seg_ready, g + 1)
                    if g >= 2:
                        act.wait_ge(ydiag_done, g - 1)
                    act.activation(mix[g % 2][:, :, :], pseg[g % 2][:, :].rearrange("p (h t) -> p h t", t=Q), ACT.Exp).then_inc(exp_ready, 1)
                for n in pieces:
                    front(nb, n)
                if g >= CPT and g % CPT == 0 and g // CPT <= NG // CPT:
                    T = g // CPT - 1
                    act.wait_ge(y_ready, T + 1)
                    if T >= 1:
                        act.wait_ge(msq_ready, T)
                    act.activation(y2[:, :], y1[:, :], ACT.Square, accum_out=sq[:, :]).then_inc(sq_ready, 1)
                if g >= CPT and g % CPT == 1 and g // CPT <= NG // CPT:
                    T = g // CPT - 1
                    act.wait_ge(yT_in_psum, T + 1)
                    act.activation(yT[:, :, :], pz[:, :].rearrange("p (k n) -> p k n", k=CB_), ACT.Copy).then_inc(yT_ready, 1)

        @block.tensor
        def _(pe):
            ident = C["ident"]
            pe.wait_ge(prepared, 8)
            pe.wait_ge(dve_done, CB_ + 1)

            def front(b, n):
                kind, t = FRONT[n][:2]
                dst = pf[n % 2]
                if b > 0 or n >= 2:
                    m = n - 2
                    pe.wait_ge(*take_no(b if m >= 0 else b - 1, m % NF))
                if kind == "xnT":
                    pe.wait_ge(xn_ready, TS * b + t + 1)
                    for k in range(KD):
                        mm = pe.transpose(dst[:, k * P:(k + 1) * P], xn[:, t, k * P:(k + 1) * P], ident)
                if kind == "conv":
                    pe.wait_ge(*take_no(b, place("xnT", 1)))
                    for i in range(2):
                        m = 2 * t + i
                        for k in range(KD):
                            mm = pe.matmul(dst[:, i * L:(i + 1) * L], W["ssd_in"][:, k, D_IN + m * P:D_IN + (m + 1) * P], xnT[:, k, :],
                                           start=(k == 0), stop=(k == KD - 1))
                if kind == "gate":
                    for k in range(KD):
                        mm = pe.matmul(dst[:, :], xnT[:, k, t * P:(t + 1) * P], W["ssd_in"][:, k, 0:D_IN], start=(k == 0), stop=(k == KD - 1))
                if kind == "dtT":
                    for k in range(KD):
                        mm = pe.matmul(dst[0:HEADS, 0:L], W["ssd_in"][:, k, D_IN + NB * P:], xnT[:, k, :], start=(k == 0), stop=(k == KD - 1))
                if kind == "dt":
                    pe.wait_ge(dtT_ready, b + 1)
                    for q in range(TS):
                        mm = pe.transpose(dst[:, q * HEADS:(q + 1) * HEADS], dtT[:, q * P:(q + 1) * P], ident[0:HEADS, 0:HEADS])
                if kind == "decays":
                    pe.wait_ge(dA_ready, b + 1)
                    flat = dA[:, :, :].rearrange("p t h -> p (t h)")
                    pe.matmul(dst[:, 0:TS * HEADS], C["upto_t"], flat, start=True, stop=True)
                    mm = pe.matmul(dst[:, TS * HEADS:2 * TS * HEADS], C["behind"], flat, start=True, stop=True)
                if kind == "chdec":
                    flat = dA[:, :, :].rearrange("p t h -> p (t h)")
                    for c4 in range(CPT):
                        mm = pe.matmul(dst[:, c4 * P:(c4 + 1) * P], C["rows_of"][:, c4 * P:(c4 + 1) * P], flat, start=True, stop=True)
                if kind == "cb":
                    pe.wait_ge(channels_ready, NB * (b + 1))
                    for q in range(TS):
                        mm = pe.matmul(dst[:, q * P:(q + 1) * P], BT[:, q * P:(q + 1) * P], CT[b % 2][:, q * P:(q + 1) * P], start=True, stop=True)
                if kind == "xtok":
                    for k in range(CB_):
                        mm = pe.transpose(dst[:, k * P:(k + 1) * P], xT[:, k, t * P:(t + 1) * P], ident)
                if kind == "btok":
                    mm = pe.transpose(dst[:, 0:NS], BT[:, t * P:(t + 1) * P], ident)
                mm.then_inc(front_in_psum, 1)

            for g, pieces, nb in slots():
                if 0 <= g < NG:
                    pe.wait_ge(spread_ready, g + 1)
                    if g >= 2:
                        pe.wait_ge(exp_ready, g - 1)
                    pe.matmul(pseg[g % 2][:, :], C["behind"], spread[g % 2][:, :, :].rearrange("p h t -> p (h t)"), start=True, stop=True).then_inc(seg_ready, 1)
                for n in pieces:
                    front(nb, n)
                g1 = g - 1
                if 0 <= g1 < NG:
                    b, c = g1 // NCH, g1 % NCH
                    T, c4 = g1 // CPT, c % CPT
                    if c < NCH - 1:
                        no = b * (NCH - 1) + c
                        if c == 0:
                            pe.wait_ge(taken["act"], NTK["act"] * (b + 1))
                            pe.wait_ge(xbd_ready, TS * (b + 1))
                        if no >= 1:
                            pe.wait_ge(state_ready, no)
                        pe.matmul(pst[:, :], Bz[T % 3][:, c4, :], xdec[T % 3][:, :], start=True, stop=True).then_inc(state_in_psum, 1)
                    if c4 == 0 and T >= 1:
                        pe.wait_ge(y_ready, T)
                    rows = slice(Q * c4, Q * c4 + Q)
                    if c == 0:
                        pe.matmul(pyo[rows, :], zerob[:, 0:Q], zerob[:, :], start=True, stop=True).then_inc(yoff_done, 1)
                    else:
                        pe.wait_ge(state_ready, b * (NCH - 1) + c)
                        pe.matmul(pyo[rows, :], CT[b % 2][:, c * Q:(c + 1) * Q], S[c % 2][:, :], start=True, stop=True).then_inc(yoff_done, 1)
                    pe.wait_ge(mix_ready, g1 + 1)
                    for h in range(HG):
                        mm = pe.matmul(pyd[rows, h * Q:(h + 1) * Q], mix[g1 % 2][:, h, :], xbd[T % 3][:, c4, h, :, :].rearrange("p f d -> p (f d)"),
                                       start=True, stop=True)
                    mm.then_inc(ydiag_done, 1)
                if g >= CPT and g % CPT == 1 and g // CPT <= NG // CPT:
                    T = g // CPT - 1
                    pe.wait_ge(y_ready, T + 1)
                    if T >= 1:
                        pe.wait_ge(x_ready, T)
                    for k in range(CB_):
                        mm = pe.transpose(pz[:, k * P:(k + 1) * P], y1[:, k * P:(k + 1) * P], ident)
                    mm.then_inc(yT_in_psum, 1)
                if g >= CPT and g % CPT == 2 and g // CPT <= NG // CPT:
                    T = g // CPT - 1
                    pe.wait_ge(yT_ready, T + 1)
                    for k in range(CB_):
                        mm = pe.matmul(pz[:, 0:D], yT[:, k, :], wo[:, k, :], start=(k == 0), stop=(k == CB_ - 1))
                    mm.then_inc(out_in_psum, 1)


COMMON = [("ident", P), ("ones", P), ("below", P), ("minus_half", NT), ("weigh", NT * E), ("steps", E * NT),
          ("upto", E * E), ("tile_no", NR * E)]
FOR_SSD = [("tri", Q), ("behind", P), ("upto_t", P), ("rows_of", CPT * P), ("A_log", HEADS), ("D", HEADS), ("dt_bias", 1),
           ("conv_w", NB * TAPS), ("conv_b", NB), ("norm_w", CB_)]
FOR_ATT = [("hide", P), ("cos", TS * QK), ("sin", TS * QK)]


def views(buffer, fields):
    got, at = {}, 0
    for name, width in fields:
        got[name] = buffer[:, at:at + width]
        at += width
    return got


def width_of(fields):
    return sum(width for _, width in fields)


def hybrid_layer(nc, hidden, ssd_in, ssd_out, qkv, wo, gate_up, down, router, common, for_ssd, for_att, out):
    slots_x = nc.dram_tensor("slots_x", [NR * P, D], F32).ap()
    slots_y = nc.dram_tensor("slots_y", [NR * P, D], F32).ap()
    with ExitStack() as ctx:
        def sb(stack, name, shape):
            return stack.enter_context(nc.sbuf_tensor(name, shape, F32))

        def sem(name):
            return ctx.enter_context(nc.semaphore(name))

        x = sb(ctx, "x", [P, NT, D])
        common_sb = sb(ctx, "common_sb", [P, width_of(COMMON)])
        router_sb = sb(ctx, "router_sb", [P, KD, E])
        gate_up_sb = sb(ctx, "gate_up_sb", [P, E + 1, KD, 2 * FI])
        first_loads = sem("first_loads")
        zeros_ready = sem("zeros_ready")
        slots_cleared = sem("slots_cleared")
        expert_loads = sem("expert_loads")
        down_loads = [sem("shared_down_load"), sem("routed_down_load")]
        att_loads = sem("att_loads")
        stored = sem("stored")

        C = views(common_sb, COMMON)
        for name, inner in (("weigh", E), ("steps", NT), ("upto", E)):
            C[name] = C[name].rearrange("p (a b) -> p a b", b=inner)
        C["tile_no"] = C["tile_no"][0:1, :].rearrange("p (a b) -> p a b", b=E)
        W = dict(consts=C, slots_x=slots_x, slots_y=slots_y, gate_up=gate_up_sb, router=router_sb)

        with ExitStack() as ssd_ctx:
            ssd_in_sb = sb(ssd_ctx, "ssd_in_sb", [P, KD, D_IN + NB * P + HEADS])
            ssd_out_sb = sb(ssd_ctx, "ssd_out_sb", [P, CB_, D])
            for_ssd_sb = sb(ssd_ctx, "for_ssd_sb", [P, width_of(FOR_SSD)])
            zeros = sb(ssd_ctx, "zeros", [P, D])

            with nc.Block() as block:
                @block.sync
                def _(sp):
                    sp.dma_start(x[:, :, :], hidden).then_inc(first_loads, 16)
                    sp.dma_start(ssd_in_sb[:, :, :], ssd_in).then_inc(first_loads, 16)
                    sp.dma_start(ssd_out_sb[:, :, :], ssd_out).then_inc(first_loads, 16)
                    sp.dma_start(gate_up_sb[:, :, :, :], gate_up).then_inc(expert_loads, 16)
                    sp.dma_start(router_sb[:, :, :], router).then_inc(expert_loads, 16)
                    sp.wait_ge(zeros_ready, 1)
                    sp.dma_start(slots_x.rearrange("(t p) n -> p t n", p=P),
                                 zeros[:, :].unsqueeze(1).broadcast_to([P, NR, D])).then_inc(slots_cleared, 16)
                    sp.wait_ge(first_loads, 16 * 5)

                @block.scalar
                def _(act):
                    act.dma_start(common_sb[:, :], common).then_inc(first_loads, 16)
                    act.dma_start(for_ssd_sb[:, :], for_ssd).then_inc(first_loads, 16)

                @block.vector
                def _(dve):
                    dve.memset(zeros[:, :], 0.0).then_inc(zeros_ready, 1)

            ssd_stage(nc, x, dict(consts={**C, **views(for_ssd_sb, FOR_SSD)}, ssd_in=ssd_in_sb, ssd_out=ssd_out_sb), "ssd_")
            with nc.Block() as block:
                @block.sync
                def _(sp):
                    sp.wait_ge(slots_cleared, 16)
                    sp.wait_ge(expert_loads, 32)

        down_sb = sb(ctx, "down_sb", [P, E + 1, KF, D])
        qkv_sb = sb(ctx, "qkv_sb", [P, KD, QKV])
        wo_sb = sb(ctx, "wo_sb", [P, KD, D])
        for_att_sb = sb(ctx, "for_att_sb", [P, width_of(FOR_ATT)])
        att = views(for_att_sb, FOR_ATT)
        for name in ("cos", "sin"):
            att[name] = att[name].rearrange("p (t n) -> p t n", t=TS)
        W["down"] = down_sb

        def load_behind(sp):
            sp.dma_start(down_sb[:, E, :, :], down[:, E, :, :]).then_inc(down_loads[0], 16)
            sp.dma_start(down_sb[:, 0:E, :, :], down[:, 0:E, :, :]).then_inc(down_loads[1], 16)
            sp.dma_start(qkv_sb[:, :, :], qkv).then_inc(att_loads, 16)
            sp.dma_start(wo_sb[:, :, :], wo).then_inc(att_loads, 16)
            sp.dma_start(for_att_sb[:, :], for_att).then_inc(att_loads, 16)

        W["down_loads"] = down_loads
        ffn_stage(nc, x, W, "ffn1_", load_behind)
        with nc.Block() as block:
            @block.sync
            def _(sp):
                sp.wait_ge(att_loads, 48)
        attention_stage(nc, x, dict(consts={**C, **att}, qkv=qkv_sb, wo=wo_sb), "att_")
        ffn_stage(nc, x, W, "ffn2_", None)
        with nc.Block() as block:
            @block.sync
            def _(sp):
                sp.dma_start(out, x[:, :, :]).then_inc(stored, 16)
                sp.wait_ge(stored, 16)


def kernel(**inputs):
    import numpy as np
    import concourse.bacc as bacc
    from concourse.bass_utils import run_bass_kernel_spmd

    def given(name):
        return np.asarray(inputs["L0_" + name])

    def chunks(w, rows):
        return w.reshape(rows, P, -1).transpose(1, 0, 2)

    k = np.arange(P)
    same = k[:, None] // Q == k[None, :] // Q
    tables = {
        "ident": np.eye(P), "ones": np.ones((P, P)), "below": k[:, None] < k[None, :],
        "minus_half": np.full((P, NT), -0.5),
        "weigh": np.tile(float(E) - np.arange(E), (P, NT)),
        "steps": np.tile(float(P) * np.arange(NT), (P, E)),
        "upto": np.tile((np.arange(E)[None, :] <= np.arange(E)[:, None]).reshape(-1), (P, 1)),
        "tile_no": np.tile(np.repeat(np.arange(float(NR)), E), (P, 1)),
        "tri": k[:, None] % Q <= np.arange(Q)[None, :],
        "behind": same & (k[:, None] > k[None, :]), "upto_t": same & (k[:, None] <= k[None, :]),
        "rows_of": np.concatenate([np.tile((k[:, None] // Q == q), (1, P)) for q in range(CPT)], 1),
        "hide": np.where(k[None, :] > k[:, None], -1e30, 0.0),
    }
    theta = (1.0 / np.float32(10000.0) ** (np.arange(0, HD, 2, dtype=np.float32) / HD)).astype(np.float32)
    angle = np.arange(L, dtype=np.float32)[:, None] * theta[None, :]
    scale = np.array([HD ** -0.5] * H + [1.0] * HKV)
    for name, pair in (("cos", (np.cos(angle), np.cos(angle))), ("sin", (-np.sin(angle), np.sin(angle)))):
        table = np.stack(pair, -1).reshape(L, 1, HD) * scale[None, :, None]
        tables[name] = chunks(table.reshape(L, QK), TS).reshape(P, -1)
    tables.update({
        "A_log": np.tile(given("attn_a_A_log"), (P, 1)), "D": np.tile(given("attn_a_D"), (P, 1)),
        "dt_bias": np.tile(given("attn_a_dt_bias"), P // HEADS)[:, None],
        "conv_w": given("attn_a_conv_w").reshape(NB, P, TAPS).transpose(1, 0, 2).reshape(P, -1),
        "conv_b": given("attn_a_conv_b").reshape(NB, P).T, "norm_w": given("attn_a_norm_w").reshape(CB_, P).T,
    })

    def packed(fields):
        return np.concatenate([np.asarray(tables[name], np.float32) for name, _ in fields], 1)

    wq = given("attn_b_wq").reshape(G, HALF, REP, HD, D).transpose(0, 2, 1, 3, 4).reshape(H * HD, D)
    shared_up = np.concatenate([given("ffn_shared_gate_w"), given("ffn_shared_up_w")], 1)[None]
    gate_up = np.concatenate([given("ffn_gate_up_proj"), shared_up])
    down = np.concatenate([given("ffn_down_proj"), given("ffn_shared_down_w")[None]])
    arrays = {
        "hidden": chunks(given("attn_a_hidden_states").reshape(TOK, D), NT),
        "ssd_in": chunks(given("attn_a_in_proj_w").T, KD), "ssd_out": chunks(given("attn_a_out_proj_w").T, CB_),
        "qkv": chunks(np.concatenate([wq, given("attn_b_wk"), given("attn_b_wv")]).T, KD), "wo": chunks(given("attn_b_wo").T, KD),
        "gate_up": gate_up.reshape(E + 1, KD, P, 2 * FI).transpose(2, 0, 1, 3),
        "down": down.reshape(E + 1, KF, P, D).transpose(2, 0, 1, 3),
        "router": chunks(given("ffn_router_w").T, KD),
        "common": packed(COMMON), "for_ssd": packed(FOR_SSD), "for_att": packed(FOR_ATT),
    }
    nc = bacc.Bacc("TRN2", target_bir_lowering=False, num_devices=1)
    feed, args = {}, []
    for name, a in arrays.items():
        feed[name] = np.ascontiguousarray(a)
        args.append(nc.dram_tensor(name, feed[name].shape, mybir.dt.from_np(feed[name].dtype), kind="ExternalInput").ap())
    args.append(nc.dram_tensor("out", (P, NT, D), F32, kind="ExternalOutput").ap())
    hybrid_layer(nc, *args)
    r = run_bass_kernel_spmd(nc, [feed], core_ids=[0])
    return r.results[0]["out"].transpose(1, 0, 2).reshape(B, L, D)
```

```python
from contextlib import ExitStack

import concourse.bass as bass
from concourse import mybir
from concourse.alu_op_type import AluOpType as ALU

F32 = mybir.dt.float32
BF16 = mybir.dt.bfloat16
I32 = mybir.dt.int32
U32 = mybir.dt.uint32
ACT = mybir.ActivationFunctionType
AX = mybir.AxisListType

P = 128
B, L, D = 4, 256, 256
TOK = B * L
NT = TOK // P
KD = D // P
EPS = 1e-5
E, FI = 8, 512
KF = FI // P
SHARED = E
NR = NT + E - 1
NJ = NT + NR


class Steps:

    def __init__(self):
        self.n = 0

    def step(self):
        self.n += 1
        return 1


def ffn_stage(nc, x, W, tag, load_behind=None):
    with ExitStack() as ctx:
        def sb(name, shape, dt=F32):
            return ctx.enter_context(nc.sbuf_tensor(tag + name, shape, dt))

        def ps(name, shape, dt=F32):
            return ctx.enter_context(nc.psum_tensor(tag + name, shape, dt))

        def sem(name):
            return ctx.enter_context(nc.semaphore(tag + name))

        C = W["consts"]
        stats = sb("stats", [P, NT, 6])
        meanvar = sb("meanvar", [P, NT, 2])
        rstd = sb("rstd", [P, NT])
        vareps = sb("vareps", [P, NT])
        xn = sb("xn", [P, NT, D])
        xscaled = sb("xscaled", [P, NT, D])
        xnT = sb("xnT", [P, KD, TOK])
        logitT = sb("logitT", [E, TOK])
        logit = sb("logit", [P, NT, E])
        top = sb("top", [P, NT])
        score = sb("score", [P, NT])
        tmp = sb("tmp", [P, E * E])
        first = sb("first", [P, NT])
        onehot = sb("onehot", [P, NT, E])
        before = sb("before", [P, NT + 1, E])
        counts = sb("counts", [P, NT, E])
        tiles_of = sb("tiles_of", [P, E])
        tile_end = sb("tile_end", [P, E])
        base = sb("base", [P, E])
        rank = sb("rank", [P, NT, E])
        slotf = sb("slotf", [P, NT])
        slot = sb("slot", [P, NT], U32)
        expf = sb("expf", [1, NR])
        expert = sb("expert", [1, NR], I32)
        cmp = sb("cmp", [1, NR, E])
        xg = [sb(f"xg{i}", [P, D]) for i in range(2)]
        xgT = [sb(f"xgT{i}", [P, KD, P]) for i in range(2)]
        sg = [sb(f"sg{i}", [P, FI]) for i in range(2)]
        h = [sb(f"h{i}", [P, FI]) for i in range(2)]
        hT = [sb(f"hT{i}", [P, KF, P]) for i in range(2)]
        yout = [sb(f"yout{i}", [P, D]) for i in range(2)]
        yback = sb("yback", [P, NT, D])

        gu = [ps(f"gu{i}", [P, 2 * FI]) for i in range(2)]
        pt = ps("pt", [P, KF * P])
        pd = [ps(f"pd{i}", [P, 512]) for i in range(2)]
        px = ps("px", [P, 512])

        dve_done = sem("dve_done")
        var_ready = sem("var_ready")
        rstd_ready = sem("rstd_ready")
        xn_ready = sem("xn_ready")
        xnT_in_psum = sem("xnT_in_psum")
        xnT_ready = sem("xnT_ready")
        logitT_in_psum = sem("logitT_in_psum")
        logitT_ready = sem("logitT_ready")
        logit_in_psum = sem("logit_in_psum")
        top_ready = sem("top_ready")
        score_ready = sem("score_ready")
        onehot_ready = sem("onehot_ready")
        ranks_in_psum = sem("ranks_in_psum")
        route_ready = sem("route_ready")
        scattered = sem("scattered")
        gathered = [sem(f"gathered{t}") for t in range(NT)]
        xg_loaded = [sem(f"xg_loaded{i}") for i in range(2)]
        xgT_in_psum = sem("xgT_in_psum")
        xgT_ready = sem("xgT_ready")
        gu_ready = sem("gu_ready")
        silu_ready = sem("silu_ready")
        h_ready = sem("h_ready")
        hT_in_psum = sem("hT_in_psum")
        hT_ready = sem("hT_ready")
        y_in_psum = sem("y_in_psum")
        y_taken = sem("y_taken")
        y_stored = [sem(f"y_stored{i}") for i in range(2)]

        slots_x = W["slots_x"]
        slots_y = W["slots_y"]
        block = ctx.enter_context(nc.Block())

        LOOP = range(NT + 4, NJ - 1)
        assert len(LOOP) % 2 == 0

        def steps(eng, step):
            for j in range(0, LOOP.start):
                step(j, j % 2, j)
            with eng.Fori(0, len(LOOP) // 2) as i:
                for u in range(2):
                    step(2 * i + (LOOP.start + u), u, LOOP.start + u)
            for j in range(LOOP.stop, NJ + 2):
                step(j, j % 2, j)

        @block.sync
        def _(sp):
            def load(r):
                sp.dma_start(xg[r % 2][:, :], slots_x[r * P:(r + 1) * P, :]).then_inc(xg_loaded[r % 2], 16)

            if load_behind:
                load_behind(sp)
            sp.wait_ge(scattered, 16 * NT)
            for r in range(2):
                load(r)
            for r in range(NR + 3):
                if r + 2 < NR:
                    sp.wait_ge(xgT_in_psum, r + 1)
                    load(r + 2)
                if r >= 3:
                    q = r - 3
                    sp.wait_ge(y_taken, NT + q + 1)
                    sp.dma_start(slots_y[q * P:(q + 1) * P, :], yout[q % 2][:, :]).then_inc(y_stored[q % 2], 16)

        @block.gpsimd
        def _(pool):
            pool.wait_ge(var_ready, 1)
            pool.tensor_tensor(rstd[:, :], vareps[:, :], C["minus_half"], ALU.pow).then_inc(rstd_ready, 1)
            for t in range(NT):
                pool.wait_ge(route_ready, 2 + t)
                pool.indirect_dma_start(out=slots_x, out_offset=bass.IndirectOffsetOnAxis(ap=slot[:, t:t + 1], axis=0),
                                        in_=xscaled[:, t, :], in_offset=None).then_inc(scattered, 16)
            pool.wait_ge(y_stored[0], 16 * ((NR + 1) // 2))
            pool.wait_ge(y_stored[1], 16 * (NR // 2))
            for t in range(NT):
                pool.indirect_dma_start(out=yback[:, t, :], out_offset=None, in_=slots_y,
                                        in_offset=bass.IndirectOffsetOnAxis(ap=slot[:, t:t + 1], axis=0)).then_inc(gathered[t], 16)

        @block.vector
        def _(dve):
            own = Steps()
            for t in range(NT):
                dve.bn_stats(stats[:, t, :], x[:, t, :]).then_inc(dve_done, own.step())
            dve.wait_ge(dve_done, own.n)
            for t in range(NT):
                dve.bn_aggr(meanvar[:, t, :], stats[:, t, :]).then_inc(dve_done, own.step())
            dve.wait_ge(dve_done, own.n)
            dve.tensor_scalar(vareps[:, :], meanvar[:, :, 1], EPS, None, ALU.add).then_inc(var_ready, 1)
            dve.wait_ge(rstd_ready, 1)
            for t in range(NT):
                dve.tensor_scalar(xn[:, t, :], x[:, t, :], meanvar[:, t, 0:1], rstd[:, t:t + 1],
                                  ALU.subtract, ALU.mult).then_inc(xn_ready, 1)
            dve.wait_ge(logitT_in_psum, 1)
            dve.tensor_copy(logitT[:, :], gu[1][0:E, :]).then_inc(logitT_ready, 1)
            dve.wait_ge(logit_in_psum, 1)
            dve.tensor_copy(logit[:, :, :], px[:, 0:NT * E].rearrange("p (t e) -> p t e", e=E)).then_inc(dve_done, own.step())
            dve.wait_ge(dve_done, own.n)
            dve.tensor_reduce(top[:, :], logit[:, :, :], AX.X, ALU.max).then_inc(top_ready, 1)
            dve.wait_ge(top_ready, 1)
            t3 = tmp[:, :].rearrange("p (t e) -> p t e", e=E)
            dve.tensor_tensor(onehot[:, :, :], logit[:, :, :], top[:, :].unsqueeze(2).broadcast_to([P, NT, E]), ALU.is_ge).then_inc(dve_done, own.step())
            dve.wait_ge(dve_done, own.n)
            dve.tensor_tensor(t3, onehot[:, :, :], C["weigh"], ALU.mult).then_inc(dve_done, own.step())
            dve.wait_ge(dve_done, own.n)
            dve.tensor_reduce(first[:, :], t3, AX.X, ALU.max).then_inc(dve_done, own.step())
            dve.wait_ge(dve_done, own.n)
            dve.tensor_tensor(onehot[:, :, :], t3, first[:, :].unsqueeze(2).broadcast_to([P, NT, E]), ALU.is_equal).then_inc(onehot_ready, 1)
            dve.wait_ge(onehot_ready, 1)
            dve.wait_ge(ranks_in_psum, 1)
            pr = pd[0]
            dve.tensor_copy(rank[:, :, :], pr[:, 0:NT * E].rearrange("p (t e) -> p t e", e=E)).then_inc(dve_done, own.step())
            dve.tensor_copy(counts[:, :, :], pr[:, NT * E:2 * NT * E].rearrange("p (t e) -> p t e", e=E)).then_inc(dve_done, own.step())
            dve.memset(before[:, 0, :], 0.0).then_inc(dve_done, own.step())
            for t in range(NT):
                dve.wait_ge(dve_done, own.n)
                dve.tensor_tensor(before[:, t + 1, :], before[:, t, :], counts[:, t, :], ALU.add).then_inc(dve_done, own.step())
            dve.wait_ge(dve_done, own.n)
            dve.tensor_tensor(t3, before[:, NT, :].unsqueeze(2).broadcast_to([P, E, NT]), C["steps"], ALU.is_gt).then_inc(dve_done, own.step())
            dve.wait_ge(dve_done, own.n)
            dve.tensor_reduce(tiles_of[:, :], t3, AX.X, ALU.add).then_inc(dve_done, own.step())
            dve.wait_ge(dve_done, own.n)
            dve.tensor_tensor(t3, tiles_of[:, :].unsqueeze(1).broadcast_to([P, E, E]), C["upto"], ALU.mult).then_inc(dve_done, own.step())
            dve.wait_ge(dve_done, own.n)
            dve.tensor_reduce(tile_end[:, :], t3, AX.X, ALU.add).then_inc(dve_done, own.step())
            dve.wait_ge(dve_done, own.n)
            dve.tensor_tensor(base[:, :], tile_end[:, :], tiles_of[:, :], ALU.subtract).then_inc(dve_done, own.step())
            dve.tensor_tensor(rank[:, :, :], rank[:, :, :], before[:, 0:NT, :], ALU.add).then_inc(dve_done, own.step())
            dve.tensor_tensor(cmp[:, :, :], tile_end[0:1, :].unsqueeze(1).broadcast_to([1, NR, E]), C["tile_no"], ALU.is_le).then_inc(dve_done, own.step())
            dve.wait_ge(dve_done, own.n)
            dve.scalar_tensor_tensor(t3, base[:, :].unsqueeze(1).broadcast_to([P, NT, E]), float(P), rank[:, :, :], ALU.mult, ALU.add).then_inc(dve_done, own.step())
            dve.tensor_reduce(expf[:, :], cmp[:, :, :], AX.X, ALU.add).then_inc(dve_done, own.step())
            dve.wait_ge(dve_done, own.n)
            dve.tensor_tensor(rank[:, :, :], t3, onehot[:, :, :], ALU.mult).then_inc(dve_done, own.step())
            dve.tensor_scalar(expert[:, :], expf[:, :], float(E - 1), None, ALU.min).then_inc(dve_done, own.step())
            dve.wait_ge(dve_done, own.n)
            dve.tensor_reduce(slotf[:, :], rank[:, :, :], AX.X, ALU.add).then_inc(dve_done, own.step())
            dve.wait_ge(dve_done, own.n)
            dve.tensor_copy(slot[:, :], slotf[:, :]).then_inc(route_ready, 1)
            dve.wait_ge(score_ready, 1)
            for t in range(NT):
                dve.tensor_scalar(xscaled[:, t, :], xn[:, t, :], score[:, t:t + 1], None, ALU.mult).then_inc(route_ready, 1)

            def step(j, u, jn):
                if NT <= jn + 1 < NJ:
                    r1 = j + 1 - NT
                    dve.wait_ge(xgT_in_psum, r1 + 1)
                    dve.wait_ge(gu_ready, j)
                    dve.tensor_copy(xgT[(u + 1) % 2][:, :, :], px[:, 0:D].rearrange("p (k n) -> p k n", k=KD)).then_inc(xgT_ready, 1)
                if jn < NJ:
                    dve.wait_ge(silu_ready, j + 1)
                    if jn >= 2:
                        dve.wait_ge(hT_in_psum, j - 1)
                    dve.tensor_tensor(h[u][:, :], sg[u][:, :], gu[u][:, FI:], ALU.mult).then_inc(h_ready, 1)
                if jn >= 2:
                    dve.wait_ge(y_in_psum, j - 1)
                    if jn - 2 < NT:
                        dve.tensor_tensor(x[:, jn - 2, :], x[:, jn - 2, :], pd[u][:, 0:D], ALU.add).then_inc(y_taken, 1)
                    else:
                        if jn - 2 >= NT + 2:
                            dve.wait_ge(y_stored[u], 8 * (j - (2 + NT + u)))
                        dve.tensor_copy(yout[u][:, :], pd[u][:, 0:D]).then_inc(y_taken, 1)

            steps(dve, step)
            for t in range(NT):
                dve.wait_ge(gathered[t], 16)
                dve.tensor_tensor(x[:, t, :], x[:, t, :], yback[:, t, :], ALU.add)

        @block.scalar
        def _(act):
            for g in range(NT // 2):
                act.wait_ge(xnT_in_psum, g + 1)
                act.activation(xnT[:, :, 2 * g * P:2 * (g + 1) * P], gu[0][:, (g % 2) * 512:(g % 2) * 512 + 512].rearrange("p (k n) -> p k n", k=KD),
                               ACT.Copy).then_inc(xnT_ready, 1)
            act.wait_ge(top_ready, 1)
            act.activation(score[:, :], top[:, :], ACT.Sigmoid).then_inc(score_ready, 1)

            def step(j, u, jn):
                if jn < NJ:
                    act.wait_ge(gu_ready, j + 1)
                    if jn >= 2:
                        act.wait_ge(h_ready, j - 1)
                    act.activation(sg[u][:, :], gu[u][:, 0:FI], ACT.Silu).then_inc(silu_ready, 1)
                if 1 <= jn <= NJ:
                    act.wait_ge(hT_in_psum, j)
                    if jn >= 3:
                        act.wait_ge(y_in_psum, j - 2)
                    act.activation(hT[(u + 1) % 2][:, :, :], pt[:, :].rearrange("p (k n) -> p k n", k=KF), ACT.Copy).then_inc(hT_ready, 1)

            steps(act, step)

        @block.tensor
        def _(pe):
            ident = C["ident"]
            for t in range(NT):
                g, r = t // 2, t % 2
                if r == 0 and g >= 2:
                    pe.wait_ge(xnT_ready, g - 1)
                pe.wait_ge(xn_ready, t + 1)
                for k in range(KD):
                    mm = pe.transpose(gu[0][:, (g % 2) * 512 + k * 256 + r * P:(g % 2) * 512 + k * 256 + (r + 1) * P], xn[:, t, k * P:(k + 1) * P], ident)
                if r == 1:
                    mm.then_inc(xnT_in_psum, 1)
            for half in range(2):
                pe.wait_ge(xnT_ready, 2 * (half + 1))
                for k in range(KD):
                    mm = pe.matmul(gu[1][0:E, half * 512:(half + 1) * 512], W["router"][:, k, :], xnT[:, k, half * 512:(half + 1) * 512],
                                   start=(k == 0), stop=(k == KD - 1))
            mm.then_inc(logitT_in_psum, 1)
            pe.wait_ge(logitT_ready, 1)
            for t in range(NT):
                mm = pe.transpose(px[:, t * E:(t + 1) * E], logitT[:, t * P:(t + 1) * P], ident[0:E, 0:E])
            mm.then_inc(logit_in_psum, 1)

            def ranks():
                pe.wait_ge(onehot_ready, 1)
                oh = onehot[:, :, :].rearrange("p t e -> p (t e)")
                pe.matmul(pd[0][:, 0:NT * E], C["below"], oh, start=True, stop=True)
                pe.matmul(pd[0][:, NT * E:2 * NT * E], C["ones"], oh, start=True, stop=True).then_inc(ranks_in_psum, 1)

            def step(j, u, jn):
                if NT <= jn + 1 < NJ:
                    v = (u + 1) % 2
                    pe.wait_ge(xg_loaded[v], 8 * (j + (3 - NT - v)))
                    if jn >= NT:
                        pe.wait_ge(xgT_ready, j + 1 - NT)
                    for k in range(KD):
                        mm = pe.transpose(px[:, k * P:(k + 1) * P], xg[v][:, k * P:(k + 1) * P], ident)
                    mm.then_inc(xgT_in_psum, 1)
                if jn < NJ:
                    if jn < NT:
                        e = SHARED
                        pe.wait_ge(xnT_ready, jn // 2 + 1)
                    else:
                        pe.wait_ge(xgT_ready, j - NT + 1)
                        if jn == NT:
                            pe.wait_ge(W["late_loads"][1], 32)
                        e = pe.value_load(expert[0:1, bass.ds(j - NT, 1)], min_val=0, max_val=E - 1)
                    if jn >= 2:
                        pe.wait_ge(h_ready, j - 1)
                    for half in range(2):
                        for k in range(KD):
                            lhsT = xnT[:, k, jn * P:(jn + 1) * P] if jn < NT else xgT[u][:, k, :]
                            rhs = W["gate_up"][:, bass.ds(e, 1), k, half * FI:(half + 1) * FI]
                            mm = pe.matmul(gu[u][:, half * FI:(half + 1) * FI], lhsT, rhs.rearrange("p a n -> p (a n)"), start=(k == 0), stop=(k == KD - 1))
                    mm.then_inc(gu_ready, 1)
                if jn >= 2:
                    pe.wait_ge(hT_ready, j - 1)
                    if jn == 2:
                        pe.wait_ge(W["late_loads"][0], 16)
                    if jn >= 4:
                        pe.wait_ge(y_taken, j - 3)
                    e = SHARED if jn - 2 < NT else pe.value_load(expert[0:1, bass.ds(j - 2 - NT, 1)], min_val=0, max_val=E - 1)
                    for k in range(KF):
                        mm = pe.matmul(pd[u][:, 0:D], hT[u][:, k, :], W["down"][:, bass.ds(e, 1), k, :].rearrange("p a n -> p (a n)"),
                                       start=(k == 0), stop=(k == KF - 1))
                    mm.then_inc(y_in_psum, 1)
                if 1 <= jn <= NJ:
                    pe.wait_ge(h_ready, j)
                    for k in range(KF):
                        mm = pe.transpose(pt[:, k * P:(k + 1) * P], h[(u + 1) % 2][:, k * P:(k + 1) * P], ident)
                    mm.then_inc(hT_in_psum, 1)
                if jn == 0:
                    ranks()

            steps(pe, step)



H, HKV, HD = 32, 8, 8
G, HALF, REP = HKV // 2, 2, H // HKV
TS = L // P
ROWS = 64
TYPES = 6
QKV = (H + 2 * HKV) * HD
QK = (H + HKV) * HD


def attention_stage(nc, x, W, tag):
    with ExitStack() as ctx:
        def sb(name, shape, dt=F32):
            return ctx.enter_context(nc.sbuf_tensor(tag + name, shape, dt))

        def ps(name, shape, dt=F32):
            return ctx.enter_context(nc.psum_tensor(tag + name, shape, dt))

        def sem(name):
            return ctx.enter_context(nc.semaphore(tag + name))

        C = W["consts"]
        stats = sb("stats", [P, TS, 6])
        meanvar = sb("meanvar", [P, TS, 2])
        rstd = sb("rstd", [P, TS])
        vareps = sb("vareps", [P, TS])
        xn = sb("xn", [P, TS, D])
        xnT = sb("xnT", [P, KD, L])
        ropeA = sb("ropeA", [P, QK])
        ropeB = sb("ropeB", [P, QK])
        parts = sb("parts", [P, 3, QK], BF16)
        qs = sb("qs", [P, TS, H, ROWS], BF16)
        ks = sb("ks", [P, TS, HKV, ROWS], BF16)
        qTa = sb("qTa", [P, G * REP, L], BF16)
        qTb = [sb(f"qTb{i}", [P, G, REP, L], BF16) for i in range(2)]
        kz = [sb(f"kz{i}", [P, G, HALF, L], BF16) for i in range(2)]
        V = [sb(f"V{i}", [P, TS, HKV, 32]) for i in range(2)]
        top = sb("top", [P, TS, H])
        rest = sb("rest", [P, H])
        probs = [sb(f"probs{i}", [P, 2 * 512]) for i in range(2)]
        oT = sb("oT", [P, REP, P])
        recip = sb("recip", [P, REP, 4])
        y = sb("y", [P, TS, HKV, REP, HD])
        yT = sb("yT", [P, KD, P])
        identb = sb("identb", [P, P], BF16)
        hide = sb("hide", [P, HALF, P], BF16)

        sT = [ps(f"sT{i}", [P, 2 * 512]) for i in range(2)]
        po = ps("po", [P, 512])
        pf = [ps(f"pf{i}", [P, 512]) for i in range(2)]
        ot = ps("ot", [P, 512])

        dve_done = sem("dve_done")
        var_ready = sem("var_ready")
        rstd_ready = sem("rstd_ready")
        xn_ready = sem("xn_ready")
        front_in_psum = sem("front_in_psum")
        front_taken = sem("front_taken")
        parts_ready = sem("parts_ready")
        q1_copied = sem("q1_copied")
        rows_ready = sem("rows_ready")
        max_rows_ready = sem("max_rows_ready")
        scores_ready = sem("scores_ready")
        probs_ready = sem("probs_ready")
        pv_done = sem("pv_done")
        oT_in_psum = sem("oT_in_psum")
        oT_ready = sem("oT_ready")
        o_in_psum = sem("o_in_psum")
        y_ready = sem("y_ready")
        yT_in_psum = sem("yT_in_psum")
        yT_ready = sem("yT_ready")
        wo_in_psum = sem("wo_in_psum")
        x_ready = sem("x_ready")

        FRONT = ([("xnT", t, 0) for t in range(TS)] + [("qkv", t, 0) for t in range(TS)]
                 + [(kind, t, n) for t in range(TS) for kind, n in (("kT", 0), ("qTa", 0), ("qTa", 1))]
                 + [("max0", 0, n) for n in range(G * REP // 2)] + [("max1", 1, n) for n in range(G * REP)]
                 + [("qTb", t, n) for t in range(TS) for n in range(2)])
        NF = len(FRONT)
        UNITS = [(tt, kv) for tt in range(TS) for kv in range(HKV)]
        NU = len(UNITS)
        LAST = 4
        PIECES = [[] for _ in range(NU)]
        for n in range(NF):
            PIECES[min(NU - 1, n * NU // NF)].append(n)

        def slots():
            yield from ((-1, s, PIECES[s]) for s in range(NU))
            for b in range(B):
                for s in range(NU + (LAST if b == B - 1 else 0)):
                    yield b, s, PIECES[s] if b < B - 1 and s < NU else []

        def unit(b, s):
            return b * NU + s

        block = ctx.enter_context(nc.Block())

        @block.gpsimd
        def _(pool):
            for b, s, pieces in slots():
                for n in pieces:
                    if FRONT[n][:2] == ("xnT", 0):
                        pool.wait_ge(var_ready, b + 2)
                        pool.tensor_tensor(rstd[:, :], vareps[:, :], C["minus_half"][:, 0:TS], ALU.pow).then_inc(rstd_ready, 1)

        @block.vector
        def _(dve):
            own = Steps()
            dve.tensor_copy(identb[:, :], C["ident"]).then_inc(dve_done, own.step())
            dve.tensor_copy(hide[:, :, :], C["hide"].unsqueeze(1).broadcast_to([P, HALF, P])).then_inc(dve_done, own.step())
            dve.memset(qs[:, :, :, :], 0.0).then_inc(dve_done, own.step())
            dve.memset(ks[:, :, :, :], 0.0).then_inc(dve_done, own.step())
            for i in range(2):
                dve.memset(kz[i][:, :, :, :], 0.0).then_inc(dve_done, own.step())
                dve.memset(V[i][:, :, :, :], 0.0).then_inc(dve_done, own.step())
            dve.wait_ge(dve_done, own.n)
            dve.memset(ks[:, :, :, TYPES * HD:TYPES * HD + 3], 1.0).then_inc(dve_done, own.step())
            for i in range(2):
                dve.memset(V[i][:, :, :, HD:HD + 1], 1.0).then_inc(dve_done, own.step())
            dve.wait_ge(dve_done, own.n)

            def front(b, n):
                kind, t, m = FRONT[n]
                src = pf[n % 2]
                seen = NF * b + n + 1
                if (kind, t) == ("xnT", 0):
                    for q in range(TS):
                        dve.bn_stats(stats[:, q, :], x[:, TS * b + q, :]).then_inc(dve_done, own.step())
                    dve.wait_ge(dve_done, own.n)
                    for q in range(TS):
                        dve.bn_aggr(meanvar[:, q, :], stats[:, q, :]).then_inc(dve_done, own.step())
                    dve.wait_ge(dve_done, own.n)
                    dve.tensor_scalar(vareps[:, :], meanvar[:, :, 1], EPS, None, ALU.add).then_inc(var_ready, 1)
                    dve.wait_ge(rstd_ready, b + 1)
                    for q in range(TS):
                        dve.tensor_scalar(xn[:, q, :], x[:, TS * b + q, :], meanvar[:, q, 0:1], rstd[:, q:q + 1],
                                          ALU.subtract, ALU.mult).then_inc(xn_ready, 1)
                dve.wait_ge(front_in_psum, seen)
                if kind == "xnT":
                    dve.tensor_copy(xnT[:, :, t * P:(t + 1) * P], src[:, 0:KD * P].rearrange("p (k n) -> p k n", k=KD)).then_inc(front_taken, 1)
                if kind == "qkv":
                    cosT, sinT = C["cos"][:, t, :], C["sin"][:, t, :]
                    qk = src[:, 0:QK].rearrange("p (h j) -> p h j", j=2)
                    sn = sinT.rearrange("p (h j) -> p h j", j=2)
                    rb = ropeB[:, :].rearrange("p (h j) -> p h j", j=2)
                    dve.tensor_tensor(ropeA[:, :], src[:, 0:QK], cosT, ALU.mult).then_inc(dve_done, own.step())
                    dve.tensor_tensor(rb[:, :, 0], qk[:, :, 1], sn[:, :, 0], ALU.mult).then_inc(dve_done, own.step())
                    dve.tensor_tensor(rb[:, :, 1], qk[:, :, 0], sn[:, :, 1], ALU.mult).then_inc(dve_done, own.step())
                    if b >= 2:
                        dve.wait_ge(pv_done, unit(b - 1, 0))
                    dve.wait_ge(dve_done, own.n)
                    dve.tensor_copy(V[b % 2][:, t, :, 0:HD], src[:, QK:QKV].rearrange("p (h d) -> p h d", d=HD)).then_inc(front_taken, 1)
                    dve.tensor_tensor(ropeA[:, :], ropeA[:, :], ropeB[:, :], ALU.add).then_inc(dve_done, own.step())
                    dve.wait_ge(dve_done, own.n)
                    if TS * b + t >= 1:
                        dve.wait_ge(q1_copied, TS * b + t)
                    dve.tensor_copy(parts[:, 0, :], ropeA[:, :]).then_inc(dve_done, own.step())
                    dve.wait_ge(dve_done, own.n)
                    dve.tensor_tensor(ropeB[:, :], ropeA[:, :], parts[:, 0, :], ALU.subtract).then_inc(dve_done, own.step())
                    dve.wait_ge(dve_done, own.n)
                    dve.tensor_copy(parts[:, 1, :], ropeB[:, :]).then_inc(dve_done, own.step())
                    dve.wait_ge(dve_done, own.n)
                    dve.tensor_tensor(parts[:, 2, :], ropeB[:, :], parts[:, 1, :], ALU.subtract).then_inc(parts_ready, 1)
                    dve.wait_ge(parts_ready, TS * b + t + 1)
                    q2 = parts[:, 1, 0:H * HD].rearrange("p (h d) -> p h d", d=HD).unsqueeze(2).broadcast_to([P, H, 2, HD])
                    dve.tensor_copy(qs[:, t, :, 3 * HD:5 * HD].rearrange("p h (r d) -> p h r d", d=HD), q2).then_inc(dve_done, own.step())
                    dve.tensor_copy(qs[:, t, :, 5 * HD:6 * HD], parts[:, 2, 0:H * HD].rearrange("p (h d) -> p h d", d=HD)).then_inc(dve_done, own.step())
                    dve.memset(qs[:, t, :, TYPES * HD:TYPES * HD + 3], 0.0).then_inc(dve_done, own.step())
                    kp = parts[:, :, H * HD:QK].rearrange("p r (h d) -> p h r d", d=HD)
                    dve.tensor_copy(ks[:, t, :, 0:3 * HD].rearrange("p h (r d) -> p h r d", d=HD), kp).then_inc(dve_done, own.step())
                    dve.tensor_copy(ks[:, t, :, 3 * HD:5 * HD].rearrange("p h (r d) -> p h r d", d=HD), kp[:, :, 0:2, :]).then_inc(dve_done, own.step())
                    dve.tensor_copy(ks[:, t, :, 5 * HD:6 * HD], kp[:, :, 0, :]).then_inc(rows_ready, 1)
                if kind == "kT":
                    if b >= 2:
                        dve.wait_ge(scores_ready, unit(b - 1, 0))
                    kT = src[:, 0:G * P // 2].bitcast(BF16).rearrange("p (g n) -> p g n", g=G)
                    dve.tensor_copy(kz[b % 2][0:ROWS, :, 0, t * P:(t + 1) * P], kT[0:ROWS]).then_inc(dve_done, own.step())
                    dve.tensor_copy(kz[b % 2][ROWS:P, :, 1, t * P:(t + 1) * P], kT[ROWS:P]).then_inc(front_taken, 1)
                if kind in ("qTa", "qTb"):
                    if kind == "qTb" and b >= 2:
                        dve.wait_ge(scores_ready, unit(b - 1, 0))
                    dst = qTa if kind == "qTa" else qTb[b % 2][:, :, :, :].rearrange("p g i n -> p (g i) n")
                    dve.tensor_copy(dst[:, 8 * m:8 * m + 8, t * P:(t + 1) * P], src[:, :].bitcast(BF16).rearrange("p (g n) -> p g n", g=8)).then_inc(front_taken, 1)
                if kind == "max0":
                    dve.tensor_reduce(top[:, 0, 4 * m:4 * m + 4], src[:, :].rearrange("p (h s) -> p h s", h=4), AX.X, ALU.max).then_inc(front_taken, 1)
                if kind == "max1":
                    dve.tensor_reduce(top[:, 1, 2 * m:2 * m + 2], src[:, :].rearrange("p (h s) -> p h s", h=2), AX.X, ALU.max).then_inc(front_taken, 1)
                if (kind == "max0" and m == G * REP // 2 - 1) or (kind == "max1" and m == G * REP - 1):
                    at = TYPES * HD
                    dve.wait_ge(front_taken, seen)
                    dve.tensor_scalar(qs[:, t, :, at], top[:, t, :], -1.0, None, ALU.mult).then_inc(dve_done, own.step())
                    dve.wait_ge(dve_done, own.n)
                    dve.scalar_tensor_tensor(rest[:, :], top[:, t, :], -1.0, qs[:, t, :, at], ALU.mult, ALU.subtract).then_inc(dve_done, own.step())
                    dve.wait_ge(dve_done, own.n)
                    dve.tensor_copy(qs[:, t, :, at + 1], rest[:, :]).then_inc(dve_done, own.step())
                    dve.wait_ge(dve_done, own.n)
                    dve.tensor_tensor(qs[:, t, :, at + 2], rest[:, :], qs[:, t, :, at + 1], ALU.subtract).then_inc(max_rows_ready, 1)

            def tail(u):
                if u % 4 == 1 and u >= 5:
                    q = u // 4 - 1
                    t = q // 2
                    pot = ot[:, :].rearrange("p (i k r) -> p i k r", i=REP, k=4)
                    dve.wait_ge(o_in_psum, q + 1)
                    dve.reciprocal(recip[:, :, :], pot[:, :, :, HD]).then_inc(dve_done, own.step())
                    dve.wait_ge(dve_done, own.n)
                    for k in range(4):
                        ins = dve.tensor_tensor(y[:, t % TS, 4 * (q % 2) + k, :, :], pot[:, :, k, 0:HD],
                                                recip[:, :, k].unsqueeze(2).broadcast_to([P, REP, HD]), ALU.mult)
                        if k < 3:
                            ins.then_inc(dve_done, own.step())
                    ins.then_inc(y_ready, 1)
                if u % 8 == 2 and u >= 10:
                    t = u // 8 - 1
                    dve.wait_ge(yT_in_psum, t + 1)
                    dve.tensor_copy(yT[:, :, :], ot[:, 0:KD * P].rearrange("p (k n) -> p k n", k=KD)).then_inc(yT_ready, 1)
                if u % 8 == 3 and u >= 11:
                    t = u // 8 - 1
                    dve.wait_ge(wo_in_psum, t + 1)
                    dve.tensor_tensor(x[:, t, :], x[:, t, :], ot[:, 0:D], ALU.add).then_inc(x_ready, 1)

            for b, s, pieces in slots():
                for n in pieces:
                    front(b + 1, n)
                if b >= 0:
                    tail(unit(b, s))

        @block.scalar
        def _(act):
            for b, s, pieces in slots():
                if b >= 0 and s < NU:
                    u = unit(b, s)
                    tt = UNITS[s][0]
                    act.wait_ge(scores_ready, u + 1)
                    if u >= 2:
                        act.wait_ge(pv_done, u - 1)
                    act.activation(probs[u % 2][:, 0:(tt + 1) * 512], sT[u % 2][:, 0:(tt + 1) * 512], ACT.Exp).then_inc(probs_ready, 1)
                for n in pieces:
                    kind, t, m = FRONT[n]
                    if kind == "qkv":
                        act.wait_ge(parts_ready, TS * (b + 1) + t + 1)
                        if b + 1 >= 1:
                            act.wait_ge(front_in_psum, NF * (b + 1))
                        q1 = parts[:, 0, 0:H * HD].rearrange("p (h d) -> p h d", d=HD).unsqueeze(2).broadcast_to([P, H, 3, HD])
                        act.activation(qs[:, t, :, 0:3 * HD].rearrange("p h (r d) -> p h r d", d=HD), q1, ACT.Copy).then_inc(q1_copied, 1)
                u = unit(b, s)
                if b >= 0 and u % 4 == 0 and u >= 4:
                    q = u // 4 - 1
                    act.wait_ge(pv_done, u)
                    if q >= 1:
                        act.wait_ge(o_in_psum, q)
                    act.activation(oT[:, :, :], po[:, :].rearrange("p (i t) -> p i t", i=REP), ACT.Copy).then_inc(oT_ready, 1)

        @block.tensor
        def _(pe):
            ident = C["ident"]
            pe.wait_ge(dve_done, 11)

            def front(b, n):
                kind, t, m = FRONT[n]
                dst = pf[n % 2]
                seen = NF * b + n
                if seen >= 2:
                    pe.wait_ge(front_taken, seen - 1)
                if kind == "xnT":
                    pe.wait_ge(xn_ready, TS * b + t + 1)
                    for k in range(KD):
                        mm = pe.transpose(dst[:, k * P:(k + 1) * P], xn[:, t, k * P:(k + 1) * P], ident)
                if kind == "qkv":
                    pe.wait_ge(front_taken, NF * b + t + 1)
                    for k in range(KD):
                        mm = pe.matmul(dst[:, 0:QKV], xnT[:, k, t * P:(t + 1) * P], W["qkv"][:, k, :], start=(k == 0), stop=(k == KD - 1))
                if kind == "kT":
                    pe.wait_ge(rows_ready, TS * b + t + 1)
                    out = dst[:, 0:G * P // 2].bitcast(BF16)
                    for g in range(G):
                        mm = pe.transpose(out[:, g * P:(g + 1) * P], ks[:, t, 2 * g:2 * g + 2, :].rearrange("p h r -> p (h r)"), identb[:, :])
                if kind in ("qTa", "qTb"):
                    if kind == "qTa":
                        pe.wait_ge(rows_ready, TS * b + t + 1)
                        pe.wait_ge(q1_copied, TS * b + t + 1)
                    else:
                        pe.wait_ge(max_rows_ready, TS * b + t + 1)
                    out = dst[:, :].bitcast(BF16)
                    for g in range(8):
                        w = 8 * m + g
                        mm = pe.transpose(out[:, g * P:(g + 1) * P], qs[:, t, 2 * w:2 * w + 2, :].rearrange("p h r -> p (h r)"), identb[:, :])
                if kind == "max0":
                    if m == 0:
                        pe.wait_ge(front_taken, NF * b + FRONT.index(("qTa", 1, 1)) + 1)
                    for w in range(2):
                        pair = 2 * m + w
                        out = dst[:, w * 256:(w + 1) * 256]
                        pe.matmul(out, qTa[:, pair, 0:P], kz[b % 2][:, pair // REP, :, 0:P], start=True, stop=False)
                        mm = pe.matmul(out, identb[:, :], hide[:, :, :], start=False, stop=True)
                if kind == "max1":
                    pe.matmul(dst[:, :], qTa[:, m, P:2 * P], kz[b % 2][:, m // REP, :, :], start=True, stop=False)
                    mm = pe.matmul(dst[:, :].rearrange("p (h s) -> p h s", h=2)[:, :, P:2 * P], identb[:, :], hide[:, :, :], start=False, stop=True)
                mm.then_inc(front_in_psum, 1)

            def scores(b, s):
                u = unit(b, s)
                tt, kv = UNITS[s]
                if s == 0:
                    pe.wait_ge(front_taken, NF * (b + 1))
                if u >= 2:
                    pe.wait_ge(probs_ready, u - 1)
                for sbk in range(tt + 1):
                    pe.matmul(sT[u % 2][:, sbk * 512:(sbk + 1) * 512], kz[b % 2][:, kv // 2, kv % 2, sbk * P:(sbk + 1) * P],
                                   qTb[b % 2][:, kv // 2, :, tt * P:(tt + 1) * P], start=True, stop=(sbk < tt))
                pe.matmul(sT[u % 2][:, tt * 512:(tt + 1) * 512], hide[:, 0, :], identb[:, :].unsqueeze(1).broadcast_to([P, REP, P]),
                          start=False, stop=True).then_inc(scores_ready, 1)

            def weigh(u):
                b, s = u // NU, u % NU
                tt, kv = UNITS[s]
                pe.wait_ge(probs_ready, u + 1)
                if u % 4 == 0 and u >= 4:
                    pe.wait_ge(oT_ready, u // 4)
                rows = po[32 * (kv % 4):32 * (kv % 4) + 32, :]
                for sbk in range(tt + 1):
                    mm = pe.matmul(rows, V[b % 2][:, sbk, kv, :], probs[u % 2][:, sbk * 512:(sbk + 1) * 512], start=(sbk == 0), stop=(sbk == tt))
                mm.then_inc(pv_done, 1)

            def tail(u):
                if u % 4 == 1 and u >= 5:
                    q = u // 4 - 1
                    pe.wait_ge(oT_ready, q + 1)
                    if q >= 2 and q % 2 == 0:
                        pe.wait_ge(x_ready, q // 2)
                    if q % 2 == 1:
                        pe.wait_ge(y_ready, q)
                    for i in range(REP):
                        mm = pe.transpose(ot[:, i * P:(i + 1) * P], oT[:, i, :], ident)
                    mm.then_inc(o_in_psum, 1)
                if u % 8 == 2 and u >= 10:
                    t = u // 8 - 1
                    pe.wait_ge(y_ready, 2 * t + 2)
                    flat = y[:, t % TS, :, :, :].rearrange("p h i d -> p (h i d)")
                    for k in range(KD):
                        mm = pe.transpose(ot[:, k * P:(k + 1) * P], flat[:, k * P:(k + 1) * P], ident)
                    mm.then_inc(yT_in_psum, 1)
                if u % 8 == 3 and u >= 11:
                    t = u // 8 - 1
                    pe.wait_ge(yT_ready, t + 1)
                    for k in range(KD):
                        mm = pe.matmul(ot[:, 0:D], yT[:, k, :], W["wo"][:, k, :], start=(k == 0), stop=(k == KD - 1))
                    mm.then_inc(wo_in_psum, 1)

            for b, s, pieces in slots():
                if b >= 0 and s < NU:
                    scores(b, s)
                for n in pieces:
                    front(b + 1, n)
                if b >= 0:
                    u = unit(b, s)
                    if 1 <= u <= B * NU:
                        weigh(u - 1)
                    tail(u)



D_IN, HEADS, PD, NS, TAPS = 512, 64, 8, 128, 4
Q = 32
CB_ = D_IN // P
NB = CB_ + 2
NCH = L // Q
CPT = P // Q
HG = HEADS // CPT
PAD = TAPS - 1


def ssd_stage(nc, x, W, tag, load):
    with ExitStack() as ctx:
        def sb(name, shape, dt=F32):
            return ctx.enter_context(nc.sbuf_tensor(tag + name, shape, dt))

        def ps(name, shape, dt=F32):
            return ctx.enter_context(nc.psum_tensor(tag + name, shape, dt))

        def sem(name):
            return ctx.enter_context(nc.semaphore(tag + name))

        C = W["consts"]
        stats = sb("stats", [P, NT, 6])
        meanvar = sb("meanvar", [P, NT, 2])
        rstd = sb("rstd", [P, NT])
        vareps = sb("vareps", [P, NT])
        xnT = sb("xnT", [P, KD, TOK])
        raw = sb("raw", [P, NB, PAD + L])
        conv = sb("conv", [P, NB, L])
        xT, BT = conv[:, 0:CB_, :], conv[:, CB_, :]
        CT = [sb(f"CT{i}", [P, L]) for i in range(2)]
        gates = sb("gates", [P, 2, TS, D_IN])
        gate = [gates[:, i, :, :] for i in range(2)]
        dt = sb("dt", [P, NT, HEADS])
        dA = sb("dA", [P, NT, HEADS])
        dAq = sb("dAq", [P, B * NCH, HG])
        decays = sb("decays", [P, 2, NT, HEADS])
        chdec = sb("chdec", [P, CPT, NT, HEADS])
        cbm = [sb(f"cbm{i}", [P, NCH, Q]) for i in range(2)]
        xdt = sb("xdt", [P, D_IN])
        xdec = [sb(f"xdec{i}", [P, D_IN]) for i in range(3)]
        xD = [sb(f"xD{i}", [P, D_IN]) for i in range(3)]
        xbd = [W["spare"][:, i, :].rearrange("p (c g f d) -> p c g f d", c=CPT, g=HG, f=CPT) for i in range(3)]
        Bz = [sb(f"Bz{i}", [P, CPT, NS]) for i in range(3)]
        spread = [sb(f"spread{i}", [P, HG, Q]) for i in range(2)]
        mix = [sb(f"mix{i}", [P, HG, Q]) for i in range(2)]
        S = [sb(f"S{i}", [P, D_IN]) for i in range(2)]
        Sd = sb("Sd", [P, D_IN])
        y1 = sb("y1", [P, D_IN])
        y2 = sb("y2", [P, D_IN])
        sq = sb("sq", [P, 1])
        msq = sb("msq", [P, 1])
        rms = sb("rms", [P, 1])
        yT = sb("yT", [P, CB_, P])
        Arow = sb("Arow", [P, HEADS])
        negA = sb("negA", [P, HEADS])
        wo = W["ssd_out"]
        zerob = sb("zerob", [P, 512], BF16)
        xn = gates[:, :, :, :].rearrange("p i t (u n) -> p (i t u) n", n=D)
        dtabs, dtpos, dtT = y1, y2, Sd

        pf = [ps(f"pf{i}", [P, 512]) for i in range(2)]
        pseg = [ps(f"pseg{i}", [P, 512]) for i in range(2)]
        pst = ps("pst", [P, 512])
        pyd = ps("pyd", [P, 512])
        pyo = ps("pyo", [P, 512])
        pz = ps("pz", [P, 512])

        dve_done = sem("dve_done")
        act_done = sem("act_done")
        prepared = sem("prepared")
        var_ready = sem("var_ready")
        rstd_ready = sem("rstd_ready")
        xn_ready = sem("xn_ready")
        front_in_psum = sem("front_in_psum")
        taken = {"act": sem("taken_by_act"), "dve": sem("taken_by_dve")}
        conv_ready = sem("conv_ready")
        channels_ready = sem("channels_ready")
        soft_ready = sem("soft_ready")
        dtT_ready = sem("dtT_ready")
        dA_ready = sem("dA_ready")
        dAq_ready = sem("dAq_ready")
        xbd_ready = sem("xbd_ready")
        xdt_ready = sem("xdt_ready")
        spread_ready = sem("spread_ready")
        seg_ready = sem("seg_ready")
        exp_ready = sem("exp_ready")
        mix_ready = sem("mix_ready")
        state_in_psum = sem("state_in_psum")
        decayed = sem("decayed")
        state_ready = sem("state_ready")
        yoff_done = sem("yoff_done")
        ydiag_done = sem("ydiag_done")
        y_taken = sem("y_taken")
        y_ready = sem("y_ready")
        sq_ready = sem("sq_ready")
        msq_ready = sem("msq_ready")
        rms_ready = sem("rms_ready")
        yT_in_psum = sem("yT_in_psum")
        yT_ready = sem("yT_ready")
        out_in_psum = sem("out_in_psum")
        x_ready = sem("x_ready")
        wo_ready = sem("wo_ready")

        SEQ = ([("xnT", 0, q, "act", -1) for q in range(NT // 2)] + [("dtT", 0, 0, "act", -1)]
               + [("conv", 0, i, "act", -1) for i in range(NB // 2)] + [("dt", 0, 0, "dve", -1)]
               + [("gate", 0, t, "act", -1) for t in range(TS)] + [("decays", 0, w, "act", -1) for w in range(2)]
               + [("chdec", 0, c4, "act", -1) for c4 in range(CPT)] + [("cb", 0, 0, "dve", -1)]
               + [(kind, 0, t, who, -1) for t in range(TS) for kind, who in (("xtok", "dve"), ("btok", "act"))])
        for nb in range(1, B):
            first = (nb - 1) * NCH
            SEQ += ([("conv", nb, i, "act", first + i // 2) for i in range(NB // 2)] + [("gate", nb, t, "act", first + 3) for t in range(TS)]
                    + [("cb", nb, 0, "dve", first + 4)]
                    + [(kind, nb, t, who, first + 5 + t) for t in range(TS) for kind, who in (("xtok", "dve"), ("btok", "act"))])
        GO = {g: [n for n, f in enumerate(SEQ) if f[4] == g] for g in range(-1, B * NCH + 4)}

        def take_no(n):
            who = SEQ[n][3]
            return taken[who], sum(f[3] == who for f in SEQ[:n + 1])

        def place(kind, b, t=0):
            return next(n for n, f in enumerate(SEQ) if f[:3] == (kind, b, t))

        NG = B * NCH
        SLOTS = range(-1, NG + 4)

        def tile_at(g, after):
            T = (g - after) // CPT - 1
            return T if (g - after) % CPT == 0 and 0 <= T < NT else None

        block = ctx.enter_context(nc.Block())

        @block.sync
        def _(sp):
            load(sp)

        @block.gpsimd
        def _(pool):
            pool.memset(raw[:, :, 0:PAD], 0.0).then_inc(prepared, 1)
            pool.memset(zerob[:, :], 0.0).then_inc(prepared, 1)
            pool.wait_ge(W["loaded"]["common"], 16)
            pool.wait_ge(var_ready, 1)
            pool.tensor_tensor(rstd[:, :], vareps[:, :], C["minus_half"], ALU.pow).then_inc(rstd_ready, 1)
            for i in range(3):
                pool.memset(xbd[i], 0.0).then_inc(prepared, 1)
                pool.memset(Bz[i][:, :, :], 0.0).then_inc(prepared, 1)
            pool.wait_ge(W["loaded"]["for_ssd"], 16)
            pool.wait_ge(dAq_ready, 1)
            for g in SLOTS:
                if 0 <= g < NG:
                    if g >= 2:
                        pool.wait_ge(seg_ready, g - 1)
                    pool.tensor_tensor(spread[g % 2][:, :, :], dAq[:, g, :].unsqueeze(2).broadcast_to([P, HG, Q]),
                                       C["tri"].unsqueeze(1).broadcast_to([P, HG, Q]), ALU.mult).then_inc(spread_ready, 1)
                g1 = g - 1
                if 0 <= g1 < NG and 1 <= g1 % NCH < NCH - 1:
                    b, c = g1 // NCH, g1 % NCH
                    pool.wait_ge(state_ready, b * (NCH - 1) + c)
                    dec = chdec[:, c % CPT, g1 // CPT, :].unsqueeze(2).broadcast_to([P, HEADS, PD])
                    pool.tensor_tensor(Sd[:, :].rearrange("p (h d) -> p h d", d=PD), S[c % 2][:, :].rearrange("p (h d) -> p h d", d=PD),
                                       dec, ALU.mult).then_inc(decayed, 1)
                T = tile_at(g, 2)
                if T is not None:
                    pool.wait_ge(msq_ready, T + 1)
                    pool.tensor_tensor(rms[:, :], msq[:, :], C["minus_half"][:, 0:1], ALU.pow).then_inc(rms_ready, 1)

        @block.vector
        def _(dve):
            own = Steps()
            dve.memset(W["zeros"], 0.0).then_inc(W["zeros_ready"], 1)
            for t in range(NT):
                if t % 2 == 0:
                    dve.wait_ge(W["loaded"]["x"][t // 2], 16)
                dve.bn_stats(stats[:, t, :], x[:, t, :]).then_inc(dve_done, own.step())
            dve.wait_ge(dve_done, own.n)
            for t in range(NT):
                dve.bn_aggr(meanvar[:, t, :], stats[:, t, :]).then_inc(dve_done, own.step())
            dve.wait_ge(dve_done, own.n)
            dve.tensor_scalar(vareps[:, :], meanvar[:, :, 1], EPS, None, ALU.add).then_inc(var_ready, 1)
            dve.wait_ge(rstd_ready, 1)
            for t in range(NT):
                dve.tensor_scalar(xn[:, t, :], x[:, t, :], meanvar[:, t, 0:1], rstd[:, t:t + 1],
                                  ALU.subtract, ALU.mult).then_inc(xn_ready, 1)
            dve.wait_ge(act_done, 1)
            dve.tensor_scalar(negA[:, :], Arow[:, :], -1.0, None, ALU.mult).then_inc(dve_done, own.step())
            dve.wait_ge(dve_done, own.n)
            dve.wait_ge(W["loaded"]["for_ssd"], 16)
            dve.wait_ge(prepared, 8)

            def front(n):
                kind, b, t = SEQ[n][:3]
                src = pf[n % 2]
                if kind == "dtT":
                    dve.wait_ge(soft_ready, 1)
                    dve.tensor_tensor(dtT[:, :], dtT[:, :], dtpos[:, :], ALU.add).then_inc(dtT_ready, 1)
                if kind == "conv":
                    dve.wait_ge(*take_no(n))
                    for i in range(PAD):
                        for m in (2 * t, 2 * t + 1):
                            ins = dve.scalar_tensor_tensor(conv[:, m, :], raw[:, m, i:i + L], C["conv_w"][:, m * TAPS + i:m * TAPS + i + 1],
                                                           conv[:, m, :], ALU.mult, ALU.add)
                            if i < PAD - 1:
                                ins.then_inc(dve_done, own.step())
                            else:
                                ins.then_inc(conv_ready, 1)
                        if i < PAD - 1:
                            dve.wait_ge(dve_done, own.n)
                if kind == "dt":
                    dve.wait_ge(front_in_psum, n + 1)
                    dve.tensor_copy(dt[:, :, :].rearrange("p (u k) h -> p k u h", u=2),
                                    src[:, :].rearrange("p (k u h) -> p k u h", u=2, h=HEADS)).then_inc(take_no(n)[0], 1)
                    dve.wait_ge(*take_no(n))
                    dve.tensor_tensor(dA[:, :, :], dt[:, :, :], negA[:, :].unsqueeze(1).broadcast_to([P, NT, HEADS]), ALU.mult).then_inc(dA_ready, 1)
                    dve.wait_ge(dA_ready, 1)
                    for c4 in range(CPT):
                        for h4 in range(CPT):
                            ins = dve.tensor_copy(dAq[Q * h4:Q * h4 + Q, c4::CPT, :],
                                                  dA[Q * c4:Q * c4 + Q, :, h4::CPT])
                            if (c4, h4) != (CPT - 1, CPT - 1):
                                ins.then_inc(dve_done, own.step())
                    ins.then_inc(dAq_ready, 1)
                if kind == "cb":
                    dve.wait_ge(front_in_psum, n + 1)
                    for c4 in range(CPT):
                        for h4 in range(CPT):
                            ins = dve.tensor_tensor(cbm[b % 2][Q * h4:Q * h4 + Q, c4::CPT, :],
                                                    src[Q * c4:Q * c4 + Q, 0:L].rearrange("p (t n) -> p t n", n=P)[:, :, Q * c4:Q * c4 + Q],
                                                    C["tri"][Q * c4:Q * c4 + Q, :].unsqueeze(1).broadcast_to([Q, TS, Q]), ALU.mult)
                            if (c4, h4) != (CPT - 1, CPT - 1):
                                ins.then_inc(dve_done, own.step())
                    ins.then_inc(take_no(n)[0], 1)
                if kind == "xtok":
                    T = TS * b + t
                    dve.wait_ge(front_in_psum, n + 1)
                    xt = src[:, :].rearrange("p (h d) -> p h d", d=PD)
                    if T >= 1:
                        dve.wait_ge(xbd_ready, T)
                    dve.tensor_tensor(xdt[:, :].rearrange("p (h d) -> p h d", d=PD), xt, dt[:, T, :].unsqueeze(2).broadcast_to([P, HEADS, PD]),
                                      ALU.mult).then_inc(xdt_ready, 1)
                    dve.tensor_tensor(xD[T % 3][:, :].rearrange("p (h d) -> p h d", d=PD), xt, C["D"].unsqueeze(2).broadcast_to([P, HEADS, PD]),
                                      ALU.mult).then_inc(take_no(n)[0], 1)
                    dve.wait_ge(xdt_ready, T + 1)
                    if T == 0:
                        dve.wait_ge(*take_no(place("decays", 0, 1)))
                    dve.tensor_tensor(xdec[T % 3][:, :].rearrange("p (h d) -> p h d", d=PD), xdt[:, :].rearrange("p (h d) -> p h d", d=PD),
                                      decays[:, 1, T, :].unsqueeze(2).broadcast_to([P, HEADS, PD]), ALU.mult).then_inc(dve_done, own.step())
                    src4 = xdt[:, :].rearrange("p (g f d) -> p g f d", f=CPT, d=PD)
                    for c4 in range(CPT):
                        for h4 in range(CPT):
                            ins = dve.tensor_copy(xbd[T % 3][Q * h4:Q * h4 + Q, c4, :, h4, :], src4[Q * c4:Q * c4 + Q, :, h4, :])
                            if (c4, h4) != (CPT - 1, CPT - 1):
                                ins.then_inc(dve_done, own.step())
                    ins.then_inc(xbd_ready, 1)

            for g in SLOTS:
                if g == 0:
                    dve.wait_ge(W["loaded"]["ssd_out"], 16)
                    for k in range(CB_):
                        ins = dve.tensor_scalar(wo[:, k, :], wo[:, k, :], C["norm_w"][:, k:k + 1], None, ALU.mult)
                        if k < CB_ - 1:
                            ins.then_inc(dve_done, own.step())
                    ins.then_inc(wo_ready, 1)
                g1 = g - 1
                if 0 <= g1 < NG and g1 % NCH < NCH - 1:
                    b, c = g1 // NCH, g1 % NCH
                    no = b * (NCH - 1) + c + 1
                    dve.wait_ge(state_in_psum, no)
                    if g1 >= 1:
                        dve.wait_ge(yoff_done, g1)
                    if c == 0:
                        if b >= 1:
                            dve.wait_ge(decayed, b * (NCH - 2))
                        dve.tensor_copy(S[1][:, :], pst[:, :]).then_inc(state_ready, 1)
                    else:
                        dve.wait_ge(decayed, b * (NCH - 2) + c)
                        dve.tensor_tensor(S[(c + 1) % 2][:, :], Sd[:, :], pst[:, :], ALU.add).then_inc(state_ready, 1)
                if 0 <= g < NG:
                    b, c = g // NCH, g % NCH
                    dve.wait_ge(exp_ready, g + 1)
                    dve.tensor_tensor(mix[g % 2][:, :, :], mix[g % 2][:, :, :], cbm[b % 2][:, c, :].unsqueeze(1).broadcast_to([P, HG, Q]),
                                      ALU.mult).then_inc(mix_ready, 1)
                T = tile_at(g, 0)
                if T is not None:
                    b, t = T // TS, T % TS
                    dve.wait_ge(ydiag_done, CPT * (T + 1))
                    if T >= 1:
                        dve.wait_ge(yT_in_psum, T)
                        dve.wait_ge(sq_ready, T)
                    dve.tensor_tensor(y1[:, :].rearrange("p (h d) -> p h d", d=PD), pyo[:, :].rearrange("p (h d) -> p h d", d=PD),
                                      decays[:, 0, T, :].unsqueeze(2).broadcast_to([P, HEADS, PD]), ALU.mult).then_inc(dve_done, own.step())
                    dve.tensor_tensor(y2[:, :], xD[T % 3][:, :], pyd[:, :], ALU.add).then_inc(y_taken, 1)
                    dve.wait_ge(dve_done, own.n)
                    dve.wait_ge(y_taken, T + 1)
                    dve.tensor_tensor(y1[:, :], y1[:, :], y2[:, :], ALU.add).then_inc(dve_done, own.step())
                    dve.wait_ge(dve_done, own.n)
                    dve.tensor_tensor(y1[:, :], y1[:, :], gate[b % 2][:, t, :], ALU.mult).then_inc(y_ready, 1)
                T = tile_at(g, 2)
                if T is not None:
                    dve.wait_ge(sq_ready, T + 1)
                    dve.tensor_scalar(msq[:, :], sq[:, :], 1.0 / D_IN, EPS, ALU.mult, ALU.add).then_inc(msq_ready, 1)
                T = tile_at(g, 3)
                if T is not None:
                    dve.wait_ge(out_in_psum, T + 1)
                    dve.wait_ge(rms_ready, T + 1)
                    dve.scalar_tensor_tensor(x[:, T, :], pz[:, 0:D], rms[:, 0:1], x[:, T, :], ALU.mult, ALU.add).then_inc(x_ready, 1)
                for n in GO[g]:
                    front(n)

        @block.scalar
        def _(act):
            own = Steps()
            act.wait_ge(W["loaded"]["for_ssd"], 16)
            act.activation(Arow[:, :], C["A_log"], ACT.Exp).then_inc(act_done, own.step())

            def front(n):
                kind, b, t, who, _ = SEQ[n]
                src = pf[n % 2]
                if who == "act":
                    act.wait_ge(front_in_psum, n + 1)
                    tk = take_no(n)[0]
                if kind == "xnT":
                    act.activation(xnT[:, :, t * L:(t + 1) * L], src[:, :].rearrange("p (k n) -> p k n", k=KD), ACT.Copy).then_inc(tk, 1)
                if kind == "dtT":
                    act.activation(dtabs[:, :], src[:, :], ACT.Abs, bias=C["dt_bias"]).then_inc(act_done, own.step())
                    act.activation(dtpos[:, :], src[:, :], ACT.Relu, bias=C["dt_bias"]).then_inc(tk, 1)
                    act.wait_ge(act_done, own.n)
                    act.activation(dtabs[:, :], dtabs[:, :], ACT.Exp, scale=-1.0).then_inc(act_done, own.step())
                    act.wait_ge(act_done, own.n)
                    act.activation(dtT[:, :], dtabs[:, :], ACT.Ln, bias=1.0).then_inc(soft_ready, 1)
                if kind == "conv":
                    s3 = src[:, :].rearrange("p (m n) -> p m n", m=2)
                    if b >= 1:
                        act.wait_ge(conv_ready, NB * b)
                        act.wait_ge(channels_ready, NB * b)
                        act.wait_ge(front_in_psum, place("btok", b - 1, TS - 1) + 1)
                    for i in range(2):
                        m = 2 * t + i
                        act.activation(conv[:, m, :], s3[:, i, :], ACT.Identity, bias=C["conv_b"][:, m:m + 1],
                                       scale=C["conv_w"][:, m * TAPS + PAD:m * TAPS + PAD + 1]).then_inc(act_done, own.step())
                    act.activation(raw[:, 2 * t:2 * t + 2, PAD:], s3, ACT.Copy).then_inc(tk, 1)
                    act.wait_ge(act_done, own.n)
                if kind == "gate":
                    act.activation(gate[b % 2][:, t, :], src[:, :], ACT.Silu).then_inc(tk, 1)
                    if t == 1:
                        for m in range(NB):
                            act.wait_ge(conv_ready, NB * b + m + 1)
                            dst = conv[:, m, :] if m <= CB_ else CT[b % 2][:, :]
                            act.activation(dst, conv[:, m, :], ACT.Silu).then_inc(channels_ready, 1)
                if kind == "decays":
                    act.activation(decays[:, t, :, :], src[:, :].rearrange("p (t h) -> p t h", t=NT), ACT.Exp).then_inc(tk, 1)
                if kind == "chdec":
                    act.activation(chdec[:, t, :, :], src[:, :].rearrange("p (t h) -> p t h", t=NT), ACT.Exp).then_inc(tk, 1)
                if kind == "btok":
                    T = TS * b + t
                    act.wait_ge(prepared, 8)
                    for c4 in range(CPT):
                        rows = slice(Q * c4, Q * c4 + Q)
                        ins = act.activation(Bz[T % 3][rows, c4, :], src[rows, 0:NS], ACT.Copy)
                        if c4 < CPT - 1:
                            ins.then_inc(act_done, own.step())
                    ins.then_inc(tk, 1)

            for g in SLOTS:
                if 0 <= g < NG:
                    act.wait_ge(seg_ready, g + 1)
                    if g >= 2:
                        act.wait_ge(ydiag_done, g - 1)
                    act.activation(mix[g % 2][:, :, :], pseg[g % 2][:, :].rearrange("p (h t) -> p h t", t=Q), ACT.Exp).then_inc(exp_ready, 1)
                T = tile_at(g, 1)
                if T is not None:
                    act.wait_ge(y_ready, T + 1)
                    if T >= 1:
                        act.wait_ge(msq_ready, T)
                    act.activation(y2[:, :], y1[:, :], ACT.Square, accum_out=sq[:, :]).then_inc(sq_ready, 1)
                T = tile_at(g, 2)
                if T is not None:
                    act.wait_ge(yT_in_psum, T + 1)
                    act.activation(yT[:, :, :], pz[:, :].rearrange("p (k n) -> p k n", k=CB_), ACT.Copy).then_inc(yT_ready, 1)
                for n in GO[g]:
                    front(n)

        @block.tensor
        def _(pe):
            ident = C["ident"]
            pe.wait_ge(W["loaded"]["common"], 16)

            def front(n):
                kind, b, t = SEQ[n][:3]
                dst = pf[n % 2]
                if n >= 2:
                    pe.wait_ge(*take_no(n - 2))
                if kind == "xnT":
                    for r in range(2):
                        pe.wait_ge(xn_ready, 2 * t + r + 1)
                        for k in range(KD):
                            mm = pe.transpose(dst[:, k * L + r * P:k * L + (r + 1) * P], xn[:, 2 * t + r, k * P:(k + 1) * P], ident)
                if kind == "dtT":
                    pe.wait_ge(W["loaded"]["ssd_in"], 16)
                    pe.wait_ge(*take_no(place("xnT", 0, NT // 2 - 1)))
                    for u in range(2):
                        for k in range(KD):
                            mm = pe.matmul(dst[u * HEADS:(u + 1) * HEADS, :], W["ssd_in"][:, k, D_IN + NB * P:], xnT[:, k, u * 512:(u + 1) * 512],
                                           start=(k == 0), stop=(k == KD - 1))
                if kind == "conv":
                    for i in range(2):
                        m = 2 * t + i
                        for k in range(KD):
                            mm = pe.matmul(dst[:, i * L:(i + 1) * L], W["ssd_in"][:, k, D_IN + m * P:D_IN + (m + 1) * P], xnT[:, k, b * L:(b + 1) * L],
                                           start=(k == 0), stop=(k == KD - 1))
                if kind == "gate":
                    for k in range(KD):
                        mm = pe.matmul(dst[:, :], xnT[:, k, (TS * b + t) * P:(TS * b + t + 1) * P], W["ssd_in"][:, k, 0:D_IN],
                                       start=(k == 0), stop=(k == KD - 1))
                if kind == "dt":
                    pe.wait_ge(dtT_ready, 1)
                    for q in range(NT // 2):
                        mm = pe.transpose(dst[:, q * P:(q + 1) * P], dtT[:, q * P:(q + 1) * P], ident)
                if kind in ("decays", "chdec"):
                    pe.wait_ge(W["loaded"]["for_ssd"], 16)
                    pe.wait_ge(dA_ready, 1)
                    lhsT = C["rows_of"][:, t * P:(t + 1) * P] if kind == "chdec" else C[("upto_t", "behind")[t]]
                    mm = pe.matmul(dst[:, :], lhsT, dA[:, :, :].rearrange("p t h -> p (t h)"), start=True, stop=True)
                if kind == "cb":
                    pe.wait_ge(channels_ready, NB * (b + 1))
                    for q in range(TS):
                        mm = pe.matmul(dst[:, q * P:(q + 1) * P], BT[:, q * P:(q + 1) * P], CT[b % 2][:, q * P:(q + 1) * P], start=True, stop=True)
                if kind == "xtok":
                    for k in range(CB_):
                        mm = pe.transpose(dst[:, k * P:(k + 1) * P], xT[:, k, t * P:(t + 1) * P], ident)
                if kind == "btok":
                    mm = pe.transpose(dst[:, 0:NS], BT[:, t * P:(t + 1) * P], ident)
                mm.then_inc(front_in_psum, 1)

            for g in SLOTS:
                if 0 <= g < NG:
                    pe.wait_ge(spread_ready, g + 1)
                    if g >= 2:
                        pe.wait_ge(exp_ready, g - 1)
                    pe.matmul(pseg[g % 2][:, :], C["behind"], spread[g % 2][:, :, :].rearrange("p h t -> p (h t)"), start=True, stop=True).then_inc(seg_ready, 1)
                g1 = g - 1
                if 0 <= g1 < NG:
                    b, c = g1 // NCH, g1 % NCH
                    T, c4 = g1 // CPT, c % CPT
                    if c < NCH - 1:
                        no = b * (NCH - 1) + c
                        if c4 == 0:
                            pe.wait_ge(*take_no(place("btok", b, T % TS)))
                            pe.wait_ge(xbd_ready, T + 1)
                        if no >= 1:
                            pe.wait_ge(state_ready, no)
                        pe.matmul(pst[:, :], Bz[T % 3][:, c4, :], xdec[T % 3][:, :], start=True, stop=True).then_inc(state_in_psum, 1)
                for n in GO[g]:
                    front(n)
                if 0 <= g1 < NG:
                    if c4 == 0 and T >= 1:
                        pe.wait_ge(y_taken, T)
                    rows = slice(Q * c4, Q * c4 + Q)
                    if c == 0:
                        pe.wait_ge(prepared, 2)
                        pe.matmul(pyo[rows, :], zerob[:, 0:Q], zerob[:, :], start=True, stop=True).then_inc(yoff_done, 1)
                    else:
                        pe.wait_ge(state_ready, b * (NCH - 1) + c)
                        pe.matmul(pyo[rows, :], CT[b % 2][:, c * Q:(c + 1) * Q], S[c % 2][:, :], start=True, stop=True).then_inc(yoff_done, 1)
                    pe.wait_ge(mix_ready, g1 + 1)
                    for h in range(HG):
                        mm = pe.matmul(pyd[rows, h * Q:(h + 1) * Q], mix[g1 % 2][:, h, :], xbd[T % 3][:, c4, h, :, :].rearrange("p f d -> p (f d)"),
                                       start=True, stop=True)
                    mm.then_inc(ydiag_done, 1)
                T = tile_at(g, 1)
                if T is not None:
                    pe.wait_ge(y_ready, T + 1)
                    if T >= 1:
                        pe.wait_ge(x_ready, T)
                    for k in range(CB_):
                        mm = pe.transpose(pz[:, k * P:(k + 1) * P], y1[:, k * P:(k + 1) * P], ident)
                    mm.then_inc(yT_in_psum, 1)
                T = tile_at(g, 2)
                if T is not None:
                    pe.wait_ge(wo_ready, 1)
                    pe.wait_ge(yT_ready, T + 1)
                    for k in range(CB_):
                        mm = pe.matmul(pz[:, 0:D], yT[:, k, :], wo[:, k, :], start=(k == 0), stop=(k == CB_ - 1))
                    mm.then_inc(out_in_psum, 1)


COMMON = [("ident", P), ("ones", P), ("below", P), ("minus_half", NT), ("weigh", NT * E), ("steps", E * NT),
          ("upto", E * E), ("tile_no", NR * E)]
FOR_SSD = [("tri", Q), ("behind", P), ("upto_t", P), ("rows_of", CPT * P), ("A_log", HEADS), ("D", HEADS), ("dt_bias", 1),
           ("conv_w", NB * TAPS), ("conv_b", NB), ("norm_w", CB_)]
FOR_ATT = [("hide", P), ("cos", TS * QK), ("sin", TS * QK)]


LATE = 3


def views(buffer, fields):
    got, at = {}, 0
    for name, width in fields:
        got[name] = buffer[:, at:at + width]
        at += width
    return got


def width_of(fields):
    return sum(width for _, width in fields)


def hybrid_layer(nc, hidden, ssd_in, ssd_out, qkv, wo, gate_up, down, router, common, for_ssd, for_att, out):
    slots_x = nc.dram_tensor("slots_x", [NR * P, D], F32).ap()
    slots_y = nc.dram_tensor("slots_y", [NR * P, D], F32).ap()
    with ExitStack() as ctx:
        def sb(stack, name, shape):
            return stack.enter_context(nc.sbuf_tensor(name, shape, F32))

        def sem(name):
            return ctx.enter_context(nc.semaphore(name))

        x = sb(ctx, "x", [P, NT, D])
        common_sb = sb(ctx, "common_sb", [P, width_of(COMMON)])
        router_sb = sb(ctx, "router_sb", [P, KD, E])
        gate_up_sb = sb(ctx, "gate_up_sb", [P, E + 1, KD, 2 * FI])
        loaded = {name: sem(name + "_loaded") for name in ("common", "for_ssd", "ssd_in", "ssd_out")}
        loaded["x"] = [sem(f"x_loaded{i}") for i in range(NT // 2)]
        zeros_ready = sem("zeros_ready")
        slots_cleared = sem("slots_cleared")
        expert_loads = sem("expert_loads")
        late_loads = [sem("shared_down_load"), sem("routed_loads")]
        att_loads = sem("att_loads")
        stored = sem("stored")

        C = views(common_sb, COMMON)
        for name, inner in (("weigh", E), ("steps", NT), ("upto", E)):
            C[name] = C[name].rearrange("p (a b) -> p a b", b=inner)
        C["tile_no"] = C["tile_no"][0:1, :].rearrange("p (a b) -> p a b", b=E)
        W = dict(consts=C, slots_x=slots_x, slots_y=slots_y, gate_up=gate_up_sb, router=router_sb)

        with ExitStack() as ssd_ctx:
            ssd_in_sb = sb(ssd_ctx, "ssd_in_sb", [P, KD, D_IN + NB * P + HEADS])
            ssd_out_sb = sb(ssd_ctx, "ssd_out_sb", [P, CB_, D])
            for_ssd_sb = sb(ssd_ctx, "for_ssd_sb", [P, width_of(FOR_SSD)])
            zeros = sb(ssd_ctx, "zeros", [P, D])

            def load_first(sp):
                for i in range(NT // 2):
                    sp.dma_start(x[:, 2 * i:2 * i + 2, :], hidden[:, 2 * i:2 * i + 2, :]).then_inc(loaded["x"][i], 16)
                    if i == 0:
                        sp.dma_start(common_sb[:, :], common).then_inc(loaded["common"], 16)
                sp.dma_start(ssd_in_sb[:, :, :], ssd_in).then_inc(loaded["ssd_in"], 16)
                sp.dma_start(for_ssd_sb[:, :], for_ssd).then_inc(loaded["for_ssd"], 16)
                sp.dma_start(ssd_out_sb[:, :, :], ssd_out).then_inc(loaded["ssd_out"], 16)
                sp.wait_ge(zeros_ready, 1)
                sp.dma_start(slots_x.rearrange("(t p) n -> p t n", p=P),
                             zeros[:, :].unsqueeze(1).broadcast_to([P, NR, D])).then_inc(slots_cleared, 16)
                sp.dma_start(router_sb[:, :, :], router).then_inc(expert_loads, 16)
                sp.dma_start(gate_up_sb[:, LATE:, :, :], gate_up[:, LATE:, :, :]).then_inc(expert_loads, 16)

            ssd_stage(nc, x, dict(consts={**C, **views(for_ssd_sb, FOR_SSD)}, ssd_in=ssd_in_sb, ssd_out=ssd_out_sb, loaded=loaded,
                                  zeros=zeros[:, :], zeros_ready=zeros_ready,
                                  spare=gate_up_sb[:, 0:LATE, :, :].rearrange("p e k n -> p e (k n)")), "ssd_", load_first)
            with nc.Block() as block:
                @block.sync
                def _(sp):
                    sp.wait_ge(slots_cleared, 16)
                    sp.wait_ge(expert_loads, 32)

        down_sb = sb(ctx, "down_sb", [P, E + 1, KF, D])
        qkv_sb = sb(ctx, "qkv_sb", [P, KD, QKV])
        wo_sb = sb(ctx, "wo_sb", [P, KD, D])
        for_att_sb = sb(ctx, "for_att_sb", [P, width_of(FOR_ATT)])
        att = views(for_att_sb, FOR_ATT)
        for name in ("cos", "sin"):
            att[name] = att[name].rearrange("p (t n) -> p t n", t=TS)
        W["down"] = down_sb

        def load_behind(sp):
            sp.dma_start(down_sb[:, E, :, :], down[:, E, :, :]).then_inc(late_loads[0], 16)
            sp.dma_start(gate_up_sb[:, 0:LATE, :, :], gate_up[:, 0:LATE, :, :]).then_inc(late_loads[1], 16)
            sp.dma_start(down_sb[:, 0:E, :, :], down[:, 0:E, :, :]).then_inc(late_loads[1], 16)
            sp.dma_start(qkv_sb[:, :, :], qkv).then_inc(att_loads, 16)
            sp.dma_start(wo_sb[:, :, :], wo).then_inc(att_loads, 16)
            sp.dma_start(for_att_sb[:, :], for_att).then_inc(att_loads, 16)

        W["late_loads"] = late_loads
        ffn_stage(nc, x, W, "ffn1_", load_behind)
        with nc.Block() as block:
            @block.sync
            def _(sp):
                sp.wait_ge(att_loads, 48)
        attention_stage(nc, x, dict(consts={**C, **att}, qkv=qkv_sb, wo=wo_sb), "att_")
        ffn_stage(nc, x, W, "ffn2_", None)
        with nc.Block() as block:
            @block.sync
            def _(sp):
                sp.dma_start(out, x[:, :, :]).then_inc(stored, 16)
                sp.wait_ge(stored, 16)


def kernel(**inputs):
    import numpy as np
    import concourse.bacc as bacc
    from concourse.bass_utils import run_bass_kernel_spmd

    def given(name):
        return np.asarray(inputs["L0_" + name])

    def chunks(w, rows):
        return w.reshape(rows, P, -1).transpose(1, 0, 2)

    k = np.arange(P)
    same = k[:, None] // Q == k[None, :] // Q
    tables = {
        "ident": np.eye(P), "ones": np.ones((P, P)), "below": k[:, None] < k[None, :],
        "minus_half": np.full((P, NT), -0.5),
        "weigh": np.tile(float(E) - np.arange(E), (P, NT)),
        "steps": np.tile(float(P) * np.arange(NT), (P, E)),
        "upto": np.tile((np.arange(E)[None, :] <= np.arange(E)[:, None]).reshape(-1), (P, 1)),
        "tile_no": np.tile(np.repeat(np.arange(float(NR)), E), (P, 1)),
        "tri": k[:, None] % Q <= np.arange(Q)[None, :],
        "behind": same & (k[:, None] > k[None, :]), "upto_t": same & (k[:, None] <= k[None, :]),
        "rows_of": np.concatenate([np.tile((k[:, None] // Q == q), (1, P)) for q in range(CPT)], 1),
        "hide": np.where(k[None, :] > k[:, None], -1e30, 0.0),
    }
    theta = (1.0 / np.float32(10000.0) ** (np.arange(0, HD, 2, dtype=np.float32) / HD)).astype(np.float32)
    angle = np.arange(L, dtype=np.float32)[:, None] * theta[None, :]
    scale = np.array([HD ** -0.5] * H + [1.0] * HKV)
    for name, pair in (("cos", (np.cos(angle), np.cos(angle))), ("sin", (-np.sin(angle), np.sin(angle)))):
        table = np.stack(pair, -1).reshape(L, 1, HD) * scale[None, :, None]
        tables[name] = chunks(table.reshape(L, QK), TS).reshape(P, -1)
    tables.update({
        "A_log": np.tile(given("attn_a_A_log"), (P, 1)), "D": np.tile(given("attn_a_D"), (P, 1)),
        "dt_bias": np.tile(given("attn_a_dt_bias"), P // HEADS)[:, None],
        "conv_w": given("attn_a_conv_w").reshape(NB, P, TAPS).transpose(1, 0, 2).reshape(P, -1),
        "conv_b": given("attn_a_conv_b").reshape(NB, P).T, "norm_w": given("attn_a_norm_w").reshape(CB_, P).T,
    })

    def packed(fields):
        return np.concatenate([np.asarray(tables[name], np.float32) for name, _ in fields], 1)

    wq = given("attn_b_wq").reshape(G, HALF, REP, HD, D).transpose(0, 2, 1, 3, 4).reshape(H * HD, D)
    shared_up = np.concatenate([given("ffn_shared_gate_w"), given("ffn_shared_up_w")], 1)[None]
    gate_up = np.concatenate([given("ffn_gate_up_proj"), shared_up])
    down = np.concatenate([given("ffn_down_proj"), given("ffn_shared_down_w")[None]])
    arrays = {
        "hidden": chunks(given("attn_a_hidden_states").reshape(TOK, D), NT),
        "ssd_in": chunks(given("attn_a_in_proj_w").T, KD), "ssd_out": chunks(given("attn_a_out_proj_w").T, CB_),
        "qkv": chunks(np.concatenate([wq, given("attn_b_wk"), given("attn_b_wv")]).T, KD), "wo": chunks(given("attn_b_wo").T, KD),
        "gate_up": gate_up.reshape(E + 1, KD, P, 2 * FI).transpose(2, 0, 1, 3),
        "down": down.reshape(E + 1, KF, P, D).transpose(2, 0, 1, 3),
        "router": chunks(given("ffn_router_w").T, KD),
        "common": packed(COMMON), "for_ssd": packed(FOR_SSD), "for_att": packed(FOR_ATT),
    }
    nc = bacc.Bacc("TRN2", target_bir_lowering=False, num_devices=1)
    feed, args = {}, []
    for name, a in arrays.items():
        feed[name] = np.ascontiguousarray(a)
        args.append(nc.dram_tensor(name, feed[name].shape, mybir.dt.from_np(feed[name].dtype), kind="ExternalInput").ap())
    args.append(nc.dram_tensor("out", (P, NT, D), F32, kind="ExternalOutput").ap())
    hybrid_layer(nc, *args)
    r = run_bass_kernel_spmd(nc, [feed], core_ids=[0])
    return r.results[0]["out"].transpose(1, 0, 2).reshape(B, L, D)
```

```python
from contextlib import ExitStack

import concourse.bass as bass
from concourse import mybir
from concourse.alu_op_type import AluOpType as ALU

F32 = mybir.dt.float32
BF16 = mybir.dt.bfloat16
I32 = mybir.dt.int32
U32 = mybir.dt.uint32
ACT = mybir.ActivationFunctionType
AX = mybir.AxisListType

P = 128
B, L, D = 4, 256, 256
TOK = B * L
NT = TOK // P
KD = D // P
EPS = 1e-5
E, FI = 8, 512
KF = FI // P
SHARED = E
NR = NT + E - 1
NJ = NT + NR


class Steps:

    def __init__(self):
        self.n = 0

    def step(self):
        self.n += 1
        return 1


def ffn_stage(nc, x, W, tag, load_behind=None, out=None):
    with ExitStack() as ctx:
        def sb(name, shape, dt=F32):
            return ctx.enter_context(nc.sbuf_tensor(tag + name, shape, dt))

        def ps(name, shape, dt=F32):
            return ctx.enter_context(nc.psum_tensor(tag + name, shape, dt))

        def sem(name):
            return ctx.enter_context(nc.semaphore(tag + name))

        C = W["consts"]
        meanvar = W["meanvar"]
        rstd = sb("rstd", [P, NT])
        vareps = sb("vareps", [P, NT])
        xn = sb("xn", [P, NT, D])
        xscaled = sb("xscaled", [P, NT, D])
        xnT = sb("xnT", [P, KD, TOK])
        logitT = sb("logitT", [E, TOK])
        logit = sb("logit", [P, NT, E])
        top = sb("top", [P, NT])
        score = sb("score", [P, NT])
        tmp = sb("tmp", [P, E * E])
        first = sb("first", [P, NT])
        onehot = sb("onehot", [P, NT, E])
        before = sb("before", [P, NT + 1, E])
        counts = sb("counts", [P, NT, E])
        tiles_of = sb("tiles_of", [P, E])
        tile_end = sb("tile_end", [P, E])
        base = sb("base", [P, E])
        rank = sb("rank", [P, NT, E])
        slotf = sb("slotf", [P, NT])
        slot = sb("slot", [P, NT], U32)
        expf = sb("expf", [1, NR])
        expert = sb("expert", [1, NR], I32)
        cmp = sb("cmp", [1, NR, E])
        xg = [sb(f"xg{i}", [P, D]) for i in range(2)]
        xgT = [sb(f"xgT{i}", [P, KD, P]) for i in range(2)]
        sg = [sb(f"sg{i}", [P, FI]) for i in range(2)]
        h = [sb(f"h{i}", [P, FI]) for i in range(2)]
        hT = [sb(f"hT{i}", [P, KF, P]) for i in range(2)]
        yout = [sb(f"yout{i}", [P, D]) for i in range(2)]
        yback = sb("yback", [P, NT, D])

        gu = [ps(f"gu{i}", [P, 2 * FI]) for i in range(2)]
        pt = ps("pt", [P, KF * P])
        pd = [ps(f"pd{i}", [P, 512]) for i in range(2)]
        px = ps("px", [P, 512])

        dve_done = sem("dve_done")
        var_ready = sem("var_ready")
        rstd_ready = sem("rstd_ready")
        xn_ready = sem("xn_ready")
        xnT_in_psum = sem("xnT_in_psum")
        xnT_ready = sem("xnT_ready")
        logitT_in_psum = sem("logitT_in_psum")
        logitT_ready = sem("logitT_ready")
        logit_in_psum = sem("logit_in_psum")
        top_ready = sem("top_ready")
        score_ready = sem("score_ready")
        onehot_ready = sem("onehot_ready")
        ranks_in_psum = sem("ranks_in_psum")
        ranks_taken = sem("ranks_taken")
        route_ready = sem("route_ready")
        scattered = sem("scattered")
        gathered = [sem(f"gathered{t}") for t in range(NT)]
        xg_loaded = [sem(f"xg_loaded{i}") for i in range(2)]
        xgT_in_psum = sem("xgT_in_psum")
        xgT_ready = sem("xgT_ready")
        gu_ready = sem("gu_ready")
        silu_ready = sem("silu_ready")
        h_ready = sem("h_ready")
        hT_in_psum = sem("hT_in_psum")
        hT_ready = sem("hT_ready")
        y_in_psum = sem("y_in_psum")
        y_taken = sem("y_taken")
        x_ready = sem("x_ready")
        stored = sem("stored")
        y_stored = [sem(f"y_stored{i}") for i in range(2)]

        slots_x = W["slots_x"]
        slots_y = W["slots_y"]
        block = ctx.enter_context(nc.Block())

        LOOP = range(NT + 4, NJ - 1)
        ORDER = ([("shared", t) for t in range(5)] + [("routed", r) for r in range(NR)]
                 + [("shared", t) for t in range(5, NT)])
        STEP_OF = {tile: j for j, tile in enumerate(ORDER)}
        LOOP = range(10, 18)

        def routed(s):
            return ORDER[s][1] if 0 <= s < NJ and ORDER[s][0] == "routed" else None

        def steps(eng, step, first=0):
            for j in range(first, LOOP.start):
                step(j, j)
            with eng.Fori(0, len(LOOP) // 2) as i:
                for u in range(2):
                    step(2 * i + (LOOP.start + u), LOOP.start + u)
            for j in range(LOOP.stop, NJ + 2):
                step(j, j)

        @block.sync
        def _(sp):
            def load(r):
                sp.dma_start(xg[r % 2][:, :], slots_x[r * P:(r + 1) * P, :]).then_inc(xg_loaded[r % 2], 16)

            if load_behind:
                load_behind(sp)
            sp.wait_ge(scattered, 16 * NT)
            for r in range(2):
                load(r)
            for r in range(NR + 3):
                if r + 2 < NR:
                    sp.wait_ge(xgT_in_psum, r + 1)
                    load(r + 2)
                if r >= 3:
                    q = r - 3
                    sp.wait_ge(y_taken, STEP_OF["routed", q] + 1)
                    sp.dma_start(slots_y[q * P:(q + 1) * P, :], yout[q % 2][:, :]).then_inc(y_stored[q % 2], 16)
            if out is not None:
                for t in range(NT):
                    sp.wait_ge(x_ready, t + 1)
                    sp.dma_start(out[:, t, :], x[:, t, :]).then_inc(stored, 16)
                sp.wait_ge(stored, 16 * NT)

        @block.gpsimd
        def _(pool):
            pool.wait_ge(var_ready, 1)
            pool.tensor_tensor(rstd[:, :], vareps[:, :], C["minus_half"], ALU.pow).then_inc(rstd_ready, 1)
            for t in range(NT):
                pool.wait_ge(route_ready, 2 + t)
                pool.indirect_dma_start(out=slots_x, out_offset=bass.IndirectOffsetOnAxis(ap=slot[:, t:t + 1], axis=0),
                                        in_=xscaled[:, t, :], in_offset=None).then_inc(scattered, 16)
            pool.wait_ge(y_stored[0], 16 * ((NR + 1) // 2))
            pool.wait_ge(y_stored[1], 16 * (NR // 2))
            for t in range(NT):
                pool.indirect_dma_start(out=yback[:, t, :], out_offset=None, in_=slots_y,
                                        in_offset=bass.IndirectOffsetOnAxis(ap=slot[:, t:t + 1], axis=0)).then_inc(gathered[t], 16)

        @block.vector
        def _(dve):
            own = Steps()
            dve.tensor_scalar(vareps[:, :], meanvar[:, :, 1], EPS, None, ALU.add).then_inc(var_ready, 1)
            dve.wait_ge(rstd_ready, 1)
            for t in range(NT):
                dve.tensor_scalar(xn[:, t, :], x[:, t, :], meanvar[:, t, 0:1], rstd[:, t:t + 1],
                                  ALU.subtract, ALU.mult).then_inc(xn_ready, 1)
            def step(j, s):
                u = s % 2
                r1 = routed(s + 1)
                if r1 is not None:
                    dve.wait_ge(xgT_in_psum, j + (r1 + 1 - s))
                    dve.wait_ge(gu_ready, j)
                    dve.tensor_copy(xgT[r1 % 2][:, :, :], px[:, 0:D].rearrange("p (k n) -> p k n", k=KD)).then_inc(xgT_ready, 1)
                if s < NJ:
                    dve.wait_ge(silu_ready, j + 1)
                    if s >= 2:
                        dve.wait_ge(hT_in_psum, j - 1)
                    dve.tensor_tensor(h[u][:, :], sg[u][:, :], gu[u][:, FI:], ALU.mult).then_inc(h_ready, 1)
                if s >= 2:
                    dve.wait_ge(y_in_psum, j - 1)
                    r = routed(s - 2)
                    if r is None:
                        t = ORDER[s - 2][1]
                        dve.tensor_tensor(x[:, t, :], x[:, t, :], pd[u][:, 0:D], ALU.add).then_inc(y_taken, 1)
                    else:
                        if r >= 2:
                            dve.wait_ge(y_stored[r % 2], 8 * (j + (r - s - r % 2)))
                        dve.tensor_copy(yout[r % 2][:, :], pd[u][:, 0:D]).then_inc(y_taken, 1)

            dve.wait_ge(logitT_in_psum, 1)
            dve.tensor_copy(logitT[:, :], gu[1][0:E, :]).then_inc(logitT_ready, 1)
            dve.wait_ge(logit_in_psum, 1)
            dve.tensor_copy(logit[:, :, :], px[:, 0:NT * E].rearrange("p (t e) -> p t e", e=E)).then_inc(dve_done, own.step())
            dve.wait_ge(dve_done, own.n)
            dve.tensor_reduce(top[:, :], logit[:, :, :], AX.X, ALU.max).then_inc(top_ready, 1)
            dve.wait_ge(top_ready, 1)
            t3 = tmp[:, :].rearrange("p (t e) -> p t e", e=E)
            dve.tensor_tensor(onehot[:, :, :], logit[:, :, :], top[:, :].unsqueeze(2).broadcast_to([P, NT, E]), ALU.is_ge).then_inc(dve_done, own.step())
            dve.wait_ge(dve_done, own.n)
            dve.tensor_tensor(t3, onehot[:, :, :], C["weigh"], ALU.mult).then_inc(dve_done, own.step())
            dve.wait_ge(dve_done, own.n)
            dve.tensor_reduce(first[:, :], t3, AX.X, ALU.max).then_inc(dve_done, own.step())
            dve.wait_ge(dve_done, own.n)
            dve.tensor_tensor(onehot[:, :, :], t3, first[:, :].unsqueeze(2).broadcast_to([P, NT, E]), ALU.is_equal).then_inc(onehot_ready, 1)
            step(0, 0)
            dve.wait_ge(onehot_ready, 1)
            dve.wait_ge(ranks_in_psum, 1)
            pr = pd[0]
            dve.tensor_copy(rank[:, :, :], pr[:, 0:NT * E].rearrange("p (t e) -> p t e", e=E)).then_inc(dve_done, own.step())
            dve.tensor_copy(counts[:, :, :], pr[:, NT * E:2 * NT * E].rearrange("p (t e) -> p t e", e=E)).then_inc(ranks_taken, 1)
            dve.memset(before[:, 0, :], 0.0).then_inc(dve_done, own.step())
            dve.wait_ge(ranks_taken, 1)
            for t in range(NT):
                dve.wait_ge(dve_done, own.n)
                dve.tensor_tensor(before[:, t + 1, :], before[:, t, :], counts[:, t, :], ALU.add).then_inc(dve_done, own.step())
            dve.wait_ge(dve_done, own.n)
            step(1, 1)
            dve.tensor_tensor(t3, before[:, NT, :].unsqueeze(2).broadcast_to([P, E, NT]), C["steps"], ALU.is_gt).then_inc(dve_done, own.step())
            dve.wait_ge(dve_done, own.n)
            dve.tensor_reduce(tiles_of[:, :], t3, AX.X, ALU.add).then_inc(dve_done, own.step())
            dve.wait_ge(dve_done, own.n)
            dve.tensor_tensor(t3, tiles_of[:, :].unsqueeze(1).broadcast_to([P, E, E]), C["upto"], ALU.mult).then_inc(dve_done, own.step())
            dve.wait_ge(dve_done, own.n)
            dve.tensor_reduce(tile_end[:, :], t3, AX.X, ALU.add).then_inc(dve_done, own.step())
            dve.wait_ge(dve_done, own.n)
            dve.tensor_tensor(base[:, :], tile_end[:, :], tiles_of[:, :], ALU.subtract).then_inc(dve_done, own.step())
            dve.tensor_tensor(rank[:, :, :], rank[:, :, :], before[:, 0:NT, :], ALU.add).then_inc(dve_done, own.step())
            dve.tensor_tensor(cmp[:, :, :], tile_end[0:1, :].unsqueeze(1).broadcast_to([1, NR, E]), C["tile_no"], ALU.is_le).then_inc(dve_done, own.step())
            dve.wait_ge(dve_done, own.n)
            dve.scalar_tensor_tensor(t3, base[:, :].unsqueeze(1).broadcast_to([P, NT, E]), float(P), rank[:, :, :], ALU.mult, ALU.add).then_inc(dve_done, own.step())
            dve.tensor_reduce(expf[:, :], cmp[:, :, :], AX.X, ALU.add).then_inc(dve_done, own.step())
            dve.wait_ge(dve_done, own.n)
            dve.tensor_tensor(rank[:, :, :], t3, onehot[:, :, :], ALU.mult).then_inc(dve_done, own.step())
            dve.tensor_copy(expert[:, :], expf[:, :]).then_inc(dve_done, own.step())
            dve.wait_ge(dve_done, own.n)
            dve.tensor_reduce(slotf[:, :], rank[:, :, :], AX.X, ALU.add).then_inc(dve_done, own.step())
            dve.wait_ge(dve_done, own.n)
            dve.tensor_copy(slot[:, :], slotf[:, :]).then_inc(route_ready, 1)
            dve.wait_ge(score_ready, 1)
            for t in range(NT):
                dve.tensor_scalar(xscaled[:, t, :], xn[:, t, :], score[:, t:t + 1], None, ALU.mult).then_inc(route_ready, 1)

            steps(dve, step, 2)
            dve.wait_ge(y_taken, NJ)
            for t in range(NT):
                dve.wait_ge(gathered[t], 16)
                dve.tensor_tensor(x[:, t, :], x[:, t, :], yback[:, t, :], ALU.add).then_inc(x_ready, 1)
                if out is None:
                    dve.wait_ge(x_ready, t + 1)
                    dve.bn_stats(W["stats"][:, t, :], x[:, t, :]).then_inc(dve_done, own.step())
                    dve.wait_ge(dve_done, own.n)
                    dve.bn_aggr(meanvar[:, t, :], W["stats"][:, t, :]).then_inc(dve_done, own.step())

        @block.scalar
        def _(act):
            for g in range(NT // 2):
                act.wait_ge(xnT_in_psum, g + 1)
                act.activation(xnT[:, :, 2 * g * P:2 * (g + 1) * P], gu[0][:, (g % 2) * 512:(g % 2) * 512 + 512].rearrange("p (k n) -> p k n", k=KD),
                               ACT.Copy).then_inc(xnT_ready, 1)
            act.wait_ge(top_ready, 1)
            act.activation(score[:, :], top[:, :], ACT.Sigmoid).then_inc(score_ready, 1)

            def step(j, s):
                u = s % 2
                if s < NJ:
                    act.wait_ge(gu_ready, j + 1)
                    if s >= 2:
                        act.wait_ge(h_ready, j - 1)
                    act.activation(sg[u][:, :], gu[u][:, 0:FI], ACT.Silu).then_inc(silu_ready, 1)
                if 1 <= s <= NJ:
                    act.wait_ge(hT_in_psum, j)
                    if s >= 3:
                        act.wait_ge(y_in_psum, j - 2)
                    act.activation(hT[(u + 1) % 2][:, :, :], pt[:, :].rearrange("p (k n) -> p k n", k=KF), ACT.Copy).then_inc(hT_ready, 1)

            steps(act, step)

        @block.tensor
        def _(pe):
            ident = C["ident"]
            for t in range(NT):
                g, r = t // 2, t % 2
                if r == 0 and g >= 2:
                    pe.wait_ge(xnT_ready, g - 1)
                pe.wait_ge(xn_ready, t + 1)
                for k in range(KD):
                    mm = pe.transpose(gu[0][:, (g % 2) * 512 + k * 256 + r * P:(g % 2) * 512 + k * 256 + (r + 1) * P], xn[:, t, k * P:(k + 1) * P], ident)
                if r == 1:
                    mm.then_inc(xnT_in_psum, 1)
            for half in range(2):
                pe.wait_ge(xnT_ready, 2 * (half + 1))
                for k in range(KD):
                    mm = pe.matmul(gu[1][0:E, half * 512:(half + 1) * 512], W["router"][:, k, :], xnT[:, k, half * 512:(half + 1) * 512],
                                   start=(k == 0), stop=(k == KD - 1))
            mm.then_inc(logitT_in_psum, 1)

            def logits_to_tokens():
                pe.wait_ge(logitT_ready, 1)
                for t in range(NT):
                    mm = pe.transpose(px[:, t * E:(t + 1) * E], logitT[:, t * P:(t + 1) * P], ident[0:E, 0:E])
                mm.then_inc(logit_in_psum, 1)

            def ranks():
                pe.wait_ge(onehot_ready, 1)
                oh = onehot[:, :, :].rearrange("p t e -> p (t e)")
                pe.matmul(pd[0][:, 0:NT * E], C["below"], oh, start=True, stop=True)
                pe.matmul(pd[0][:, NT * E:2 * NT * E], C["ones"], oh, start=True, stop=True).then_inc(ranks_in_psum, 1)

            def gate_up(u, lhsT, e):
                for half in range(2):
                    cols = slice(half * FI, (half + 1) * FI)
                    for k in range(KD):
                        rhs = W["gate_up"][:, bass.ds(e, 1), k, cols].rearrange("p a n -> p (a n)")
                        mm = pe.matmul(gu[u][:, cols], lhsT(k), rhs, start=(k == 0), stop=(k == KD - 1))
                mm.then_inc(gu_ready, 1)

            def down(u, e):
                for k in range(KF):
                    rhs = W["down"][:, bass.ds(e, 1), k, :].rearrange("p a n -> p (a n)")
                    mm = pe.matmul(pd[u][:, 0:D], hT[u][:, k, :], rhs, start=(k == 0), stop=(k == KF - 1))
                mm.then_inc(y_in_psum, 1)

            def with_expert(r, may_be_unused, work, bank, done):
                e = pe.value_load(expert[0:1, bass.ds(r, 1)], min_val=0, max_val=E)
                if not may_be_unused:
                    work(e)
                    return
                with pe.If(e < E):
                    work(e)
                with pe.If(e > E - 1):
                    pe.matmul(bank[:, 0:E], ident, ident[:, 0:E], start=True, stop=True).then_inc(done, 1)

            def step(j, s):
                u = s % 2
                if s < NJ:
                    r = routed(s)
                    if s >= 2:
                        pe.wait_ge(h_ready, j - 1)
                    if r is None:
                        t = ORDER[s][1]
                        gate_up(u, lambda k: xnT[:, k, t * P:(t + 1) * P], SHARED)
                    else:
                        pe.wait_ge(xgT_ready, j + (r + 1 - s))
                        if r == 0:
                            pe.wait_ge(W["late_loads"][1], 32)
                        may_be_unused = r >= NT or s in LOOP and routed(LOOP.stop - 1) >= NT
                        with_expert(j + (r - s), may_be_unused, lambda e: gate_up(u, lambda k: xgT[r % 2][:, k, :], e), gu[u], gu_ready)
                r1 = routed(s + 1)
                if r1 is not None:
                    pe.wait_ge(xg_loaded[r1 % 2], 8 * (j + (r1 + 2 - s - r1 % 2)))
                    if r1 >= 1:
                        pe.wait_ge(xgT_ready, j + (r1 - s))
                    for k in range(KD):
                        mm = pe.transpose(px[:, k * P:(k + 1) * P], xg[r1 % 2][:, k * P:(k + 1) * P], ident)
                    mm.then_inc(xgT_in_psum, 1)
                if s == 0:
                    logits_to_tokens()
                if s == 1:
                    ranks()
                if s >= 2:
                    r = routed(s - 2)
                    pe.wait_ge(hT_ready, j - 1)
                    if s == 2:
                        pe.wait_ge(W["late_loads"][0], 16)
                        pe.wait_ge(ranks_taken, 1)
                    if s >= 4:
                        pe.wait_ge(y_taken, j - 3)
                    if r is None:
                        down(u, SHARED)
                    else:
                        may_be_unused = r >= NT or s in LOOP and routed(LOOP.stop - 3) >= NT
                        with_expert(j + (r - s), may_be_unused, lambda e: down(u, e), pd[u], y_in_psum)
                if 1 <= s <= NJ:
                    pe.wait_ge(h_ready, j)
                    for k in range(KF):
                        mm = pe.transpose(pt[:, k * P:(k + 1) * P], h[(u + 1) % 2][:, k * P:(k + 1) * P], ident)
                    mm.then_inc(hT_in_psum, 1)

            steps(pe, step)



H, HKV, HD = 32, 8, 8
G, HALF, REP = HKV // 2, 2, H // HKV
TS = L // P
ROWS = 64
TYPES = 6
QKV = (H + 2 * HKV) * HD
QK = (H + HKV) * HD


def attention_stage(nc, x, W, tag):
    with ExitStack() as ctx:
        def sb(name, shape, dt=F32):
            return ctx.enter_context(nc.sbuf_tensor(tag + name, shape, dt))

        def ps(name, shape, dt=F32):
            return ctx.enter_context(nc.psum_tensor(tag + name, shape, dt))

        def sem(name):
            return ctx.enter_context(nc.semaphore(tag + name))

        C = W["consts"]
        SB, FB, LAG = 3, 3, 2
        meanvar = W["meanvar"]
        rstd = sb("rstd", [P, TS])
        vareps = sb("vareps", [P, TS])
        xn = sb("xn", [P, TS, D])
        xnT = sb("xnT", [P, KD, L])
        ropeA = sb("ropeA", [P, QK])
        ropeB = sb("ropeB", [P, QK])
        parts = sb("parts", [P, 3, QK], BF16)
        qs = sb("qs", [P, TS, H, ROWS], BF16)
        ks = sb("ks", [P, TS, HKV, ROWS], BF16)
        qTa = sb("qTa", [P, G * REP, L], BF16)
        qTb = [sb(f"qTb{i}", [P, G, REP, L], BF16) for i in range(2)]
        kz = [sb(f"kz{i}", [P, G, HALF, L], BF16) for i in range(2)]
        V = [sb(f"V{i}", [P, TS, HKV, 32]) for i in range(3)]
        top = sb("top", [P, TS, H])
        rest = sb("rest", [P, H])
        probs = [sb(f"probs{i}", [P, REP * P]) for i in range(SB)]
        oT = sb("oT", [P, REP, P])
        recip = sb("recip", [P, REP, 4])
        y = sb("y", [P, TS, HKV, REP, HD])
        yT = sb("yT", [P, KD, P])
        identb = sb("identb", [P, P], BF16)
        hide = sb("hide", [P, HALF, P], BF16)

        sT = [ps(f"sT{i}", [P, REP * P]) for i in range(SB)]
        po = ps("po", [P, 512])
        pf = [ps(f"pf{i}", [P, 512]) for i in range(FB)]
        ot = ps("ot", [P, 512])

        dve_done = sem("dve_done")
        blank = sem("blank")
        var_ready = sem("var_ready")
        rstd_ready = sem("rstd_ready")
        xn_ready = sem("xn_ready")
        front_in_psum = sem("front_in_psum")
        taken = {"act": sem("taken_by_act"), "dve": sem("taken_by_dve")}
        parts_ready = sem("parts_ready")
        q1_copied = sem("q1_copied")
        tables_ready = sem("tables_ready")
        kz_half = sem("kz_half")
        rows_ready = sem("rows_ready")
        max_rows_ready = [sem(f"max_rows_ready{t}") for t in range(TS)]
        scores_ready = sem("scores_ready")
        probs_ready = sem("probs_ready")
        pv_done = sem("pv_done")
        oT_in_psum = sem("oT_in_psum")
        oT_ready = sem("oT_ready")
        o_in_psum = sem("o_in_psum")
        y_ready = sem("y_ready")
        yT_in_psum = sem("yT_in_psum")
        yT_ready = sem("yT_ready")
        wo_in_psum = sem("wo_in_psum")
        x_ready = sem("x_ready")

        BLOCKS = [(tt, kv, sbk) for tt in range(TS) for kv in range(HKV) for sbk in range(tt + 1)]
        NU = len(BLOCKS)
        ENDS = {b * NU + last + LAG: (HKV // 4) * TS * b + q for b in range(B)
                for q, last in enumerate(n for n, (tt, kv, sbk) in enumerate(BLOCKS) if kv % 4 == 3 and sbk == tt)}
        SLOTS = range(-1, B * NU + LAG + 4)

        SEQ = []

        def pieces(kind, b, t, who, slots_of_parts):
            SEQ.extend((kind, b, t, m, who, g) for m, g in enumerate(slots_of_parts))

        for nb in range(B):
            def at(*slots, first=None, second=None, third=None):
                if nb == 0:
                    return first or [-1] * len(slots)
                own = {1: second, 2: third}.get(nb) or slots
                return [(nb - 1) * NU + g for g in own]

            def rate(first, count, each):
                return [first + m // each for m in range(count)]

            pieces("xnT", nb, 0, "act", at(-2, second=[6]))
            pieces("xnT", nb, 1, "act", at(-2, second=[6]))
            pieces("qkv", nb, 0, "dve", at(-1, second=[8]))
            pieces("qkv", nb, 1, "dve", at(1, second=[10], third=[4]))
            pieces("kT", nb, 0, "act", at(2, second=[11]))
            pieces("qTa", nb, 0, "act", at(3, 3, second=[11, 12]))
            pieces("kT", nb, 1, "act", at(4, second=[13], third=[6]))
            pieces("qTa", nb, 1, "act", at(5, 5, second=[13, 14], third=[6, 7]))
            pieces("max0", nb, 0, "dve", at(5, 6, 6, 7, 7, 8, 8, 9, second=rate(14, 8, 2)))
            pieces("qTb", nb, 0, "act", at(11, 12, second=[20, 20]))
            pieces("max1", nb, 1, "dve", at(9, 10, 10, 11, 12, 12, 13, 14, 14, 15, 16, 16, 17, 18, 18, 19,
                                            first=rate(0, 16, 2), second=rate(18, 16, 2)))
            pieces("qTb", nb, 1, "act", at(21, 21, first=[7, 7], second=[27, 27]))
        SEQ.sort(key=lambda f: f[5])
        GO = {g: [n for n, f in enumerate(SEQ) if f[5] == g] for g in SLOTS}
        NORM_AT = {-1: [1], **{(b - 1) * NU - 3: [b] for b in range(2, B)}}

        LATE_STATS = {(B - 1) * NU + 13 + t: t for t in range(NT - TS)}
        LATE_STATS.update({max(e for e, q in ENDS.items() if q == 2 * t + 1) + 3: t for t in range(NT - TS, NT)})

        def take_no(n):
            who = SEQ[n][4]
            return taken[who], sum(f[4] == who for f in SEQ[:n + 1])

        def place(*piece):
            return next(n for n, f in enumerate(SEQ) if f[:4] == piece)

        block = ctx.enter_context(nc.Block())

        @block.gpsimd
        def _(pool):
            for b in range(B):
                pool.wait_ge(var_ready, b + 1)
                pool.tensor_tensor(rstd[:, :], vareps[:, :], C["minus_half"][:, 0:TS], ALU.pow).then_inc(rstd_ready, 1)
                if b == 0:
                    for i in range(3):
                        if i < 2:
                            pool.memset(kz[i][:, :, :, :], 0.0).then_inc(blank, 1)
                        pool.memset(V[i][:, :, :, HD + 1:], 0.0).then_inc(blank, 1)

        @block.vector
        def _(dve):
            own = Steps()

            def normalise(b):
                dve.tensor_scalar(vareps[:, :], meanvar[:, TS * b:TS * (b + 1), 1], EPS, None, ALU.add).then_inc(var_ready, 1)
                dve.wait_ge(rstd_ready, b + 1)
                if b >= 1:
                    dve.wait_ge(front_in_psum, place("xnT", b - 1, 1, 0) + 1)
                for q in range(TS):
                    dve.tensor_scalar(xn[:, q, :], x[:, TS * b + q, :], meanvar[:, TS * b + q, 0:1], rstd[:, q:q + 1],
                                      ALU.subtract, ALU.mult).then_inc(xn_ready, 1)

            normalise(0)
            dve.tensor_copy(identb[:, :], C["ident"]).then_inc(tables_ready, 1)
            dve.tensor_copy(hide[:, :, :], C["hide"].unsqueeze(1).broadcast_to([P, HALF, P])).then_inc(tables_ready, 1)
            dve.memset(qs[:, :, :, TYPES * HD:], 0.0).then_inc(tables_ready, 1)
            dve.memset(ks[:, :, :, TYPES * HD + 3:], 0.0).then_inc(tables_ready, 1)
            dve.memset(ks[:, :, :, TYPES * HD:TYPES * HD + 3], 1.0).then_inc(tables_ready, 1)
            for i in range(3):
                dve.memset(V[i][:, :, :, HD:HD + 1], 1.0).then_inc(tables_ready, 1)
            dve.wait_ge(tables_ready, 8)

            def front(n):
                kind, b, t, m, who, _ = SEQ[n]
                if who != "dve":
                    return
                src = pf[n % FB]
                dve.wait_ge(front_in_psum, n + 1)
                tk, no = take_no(n)
                if kind == "qkv":
                    cosT, sinT = C["cos"][:, t, :], C["sin"][:, t, :]
                    qk = src[:, 0:QK].rearrange("p (h j) -> p h j", j=2)
                    sn = sinT.rearrange("p (h j) -> p h j", j=2)
                    rb = ropeB[:, :].rearrange("p (h j) -> p h j", j=2)
                    dve.tensor_tensor(ropeA[:, :], src[:, 0:QK], cosT, ALU.mult).then_inc(dve_done, own.step())
                    dve.tensor_tensor(rb[:, :, 0], qk[:, :, 1], sn[:, :, 0], ALU.mult).then_inc(dve_done, own.step())
                    dve.tensor_tensor(rb[:, :, 1], qk[:, :, 0], sn[:, :, 1], ALU.mult).then_inc(dve_done, own.step())
                    if b >= 3:
                        dve.wait_ge(pv_done, (b - 2) * NU)
                    dve.wait_ge(dve_done, own.n)
                    dve.tensor_copy(V[b % 3][:, t, :, 0:HD], src[:, QK:QKV].rearrange("p (h d) -> p h d", d=HD)).then_inc(tk, 1)
                    dve.tensor_tensor(ropeA[:, :], ropeA[:, :], ropeB[:, :], ALU.add).then_inc(dve_done, own.step())
                    dve.wait_ge(dve_done, own.n)
                    if TS * b + t >= 1:
                        dve.wait_ge(q1_copied, TS * b + t)
                    dve.tensor_copy(parts[:, 0, :], ropeA[:, :]).then_inc(dve_done, own.step())
                    dve.wait_ge(dve_done, own.n)
                    dve.tensor_tensor(ropeB[:, :], ropeA[:, :], parts[:, 0, :], ALU.subtract).then_inc(dve_done, own.step())
                    dve.wait_ge(dve_done, own.n)
                    dve.tensor_copy(parts[:, 1, :], ropeB[:, :]).then_inc(dve_done, own.step())
                    dve.wait_ge(dve_done, own.n)
                    dve.tensor_tensor(parts[:, 2, :], ropeB[:, :], parts[:, 1, :], ALU.subtract).then_inc(parts_ready, 1)
                    dve.wait_ge(parts_ready, TS * b + t + 1)
                    q2 = parts[:, 1, 0:H * HD].rearrange("p (h d) -> p h d", d=HD).unsqueeze(2).broadcast_to([P, H, 2, HD])
                    dve.tensor_copy(qs[:, t, :, 3 * HD:5 * HD].rearrange("p h (r d) -> p h r d", d=HD), q2).then_inc(dve_done, own.step())
                    dve.tensor_copy(qs[:, t, :, 5 * HD:6 * HD], parts[:, 2, 0:H * HD].rearrange("p (h d) -> p h d", d=HD)).then_inc(dve_done, own.step())
                    dve.memset(qs[:, t, :, TYPES * HD:TYPES * HD + 3], 0.0).then_inc(dve_done, own.step())
                    kp = parts[:, :, H * HD:QK].rearrange("p r (h d) -> p h r d", d=HD)
                    dve.tensor_copy(ks[:, t, :, 0:3 * HD].rearrange("p h (r d) -> p h r d", d=HD), kp).then_inc(dve_done, own.step())
                    dve.tensor_copy(ks[:, t, :, 3 * HD:5 * HD].rearrange("p h (r d) -> p h r d", d=HD), kp[:, :, 0:2, :]).then_inc(dve_done, own.step())
                    dve.tensor_copy(ks[:, t, :, 5 * HD:6 * HD], kp[:, :, 0, :]).then_inc(rows_ready, 1)
                if kind == "max0":
                    dve.tensor_reduce(top[:, 0, 4 * m:4 * m + 4], src[:, :].rearrange("p (h s) -> p h s", h=4), AX.X, ALU.max).then_inc(tk, 1)
                if kind == "max1":
                    dve.tensor_reduce(top[:, 1, 2 * m:2 * m + 2], src[:, :].rearrange("p (h s) -> p h s", h=2), AX.X, ALU.max).then_inc(tk, 1)
                if (kind == "max0" and m == G * REP // 2 - 1) or (kind == "max1" and m == G * REP - 1):
                    at = TYPES * HD
                    dve.wait_ge(tk, no)
                    dve.tensor_scalar(qs[:, t, :, at], top[:, t, :], -1.0, None, ALU.mult).then_inc(dve_done, own.step())
                    dve.wait_ge(dve_done, own.n)
                    dve.scalar_tensor_tensor(rest[:, :], top[:, t, :], -1.0, qs[:, t, :, at], ALU.mult, ALU.subtract).then_inc(dve_done, own.step())
                    dve.wait_ge(dve_done, own.n)
                    dve.tensor_copy(qs[:, t, :, at + 1], rest[:, :]).then_inc(dve_done, own.step())
                    dve.wait_ge(dve_done, own.n)
                    dve.tensor_tensor(qs[:, t, :, at + 2], rest[:, :], qs[:, t, :, at + 1], ALU.subtract).then_inc(max_rows_ready[t], 1)

            def tail(g):
                if g - 1 in ENDS:
                    q = ENDS[g - 1]
                    t = q // 2
                    pot = ot[:, :].rearrange("p (i k r) -> p i k r", i=REP, k=4)
                    dve.wait_ge(o_in_psum, q + 1)
                    dve.reciprocal(recip[:, :, :], pot[:, :, :, HD]).then_inc(dve_done, own.step())
                    dve.wait_ge(dve_done, own.n)
                    for k in range(4):
                        ins = dve.tensor_tensor(y[:, t % TS, 4 * (q % 2) + k, :, :], pot[:, :, k, 0:HD],
                                                recip[:, :, k].unsqueeze(2).broadcast_to([P, REP, HD]), ALU.mult)
                        if k < 3:
                            ins.then_inc(dve_done, own.step())
                    ins.then_inc(y_ready, 1)
                if ENDS.get(g - 2, 0) % 2:
                    t = ENDS[g - 2] // 2
                    dve.wait_ge(yT_in_psum, t + 1)
                    dve.tensor_copy(yT[:, :, :], ot[:, 0:KD * P].rearrange("p (k n) -> p k n", k=KD)).then_inc(yT_ready, 1)
                if ENDS.get(g - 3, 0) % 2:
                    t = ENDS[g - 3] // 2
                    dve.wait_ge(wo_in_psum, t + 1)
                    dve.tensor_tensor(x[:, t, :], x[:, t, :], ot[:, 0:D], ALU.add).then_inc(x_ready, 1)

            for g in SLOTS:
                for n in GO[g]:
                    front(n)
                for b in NORM_AT.get(g, []):
                    normalise(b)
                tail(g)
                t = LATE_STATS.get(g)
                if t is not None:
                    dve.wait_ge(x_ready, t + 1)
                    dve.bn_stats(W["stats"][:, t, :], x[:, t, :]).then_inc(dve_done, own.step())
                    dve.wait_ge(dve_done, own.n)
                    dve.bn_aggr(W["meanvar"][:, t, :], W["stats"][:, t, :]).then_inc(dve_done, own.step())

        @block.scalar
        def _(act):
            def copy_q1(n):
                kind, b, t = SEQ[n][:3]
                if kind == "qkv":
                    act.wait_ge(parts_ready, TS * b + t + 1)
                    if b >= 1:
                        act.wait_ge(front_in_psum, place("qTb", b - 1, t, 1) + 1)
                    q1 = parts[:, 0, 0:H * HD].rearrange("p (h d) -> p h d", d=HD).unsqueeze(2).broadcast_to([P, H, 3, HD])
                    act.activation(qs[:, t, :, 0:3 * HD].rearrange("p h (r d) -> p h r d", d=HD), q1, ACT.Copy).then_inc(q1_copied, 1)

            def front(n):
                kind, b, t, m, who, _ = SEQ[n]
                if who != "act":
                    return
                src = pf[n % FB]
                act.wait_ge(front_in_psum, n + 1)
                tk = take_no(n)[0]
                if kind in ("kT", "qTb") and b >= 2:
                    act.wait_ge(scores_ready, (b - 1) * NU)
                if kind == "xnT":
                    act.activation(xnT[:, :, t * P:(t + 1) * P], src[:, 0:KD * P].rearrange("p (k n) -> p k n", k=KD), ACT.Copy).then_inc(tk, 1)
                if kind == "kT":
                    act.wait_ge(blank, 1 + 2 * (b % 2))
                    kT = src[:, 0:G * P // 2].bitcast(BF16).rearrange("p (g n) -> p g n", g=G)
                    act.activation(kz[b % 2][0:ROWS, :, 0, t * P:(t + 1) * P], kT[0:ROWS], ACT.Copy).then_inc(kz_half, 1)
                    act.activation(kz[b % 2][ROWS:P, :, 1, t * P:(t + 1) * P], kT[ROWS:P], ACT.Copy).then_inc(tk, 1)
                if kind in ("qTa", "qTb"):
                    dst = qTa if kind == "qTa" else qTb[b % 2][:, :, :, :].rearrange("p g i n -> p (g i) n")
                    act.activation(dst[:, 8 * m:8 * m + 8, t * P:(t + 1) * P], src[:, :].bitcast(BF16).rearrange("p (g n) -> p g n", g=8), ACT.Copy).then_inc(tk, 1)

            for g in SLOTS:
                if 0 <= g < B * NU:
                    act.wait_ge(scores_ready, g + 1)
                    if g >= SB:
                        act.wait_ge(pv_done, g - SB + 1)
                    act.activation(probs[g % SB][:, :], sT[g % SB][:, :], ACT.Exp).then_inc(probs_ready, 1)
                if g >= 1:
                    for n in GO[g - 1]:
                        copy_q1(n)
                for n in GO[g]:
                    if g == -1:
                        copy_q1(n)
                    front(n)
                if g in ENDS:
                    q = ENDS[g]
                    act.wait_ge(pv_done, g - LAG + 1)
                    if q >= 1:
                        act.wait_ge(o_in_psum, q)
                    act.activation(oT[:, :, :], po[:, :].rearrange("p (i t) -> p i t", i=REP), ACT.Copy).then_inc(oT_ready, 1)

        @block.tensor
        def _(pe):
            ident = C["ident"]

            def front(n):
                kind, b, t, m = SEQ[n][:4]
                dst = pf[n % FB]
                if n >= FB:
                    pe.wait_ge(*take_no(n - FB))
                if kind == "xnT":
                    pe.wait_ge(xn_ready, TS * b + t + 1)
                    for k in range(KD):
                        mm = pe.transpose(dst[:, k * P:(k + 1) * P], xn[:, t, k * P:(k + 1) * P], ident)
                if kind == "qkv":
                    pe.wait_ge(*take_no(place("xnT", b, t, 0)))
                    for k in range(KD):
                        mm = pe.matmul(dst[:, 0:QKV], xnT[:, k, t * P:(t + 1) * P], W["qkv"][:, k, :], start=(k == 0), stop=(k == KD - 1))
                if kind == "kT":
                    pe.wait_ge(tables_ready, 8)
                    pe.wait_ge(rows_ready, TS * b + t + 1)
                    out = dst[:, 0:G * P // 2].bitcast(BF16)
                    for g in range(G):
                        mm = pe.transpose(out[:, g * P:(g + 1) * P], ks[:, t, 2 * g:2 * g + 2, :].rearrange("p h r -> p (h r)"), identb[:, :])
                if kind in ("qTa", "qTb"):
                    if kind == "qTa":
                        pe.wait_ge(rows_ready, TS * b + t + 1)
                        pe.wait_ge(q1_copied, TS * b + t + 1)
                    else:
                        pe.wait_ge(max_rows_ready[t], b + 1)
                    out = dst[:, :].bitcast(BF16)
                    for g in range(8):
                        w = 8 * m + g
                        mm = pe.transpose(out[:, g * P:(g + 1) * P], qs[:, t, 2 * w:2 * w + 2, :].rearrange("p h r -> p (h r)"), identb[:, :])
                if kind == "max0":
                    if m == 0:
                        pe.wait_ge(blank, min(2 * b + 2, 5))
                        pe.wait_ge(*take_no(place("qTa", b, 0, 1)))
                    for w in range(2):
                        pair = 2 * m + w
                        out = dst[:, w * 256:(w + 1) * 256]
                        pe.matmul(out, qTa[:, pair, 0:P], kz[b % 2][:, pair // REP, :, 0:P], start=True, stop=False)
                        mm = pe.matmul(out, identb[:, :], hide[:, :, :], start=False, stop=True)
                if kind == "max1":
                    if m == 0:
                        pe.wait_ge(*take_no(place("qTa", b, 1, 1)))
                    pe.matmul(dst[:, :], qTa[:, m, P:2 * P], kz[b % 2][:, m // REP, :, :], start=True, stop=False)
                    mm = pe.matmul(dst[:, :].rearrange("p (h s) -> p h s", h=2)[:, :, P:2 * P], identb[:, :], hide[:, :, :], start=False, stop=True)
                mm.then_inc(front_in_psum, 1)

            def scores(g):
                b = g // NU
                tt, kv, sbk = BLOCKS[g % NU]
                if (kv, sbk) == (0, 0):
                    pe.wait_ge(*take_no(place("qTb", b, tt, 1)))
                if g >= SB:
                    pe.wait_ge(probs_ready, g - SB + 1)
                mm = pe.matmul(sT[g % SB][:, :], kz[b % 2][:, kv // 2, kv % 2, sbk * P:(sbk + 1) * P],
                               qTb[b % 2][:, kv // 2, :, tt * P:(tt + 1) * P], start=True, stop=(sbk < tt))
                if sbk == tt:
                    mm = pe.matmul(sT[g % SB][:, :], hide[:, 0, :], identb[:, :].unsqueeze(1).broadcast_to([P, REP, P]),
                                   start=False, stop=True)
                mm.then_inc(scores_ready, 1)

            def weigh(g):
                b = g // NU
                tt, kv, sbk = BLOCKS[g % NU]
                pe.wait_ge(probs_ready, g + 1)
                if (kv % 4, sbk) == (0, 0) and g >= 1:
                    pe.wait_ge(oT_ready, ENDS[max(e for e in ENDS if e < g + LAG)] + 1)
                pe.matmul(po[32 * (kv % 4):32 * (kv % 4) + 32, :], V[b % 3][:, sbk, kv, :], probs[g % SB][:, :],
                          start=(sbk == 0), stop=(sbk == tt)).then_inc(pv_done, 1)

            def tail(g):
                if g - 1 in ENDS:
                    q = ENDS[g - 1]
                    pe.wait_ge(oT_ready, q + 1)
                    if q >= 2 and q % 2 == 0:
                        pe.wait_ge(x_ready, q // 2)
                    if q % 2 == 1:
                        pe.wait_ge(y_ready, q)
                    for i in range(REP):
                        mm = pe.transpose(ot[:, i * P:(i + 1) * P], oT[:, i, :], ident)
                    mm.then_inc(o_in_psum, 1)
                if ENDS.get(g - 2, 0) % 2:
                    t = ENDS[g - 2] // 2
                    pe.wait_ge(y_ready, 2 * t + 2)
                    flat = y[:, t % TS, :, :, :].rearrange("p h i d -> p (h i d)")
                    for k in range(KD):
                        mm = pe.transpose(ot[:, k * P:(k + 1) * P], flat[:, k * P:(k + 1) * P], ident)
                    mm.then_inc(yT_in_psum, 1)
                if ENDS.get(g - 3, 0) % 2:
                    t = ENDS[g - 3] // 2
                    pe.wait_ge(yT_ready, t + 1)
                    for k in range(KD):
                        mm = pe.matmul(ot[:, 0:D], yT[:, k, :], W["wo"][:, k, :], start=(k == 0), stop=(k == KD - 1))
                    mm.then_inc(wo_in_psum, 1)

            for g in SLOTS:
                if 0 <= g < B * NU:
                    scores(g)
                for n in GO[g][:1]:
                    front(n)
                if 0 <= g - LAG < B * NU:
                    weigh(g - LAG)
                for n in GO[g][1:]:
                    front(n)
                tail(g)



D_IN, HEADS, PD, NS, TAPS = 512, 64, 8, 128, 4
Q = 32
CB_ = D_IN // P
NB = CB_ + 2
NCH = L // Q
CPT = P // Q
HG = HEADS // CPT
PAD = TAPS - 1


def ssd_stage(nc, x, W, tag, load):
    with ExitStack() as ctx:
        def sb(name, shape, dt=F32):
            return ctx.enter_context(nc.sbuf_tensor(tag + name, shape, dt))

        def ps(name, shape, dt=F32):
            return ctx.enter_context(nc.psum_tensor(tag + name, shape, dt))

        def sem(name):
            return ctx.enter_context(nc.semaphore(tag + name))

        C = W["consts"]
        stats = sb("stats", [P, NT, 6])
        meanvar = sb("meanvar", [P, NT, 2])
        rstd = sb("rstd", [P, NT])
        vareps = sb("vareps", [P, NT])
        xnT = sb("xnT", [P, KD, TOK])
        raw = sb("raw", [P, NB, PAD + L])
        conv = sb("conv", [P, NB, L])
        xT, BT = conv[:, 0:CB_, :], conv[:, CB_, :]
        CT = [sb(f"CT{i}", [P, L]) for i in range(2)]
        gates = sb("gates", [P, 2, TS, D_IN])
        gate = [gates[:, i, :, :] for i in range(2)]
        dt = sb("dt", [P, NT, HEADS])
        dA = sb("dA", [P, NT, HEADS])
        dAq = sb("dAq", [P, B * NCH, HG])
        decays = sb("decays", [P, 2, NT, HEADS])
        chdec = sb("chdec", [P, CPT, NT, HEADS])
        cbm = [sb(f"cbm{i}", [P, NCH, Q]) for i in range(2)]
        xdt = sb("xdt", [P, D_IN])
        xdec = [sb(f"xdec{i}", [P, D_IN]) for i in range(3)]
        xD = [sb(f"xD{i}", [P, D_IN]) for i in range(3)]
        xbd = [W["spare"][:, i, :].rearrange("p (c g f d) -> p c g f d", c=CPT, g=HG, f=CPT) for i in range(3)]
        Bz = [sb(f"Bz{i}", [P, CPT, NS]) for i in range(3)]
        spread = [sb(f"spread{i}", [P, HG, Q]) for i in range(2)]
        mix = [sb(f"mix{i}", [P, HG, Q]) for i in range(2)]
        S = [sb(f"S{i}", [P, D_IN]) for i in range(2)]
        Sd = sb("Sd", [P, D_IN])
        y1 = sb("y1", [P, D_IN])
        y2 = sb("y2", [P, D_IN])
        sq = sb("sq", [P, 1])
        msq = sb("msq", [P, 1])
        rms = sb("rms", [P, 1])
        yT = sb("yT", [P, CB_, P])
        Arow = sb("Arow", [P, HEADS])
        negA = sb("negA", [P, HEADS])
        wo = W["ssd_out"]
        zerob = sb("zerob", [P, 512], BF16)
        xn = gates[:, :, :, :].rearrange("p i t (u n) -> p (i t u) n", n=D)
        dtabs, dtpos, dtT = y1, y2, Sd

        pf = [ps(f"pf{i}", [P, 512]) for i in range(2)]
        pseg = [ps(f"pseg{i}", [P, 512]) for i in range(2)]
        pst = ps("pst", [P, 512])
        pyd = ps("pyd", [P, 512])
        pyo = ps("pyo", [P, 512])
        pz = ps("pz", [P, 512])

        dve_done = sem("dve_done")
        act_done = sem("act_done")
        prepared = sem("prepared")
        var_ready = sem("var_ready")
        rstd_ready = sem("rstd_ready")
        xn_ready = sem("xn_ready")
        front_in_psum = sem("front_in_psum")
        taken = {"act": sem("taken_by_act"), "dve": sem("taken_by_dve")}
        conv_ready = sem("conv_ready")
        channels_ready = sem("channels_ready")
        soft_ready = sem("soft_ready")
        dtT_ready = sem("dtT_ready")
        dA_ready = sem("dA_ready")
        dAq_ready = sem("dAq_ready")
        xbd_ready = sem("xbd_ready")
        xdt_ready = sem("xdt_ready")
        spread_ready = sem("spread_ready")
        seg_ready = sem("seg_ready")
        exp_ready = sem("exp_ready")
        mix_ready = sem("mix_ready")
        state_in_psum = sem("state_in_psum")
        decayed = sem("decayed")
        state_ready = sem("state_ready")
        yoff_done = sem("yoff_done")
        ydiag_done = sem("ydiag_done")
        y_taken = sem("y_taken")
        y_ready = sem("y_ready")
        sq_ready = sem("sq_ready")
        msq_ready = sem("msq_ready")
        rms_ready = sem("rms_ready")
        yT_in_psum = sem("yT_in_psum")
        yT_ready = sem("yT_ready")
        out_in_psum = sem("out_in_psum")
        x_ready = sem("x_ready")
        wo_ready = sem("wo_ready")

        SEQ = ([("xnT", 0, q, "act", -1) for q in range(NT // 2)] + [("dtT", 0, 0, "act", -1)]
               + [("conv", 0, i, "act", -1) for i in range(NB // 2)] + [("dt", 0, 0, "dve", -1)]
               + [("gate", 0, t, "act", -1) for t in range(TS)] + [("decays", 0, w, "act", -1) for w in range(2)]
               + [("chdec", 0, c4, "act", -1) for c4 in range(CPT)] + [("cb", 0, 0, "dve", -1)]
               + [(kind, 0, t, who, -1) for t in range(TS) for kind, who in (("xtok", "dve"), ("btok", "act"))])
        for nb in range(1, B):
            first = (nb - 1) * NCH
            SEQ += ([("conv", nb, i, "act", first + i // 2) for i in range(NB // 2)] + [("gate", nb, t, "act", first + 3) for t in range(TS)]
                    + [("cb", nb, 0, "dve", first + 4)]
                    + [(kind, nb, t, who, first + 5 + t) for t in range(TS) for kind, who in (("xtok", "dve"), ("btok", "act"))])
        GO = {g: [n for n, f in enumerate(SEQ) if f[4] == g] for g in range(-1, B * NCH + 4)}

        def take_no(n):
            who = SEQ[n][3]
            return taken[who], sum(f[3] == who for f in SEQ[:n + 1])

        def place(kind, b, t=0):
            return next(n for n, f in enumerate(SEQ) if f[:3] == (kind, b, t))

        NG = B * NCH
        SLOTS = range(-1, NG + 4)

        def tile_at(g, after):
            T = (g - after) // CPT - 1
            return T if (g - after) % CPT == 0 and 0 <= T < NT else None

        block = ctx.enter_context(nc.Block())

        @block.sync
        def _(sp):
            load(sp)

        @block.gpsimd
        def _(pool):
            pool.memset(raw[:, :, 0:PAD], 0.0).then_inc(prepared, 1)
            pool.memset(zerob[:, :], 0.0).then_inc(prepared, 1)
            pool.wait_ge(W["loaded"]["common"], 16)
            pool.wait_ge(var_ready, 1)
            pool.tensor_tensor(rstd[:, :], vareps[:, :], C["minus_half"], ALU.pow).then_inc(rstd_ready, 1)
            for i in range(3):
                pool.memset(xbd[i], 0.0).then_inc(prepared, 1)
                pool.memset(Bz[i][:, :, :], 0.0).then_inc(prepared, 1)
            pool.wait_ge(W["loaded"]["for_ssd"], 16)
            pool.wait_ge(dAq_ready, 1)
            for g in SLOTS:
                if 0 <= g < NG:
                    if g >= 2:
                        pool.wait_ge(seg_ready, g - 1)
                    pool.tensor_tensor(spread[g % 2][:, :, :], dAq[:, g, :].unsqueeze(2).broadcast_to([P, HG, Q]),
                                       C["tri"].unsqueeze(1).broadcast_to([P, HG, Q]), ALU.mult).then_inc(spread_ready, 1)
                g1 = g - 1
                if 0 <= g1 < NG and 1 <= g1 % NCH < NCH - 1:
                    b, c = g1 // NCH, g1 % NCH
                    pool.wait_ge(state_ready, b * (NCH - 1) + c)
                    dec = chdec[:, c % CPT, g1 // CPT, :].unsqueeze(2).broadcast_to([P, HEADS, PD])
                    pool.tensor_tensor(Sd[:, :].rearrange("p (h d) -> p h d", d=PD), S[c % 2][:, :].rearrange("p (h d) -> p h d", d=PD),
                                       dec, ALU.mult).then_inc(decayed, 1)
                T = tile_at(g, 2)
                if T is not None:
                    pool.wait_ge(msq_ready, T + 1)
                    pool.tensor_tensor(rms[:, :], msq[:, :], C["minus_half"][:, 0:1], ALU.pow).then_inc(rms_ready, 1)

        @block.vector
        def _(dve):
            own = Steps()
            dve.memset(W["zeros"], 0.0).then_inc(W["zeros_ready"], 1)
            for t in range(NT):
                if t % 2 == 0:
                    dve.wait_ge(W["loaded"]["x"][t // 2], 16)
                dve.bn_stats(stats[:, t, :], x[:, t, :]).then_inc(dve_done, own.step())
            dve.wait_ge(dve_done, own.n)
            for t in range(NT):
                dve.bn_aggr(meanvar[:, t, :], stats[:, t, :]).then_inc(dve_done, own.step())
            dve.wait_ge(dve_done, own.n)
            dve.tensor_scalar(vareps[:, :], meanvar[:, :, 1], EPS, None, ALU.add).then_inc(var_ready, 1)
            dve.wait_ge(rstd_ready, 1)
            for t in range(NT):
                dve.tensor_scalar(xn[:, t, :], x[:, t, :], meanvar[:, t, 0:1], rstd[:, t:t + 1],
                                  ALU.subtract, ALU.mult).then_inc(xn_ready, 1)
            dve.wait_ge(act_done, 1)
            dve.tensor_scalar(negA[:, :], Arow[:, :], -1.0, None, ALU.mult).then_inc(dve_done, own.step())
            dve.wait_ge(dve_done, own.n)
            dve.wait_ge(W["loaded"]["for_ssd"], 16)
            dve.wait_ge(prepared, 8)

            def front(n):
                kind, b, t = SEQ[n][:3]
                src = pf[n % 2]
                if kind == "dtT":
                    dve.wait_ge(soft_ready, 1)
                    dve.tensor_tensor(dtT[:, :], dtT[:, :], dtpos[:, :], ALU.add).then_inc(dtT_ready, 1)
                if kind == "conv":
                    dve.wait_ge(*take_no(n))
                    for i in range(PAD):
                        for m in (2 * t, 2 * t + 1):
                            ins = dve.scalar_tensor_tensor(conv[:, m, :], raw[:, m, i:i + L], C["conv_w"][:, m * TAPS + i:m * TAPS + i + 1],
                                                           conv[:, m, :], ALU.mult, ALU.add)
                            if i < PAD - 1:
                                ins.then_inc(dve_done, own.step())
                            else:
                                ins.then_inc(conv_ready, 1)
                        if i < PAD - 1:
                            dve.wait_ge(dve_done, own.n)
                if kind == "dt":
                    dve.wait_ge(front_in_psum, n + 1)
                    dve.tensor_copy(dt[:, :, :].rearrange("p (u k) h -> p k u h", u=2),
                                    src[:, :].rearrange("p (k u h) -> p k u h", u=2, h=HEADS)).then_inc(take_no(n)[0], 1)
                    dve.wait_ge(*take_no(n))
                    dve.tensor_tensor(dA[:, :, :], dt[:, :, :], negA[:, :].unsqueeze(1).broadcast_to([P, NT, HEADS]), ALU.mult).then_inc(dA_ready, 1)
                    dve.wait_ge(dA_ready, 1)
                    for c4 in range(CPT):
                        for h4 in range(CPT):
                            ins = dve.tensor_copy(dAq[Q * h4:Q * h4 + Q, c4::CPT, :],
                                                  dA[Q * c4:Q * c4 + Q, :, h4::CPT])
                            if (c4, h4) != (CPT - 1, CPT - 1):
                                ins.then_inc(dve_done, own.step())
                    ins.then_inc(dAq_ready, 1)
                if kind == "cb":
                    dve.wait_ge(front_in_psum, n + 1)
                    for c4 in range(CPT):
                        for h4 in range(CPT):
                            ins = dve.tensor_tensor(cbm[b % 2][Q * h4:Q * h4 + Q, c4::CPT, :],
                                                    src[Q * c4:Q * c4 + Q, 0:L].rearrange("p (t n) -> p t n", n=P)[:, :, Q * c4:Q * c4 + Q],
                                                    C["tri"][Q * c4:Q * c4 + Q, :].unsqueeze(1).broadcast_to([Q, TS, Q]), ALU.mult)
                            if (c4, h4) != (CPT - 1, CPT - 1):
                                ins.then_inc(dve_done, own.step())
                    ins.then_inc(take_no(n)[0], 1)
                if kind == "xtok":
                    T = TS * b + t
                    dve.wait_ge(front_in_psum, n + 1)
                    xt = src[:, :].rearrange("p (h d) -> p h d", d=PD)
                    if T >= 1:
                        dve.wait_ge(xbd_ready, T)
                    dve.tensor_tensor(xdt[:, :].rearrange("p (h d) -> p h d", d=PD), xt, dt[:, T, :].unsqueeze(2).broadcast_to([P, HEADS, PD]),
                                      ALU.mult).then_inc(xdt_ready, 1)
                    dve.tensor_tensor(xD[T % 3][:, :].rearrange("p (h d) -> p h d", d=PD), xt, C["D"].unsqueeze(2).broadcast_to([P, HEADS, PD]),
                                      ALU.mult).then_inc(take_no(n)[0], 1)
                    dve.wait_ge(xdt_ready, T + 1)
                    if T == 0:
                        dve.wait_ge(*take_no(place("decays", 0, 1)))
                    dve.tensor_tensor(xdec[T % 3][:, :].rearrange("p (h d) -> p h d", d=PD), xdt[:, :].rearrange("p (h d) -> p h d", d=PD),
                                      decays[:, 1, T, :].unsqueeze(2).broadcast_to([P, HEADS, PD]), ALU.mult).then_inc(dve_done, own.step())
                    src4 = xdt[:, :].rearrange("p (g f d) -> p g f d", f=CPT, d=PD)
                    for c4 in range(CPT):
                        for h4 in range(CPT):
                            ins = dve.tensor_copy(xbd[T % 3][Q * h4:Q * h4 + Q, c4, :, h4, :], src4[Q * c4:Q * c4 + Q, :, h4, :])
                            if (c4, h4) != (CPT - 1, CPT - 1):
                                ins.then_inc(dve_done, own.step())
                    ins.then_inc(xbd_ready, 1)

            for g in SLOTS:
                if g == 0:
                    dve.wait_ge(W["loaded"]["ssd_out"], 16)
                    for k in range(CB_):
                        ins = dve.tensor_scalar(wo[:, k, :], wo[:, k, :], C["norm_w"][:, k:k + 1], None, ALU.mult)
                        if k < CB_ - 1:
                            ins.then_inc(dve_done, own.step())
                    ins.then_inc(wo_ready, 1)
                g1 = g - 1
                if 0 <= g1 < NG and g1 % NCH < NCH - 1:
                    b, c = g1 // NCH, g1 % NCH
                    no = b * (NCH - 1) + c + 1
                    dve.wait_ge(state_in_psum, no)
                    if g1 >= 1:
                        dve.wait_ge(yoff_done, g1)
                    if c == 0:
                        if b >= 1:
                            dve.wait_ge(decayed, b * (NCH - 2))
                        dve.tensor_copy(S[1][:, :], pst[:, :]).then_inc(state_ready, 1)
                    else:
                        dve.wait_ge(decayed, b * (NCH - 2) + c)
                        dve.tensor_tensor(S[(c + 1) % 2][:, :], Sd[:, :], pst[:, :], ALU.add).then_inc(state_ready, 1)
                if 0 <= g < NG:
                    b, c = g // NCH, g % NCH
                    dve.wait_ge(exp_ready, g + 1)
                    dve.tensor_tensor(mix[g % 2][:, :, :], mix[g % 2][:, :, :], cbm[b % 2][:, c, :].unsqueeze(1).broadcast_to([P, HG, Q]),
                                      ALU.mult).then_inc(mix_ready, 1)
                T = tile_at(g, 0)
                if T is not None:
                    b, t = T // TS, T % TS
                    dve.wait_ge(ydiag_done, CPT * (T + 1))
                    if T >= 1:
                        dve.wait_ge(yT_in_psum, T)
                        dve.wait_ge(sq_ready, T)
                    dve.tensor_tensor(y1[:, :].rearrange("p (h d) -> p h d", d=PD), pyo[:, :].rearrange("p (h d) -> p h d", d=PD),
                                      decays[:, 0, T, :].unsqueeze(2).broadcast_to([P, HEADS, PD]), ALU.mult).then_inc(dve_done, own.step())
                    dve.tensor_tensor(y2[:, :], xD[T % 3][:, :], pyd[:, :], ALU.add).then_inc(y_taken, 1)
                    dve.wait_ge(dve_done, own.n)
                    dve.wait_ge(y_taken, T + 1)
                    dve.tensor_tensor(y1[:, :], y1[:, :], y2[:, :], ALU.add).then_inc(dve_done, own.step())
                    dve.wait_ge(dve_done, own.n)
                    dve.tensor_tensor(y1[:, :], y1[:, :], gate[b % 2][:, t, :], ALU.mult).then_inc(y_ready, 1)
                T = tile_at(g, 2)
                if T is not None:
                    dve.wait_ge(sq_ready, T + 1)
                    dve.tensor_scalar(msq[:, :], sq[:, :], 1.0 / D_IN, EPS, ALU.mult, ALU.add).then_inc(msq_ready, 1)
                T = tile_at(g, 3)
                if T is not None:
                    dve.wait_ge(out_in_psum, T + 1)
                    dve.wait_ge(rms_ready, T + 1)
                    dve.scalar_tensor_tensor(x[:, T, :], pz[:, 0:D], rms[:, 0:1], x[:, T, :], ALU.mult, ALU.add).then_inc(x_ready, 1)
                    dve.wait_ge(x_ready, T + 1)
                    dve.bn_stats(W["stats"][:, T, :], x[:, T, :]).then_inc(dve_done, own.step())
                    dve.wait_ge(dve_done, own.n)
                    dve.bn_aggr(W["meanvar"][:, T, :], W["stats"][:, T, :]).then_inc(dve_done, own.step())
                for n in GO[g]:
                    front(n)

        @block.scalar
        def _(act):
            own = Steps()
            act.wait_ge(W["loaded"]["for_ssd"], 16)
            act.activation(Arow[:, :], C["A_log"], ACT.Exp).then_inc(act_done, own.step())

            def front(n):
                kind, b, t, who, _ = SEQ[n]
                src = pf[n % 2]
                if who == "act":
                    act.wait_ge(front_in_psum, n + 1)
                    tk = take_no(n)[0]
                if kind == "xnT":
                    act.activation(xnT[:, :, t * L:(t + 1) * L], src[:, :].rearrange("p (k n) -> p k n", k=KD), ACT.Copy).then_inc(tk, 1)
                if kind == "dtT":
                    act.activation(dtabs[:, :], src[:, :], ACT.Abs, bias=C["dt_bias"]).then_inc(act_done, own.step())
                    act.activation(dtpos[:, :], src[:, :], ACT.Relu, bias=C["dt_bias"]).then_inc(tk, 1)
                    act.wait_ge(act_done, own.n)
                    act.activation(dtabs[:, :], dtabs[:, :], ACT.Exp, scale=-1.0).then_inc(act_done, own.step())
                    act.wait_ge(act_done, own.n)
                    act.activation(dtT[:, :], dtabs[:, :], ACT.Ln, bias=1.0).then_inc(soft_ready, 1)
                if kind == "conv":
                    s3 = src[:, :].rearrange("p (m n) -> p m n", m=2)
                    if b >= 1:
                        act.wait_ge(conv_ready, NB * b)
                        act.wait_ge(channels_ready, NB * b)
                        act.wait_ge(front_in_psum, place("btok", b - 1, TS - 1) + 1)
                    for i in range(2):
                        m = 2 * t + i
                        act.activation(conv[:, m, :], s3[:, i, :], ACT.Identity, bias=C["conv_b"][:, m:m + 1],
                                       scale=C["conv_w"][:, m * TAPS + PAD:m * TAPS + PAD + 1]).then_inc(act_done, own.step())
                    act.activation(raw[:, 2 * t:2 * t + 2, PAD:], s3, ACT.Copy).then_inc(tk, 1)
                    act.wait_ge(act_done, own.n)
                if kind == "gate":
                    act.activation(gate[b % 2][:, t, :], src[:, :], ACT.Silu).then_inc(tk, 1)
                    if t == 1:
                        for m in range(NB):
                            act.wait_ge(conv_ready, NB * b + m + 1)
                            dst = conv[:, m, :] if m <= CB_ else CT[b % 2][:, :]
                            act.activation(dst, conv[:, m, :], ACT.Silu).then_inc(channels_ready, 1)
                if kind == "decays":
                    act.activation(decays[:, t, :, :], src[:, :].rearrange("p (t h) -> p t h", t=NT), ACT.Exp).then_inc(tk, 1)
                if kind == "chdec":
                    act.activation(chdec[:, t, :, :], src[:, :].rearrange("p (t h) -> p t h", t=NT), ACT.Exp).then_inc(tk, 1)
                if kind == "btok":
                    T = TS * b + t
                    act.wait_ge(prepared, 8)
                    for c4 in range(CPT):
                        rows = slice(Q * c4, Q * c4 + Q)
                        ins = act.activation(Bz[T % 3][rows, c4, :], src[rows, 0:NS], ACT.Copy)
                        if c4 < CPT - 1:
                            ins.then_inc(act_done, own.step())
                    ins.then_inc(tk, 1)

            for g in SLOTS:
                if 0 <= g < NG:
                    act.wait_ge(seg_ready, g + 1)
                    if g >= 2:
                        act.wait_ge(ydiag_done, g - 1)
                    act.activation(mix[g % 2][:, :, :], pseg[g % 2][:, :].rearrange("p (h t) -> p h t", t=Q), ACT.Exp).then_inc(exp_ready, 1)
                T = tile_at(g, 1)
                if T is not None:
                    act.wait_ge(y_ready, T + 1)
                    if T >= 1:
                        act.wait_ge(msq_ready, T)
                    act.activation(y2[:, :], y1[:, :], ACT.Square, accum_out=sq[:, :]).then_inc(sq_ready, 1)
                T = tile_at(g, 2)
                if T is not None:
                    act.wait_ge(yT_in_psum, T + 1)
                    act.activation(yT[:, :, :], pz[:, :].rearrange("p (k n) -> p k n", k=CB_), ACT.Copy).then_inc(yT_ready, 1)
                for n in GO[g]:
                    front(n)

        @block.tensor
        def _(pe):
            ident = C["ident"]
            pe.wait_ge(W["loaded"]["common"], 16)

            def front(n):
                kind, b, t = SEQ[n][:3]
                dst = pf[n % 2]
                if n >= 2:
                    pe.wait_ge(*take_no(n - 2))
                if kind == "xnT":
                    for r in range(2):
                        pe.wait_ge(xn_ready, 2 * t + r + 1)
                        for k in range(KD):
                            mm = pe.transpose(dst[:, k * L + r * P:k * L + (r + 1) * P], xn[:, 2 * t + r, k * P:(k + 1) * P], ident)
                if kind == "dtT":
                    pe.wait_ge(W["loaded"]["ssd_in"], 16)
                    pe.wait_ge(*take_no(place("xnT", 0, NT // 2 - 1)))
                    for u in range(2):
                        for k in range(KD):
                            mm = pe.matmul(dst[u * HEADS:(u + 1) * HEADS, :], W["ssd_in"][:, k, D_IN + NB * P:], xnT[:, k, u * 512:(u + 1) * 512],
                                           start=(k == 0), stop=(k == KD - 1))
                if kind == "conv":
                    for i in range(2):
                        m = 2 * t + i
                        for k in range(KD):
                            mm = pe.matmul(dst[:, i * L:(i + 1) * L], W["ssd_in"][:, k, D_IN + m * P:D_IN + (m + 1) * P], xnT[:, k, b * L:(b + 1) * L],
                                           start=(k == 0), stop=(k == KD - 1))
                if kind == "gate":
                    for k in range(KD):
                        mm = pe.matmul(dst[:, :], xnT[:, k, (TS * b + t) * P:(TS * b + t + 1) * P], W["ssd_in"][:, k, 0:D_IN],
                                       start=(k == 0), stop=(k == KD - 1))
                if kind == "dt":
                    pe.wait_ge(dtT_ready, 1)
                    for q in range(NT // 2):
                        mm = pe.transpose(dst[:, q * P:(q + 1) * P], dtT[:, q * P:(q + 1) * P], ident)
                if kind in ("decays", "chdec"):
                    pe.wait_ge(W["loaded"]["for_ssd"], 16)
                    pe.wait_ge(dA_ready, 1)
                    lhsT = C["rows_of"][:, t * P:(t + 1) * P] if kind == "chdec" else C[("upto_t", "behind")[t]]
                    mm = pe.matmul(dst[:, :], lhsT, dA[:, :, :].rearrange("p t h -> p (t h)"), start=True, stop=True)
                if kind == "cb":
                    pe.wait_ge(channels_ready, NB * (b + 1))
                    for q in range(TS):
                        mm = pe.matmul(dst[:, q * P:(q + 1) * P], BT[:, q * P:(q + 1) * P], CT[b % 2][:, q * P:(q + 1) * P], start=True, stop=True)
                if kind == "xtok":
                    for k in range(CB_):
                        mm = pe.transpose(dst[:, k * P:(k + 1) * P], xT[:, k, t * P:(t + 1) * P], ident)
                if kind == "btok":
                    mm = pe.transpose(dst[:, 0:NS], BT[:, t * P:(t + 1) * P], ident)
                mm.then_inc(front_in_psum, 1)

            for g in SLOTS:
                if 0 <= g < NG:
                    pe.wait_ge(spread_ready, g + 1)
                    if g >= 2:
                        pe.wait_ge(exp_ready, g - 1)
                    pe.matmul(pseg[g % 2][:, :], C["behind"], spread[g % 2][:, :, :].rearrange("p h t -> p (h t)"), start=True, stop=True).then_inc(seg_ready, 1)
                g1 = g - 1
                if 0 <= g1 < NG:
                    b, c = g1 // NCH, g1 % NCH
                    T, c4 = g1 // CPT, c % CPT
                    if c < NCH - 1:
                        no = b * (NCH - 1) + c
                        if c4 == 0:
                            pe.wait_ge(*take_no(place("btok", b, T % TS)))
                            pe.wait_ge(xbd_ready, T + 1)
                        if no >= 1:
                            pe.wait_ge(state_ready, no)
                        pe.matmul(pst[:, :], Bz[T % 3][:, c4, :], xdec[T % 3][:, :], start=True, stop=True).then_inc(state_in_psum, 1)
                for n in GO[g]:
                    front(n)
                if 0 <= g1 < NG:
                    if c4 == 0 and T >= 1:
                        pe.wait_ge(y_taken, T)
                    rows = slice(Q * c4, Q * c4 + Q)
                    if c == 0:
                        pe.wait_ge(prepared, 2)
                        pe.matmul(pyo[rows, :], zerob[:, 0:Q], zerob[:, :], start=True, stop=True).then_inc(yoff_done, 1)
                    else:
                        pe.wait_ge(state_ready, b * (NCH - 1) + c)
                        pe.matmul(pyo[rows, :], CT[b % 2][:, c * Q:(c + 1) * Q], S[c % 2][:, :], start=True, stop=True).then_inc(yoff_done, 1)
                    pe.wait_ge(mix_ready, g1 + 1)
                    for h in range(HG):
                        mm = pe.matmul(pyd[rows, h * Q:(h + 1) * Q], mix[g1 % 2][:, h, :], xbd[T % 3][:, c4, h, :, :].rearrange("p f d -> p (f d)"),
                                       start=True, stop=True)
                    mm.then_inc(ydiag_done, 1)
                T = tile_at(g, 1)
                if T is not None:
                    pe.wait_ge(y_ready, T + 1)
                    if T >= 1:
                        pe.wait_ge(x_ready, T)
                    for k in range(CB_):
                        mm = pe.transpose(pz[:, k * P:(k + 1) * P], y1[:, k * P:(k + 1) * P], ident)
                    mm.then_inc(yT_in_psum, 1)
                T = tile_at(g, 2)
                if T is not None:
                    pe.wait_ge(wo_ready, 1)
                    pe.wait_ge(yT_ready, T + 1)
                    for k in range(CB_):
                        mm = pe.matmul(pz[:, 0:D], yT[:, k, :], wo[:, k, :], start=(k == 0), stop=(k == CB_ - 1))
                    mm.then_inc(out_in_psum, 1)


COMMON = [("ident", P), ("ones", P), ("below", P), ("minus_half", NT), ("weigh", NT * E), ("steps", E * NT),
          ("upto", E * E), ("tile_no", NR * E)]
FOR_SSD = [("tri", Q), ("behind", P), ("upto_t", P), ("rows_of", CPT * P), ("A_log", HEADS), ("D", HEADS), ("dt_bias", 1),
           ("conv_w", NB * TAPS), ("conv_b", NB), ("norm_w", CB_)]
FOR_ATT = [("hide", P), ("cos", TS * QK), ("sin", TS * QK)]


LATE = 3


def views(buffer, fields):
    got, at = {}, 0
    for name, width in fields:
        got[name] = buffer[:, at:at + width]
        at += width
    return got


def width_of(fields):
    return sum(width for _, width in fields)


def hybrid_layer(nc, hidden, ssd_in, ssd_out, qkv, wo, gate_up, down, router, common, for_ssd, for_att, out):
    slots_x = nc.dram_tensor("slots_x", [NR * P, D], F32).ap()
    slots_y = nc.dram_tensor("slots_y", [NR * P, D], F32).ap()
    with ExitStack() as ctx:
        def sb(stack, name, shape):
            return stack.enter_context(nc.sbuf_tensor(name, shape, F32))

        def sem(name):
            return ctx.enter_context(nc.semaphore(name))

        x = sb(ctx, "x", [P, NT, D])
        common_sb = sb(ctx, "common_sb", [P, width_of(COMMON)])
        router_sb = sb(ctx, "router_sb", [P, KD, E])
        gate_up_sb = sb(ctx, "gate_up_sb", [P, E + 1, KD, 2 * FI])
        loaded = {name: sem(name + "_loaded") for name in ("common", "for_ssd", "ssd_in", "ssd_out")}
        loaded["x"] = [sem(f"x_loaded{i}") for i in range(NT // 2)]
        zeros_ready = sem("zeros_ready")
        slots_cleared = sem("slots_cleared")
        expert_loads = sem("expert_loads")
        late_loads = [sem("shared_down_load"), sem("routed_loads")]
        att_loads = sem("att_loads")

        C = views(common_sb, COMMON)
        for name, inner in (("weigh", E), ("steps", NT), ("upto", E)):
            C[name] = C[name].rearrange("p (a b) -> p a b", b=inner)
        C["tile_no"] = C["tile_no"][0:1, :].rearrange("p (a b) -> p a b", b=E)
        stats_sb = sb(ctx, "stats_sb", [P, NT, 6])
        meanvar_sb = sb(ctx, "meanvar_sb", [P, NT, 2])
        norm = dict(stats=stats_sb, meanvar=meanvar_sb)
        W = dict(**norm, consts=C, slots_x=slots_x, slots_y=slots_y, gate_up=gate_up_sb, router=router_sb)

        with ExitStack() as ssd_ctx:
            ssd_in_sb = sb(ssd_ctx, "ssd_in_sb", [P, KD, D_IN + NB * P + HEADS])
            ssd_out_sb = sb(ssd_ctx, "ssd_out_sb", [P, CB_, D])
            for_ssd_sb = sb(ssd_ctx, "for_ssd_sb", [P, width_of(FOR_SSD)])
            zeros = sb(ssd_ctx, "zeros", [P, D])

            def load_first(sp):
                for i in range(NT // 2):
                    sp.dma_start(x[:, 2 * i:2 * i + 2, :], hidden[:, 2 * i:2 * i + 2, :]).then_inc(loaded["x"][i], 16)
                    if i == 0:
                        sp.dma_start(common_sb[:, :], common).then_inc(loaded["common"], 16)
                sp.dma_start(ssd_in_sb[:, :, :], ssd_in).then_inc(loaded["ssd_in"], 16)
                sp.dma_start(for_ssd_sb[:, :], for_ssd).then_inc(loaded["for_ssd"], 16)
                sp.dma_start(ssd_out_sb[:, :, :], ssd_out).then_inc(loaded["ssd_out"], 16)
                sp.wait_ge(zeros_ready, 1)
                sp.dma_start(slots_x.rearrange("(t p) n -> p t n", p=P),
                             zeros[:, :].unsqueeze(1).broadcast_to([P, NR, D])).then_inc(slots_cleared, 16)
                sp.dma_start(router_sb[:, :, :], router).then_inc(expert_loads, 16)
                sp.dma_start(gate_up_sb[:, LATE:, :, :], gate_up[:, LATE:, :, :]).then_inc(expert_loads, 16)

            ssd_stage(nc, x, dict(consts={**C, **views(for_ssd_sb, FOR_SSD)}, ssd_in=ssd_in_sb, ssd_out=ssd_out_sb, loaded=loaded,
                                  **norm, zeros=zeros[:, :], zeros_ready=zeros_ready,
                                  spare=gate_up_sb[:, 0:LATE, :, :].rearrange("p e k n -> p e (k n)")), "ssd_", load_first)
            with nc.Block() as block:
                @block.sync
                def _(sp):
                    sp.wait_ge(slots_cleared, 16)
                    sp.wait_ge(expert_loads, 32)

        down_sb = sb(ctx, "down_sb", [P, E + 1, KF, D])
        qkv_sb = sb(ctx, "qkv_sb", [P, KD, QKV])
        wo_sb = sb(ctx, "wo_sb", [P, KD, D])
        for_att_sb = sb(ctx, "for_att_sb", [P, width_of(FOR_ATT)])
        att = views(for_att_sb, FOR_ATT)
        for name in ("cos", "sin"):
            att[name] = att[name].rearrange("p (t n) -> p t n", t=TS)
        W["down"] = down_sb

        def load_behind(sp):
            sp.dma_start(down_sb[:, E, :, :], down[:, E, :, :]).then_inc(late_loads[0], 16)
            sp.dma_start(gate_up_sb[:, 0:LATE, :, :], gate_up[:, 0:LATE, :, :]).then_inc(late_loads[1], 16)
            sp.dma_start(down_sb[:, 0:E, :, :], down[:, 0:E, :, :]).then_inc(late_loads[1], 16)
            sp.dma_start(qkv_sb[:, :, :], qkv).then_inc(att_loads, 16)
            sp.dma_start(wo_sb[:, :, :], wo).then_inc(att_loads, 16)
            sp.dma_start(for_att_sb[:, :], for_att).then_inc(att_loads, 16)

        W["late_loads"] = late_loads
        ffn_stage(nc, x, W, "ffn1_", load_behind)
        with nc.Block() as block:
            @block.sync
            def _(sp):
                sp.wait_ge(att_loads, 48)
        attention_stage(nc, x, dict(**norm, consts={**C, **att}, qkv=qkv_sb, wo=wo_sb), "att_")
        ffn_stage(nc, x, W, "ffn2_", out=out)


def kernel(**inputs):
    import numpy as np
    import concourse.bacc as bacc
    from concourse.bass_utils import run_bass_kernel_spmd

    def given(name):
        return np.asarray(inputs["L0_" + name])

    def chunks(w, rows):
        return w.reshape(rows, P, -1).transpose(1, 0, 2)

    k = np.arange(P)
    same = k[:, None] // Q == k[None, :] // Q
    tables = {
        "ident": np.eye(P), "ones": np.ones((P, P)), "below": k[:, None] < k[None, :],
        "minus_half": np.full((P, NT), -0.5),
        "weigh": np.tile(float(E) - np.arange(E), (P, NT)),
        "steps": np.tile(float(P) * np.arange(NT), (P, E)),
        "upto": np.tile((np.arange(E)[None, :] <= np.arange(E)[:, None]).reshape(-1), (P, 1)),
        "tile_no": np.tile(np.repeat(np.arange(float(NR)), E), (P, 1)),
        "tri": k[:, None] % Q <= np.arange(Q)[None, :],
        "behind": same & (k[:, None] > k[None, :]), "upto_t": same & (k[:, None] <= k[None, :]),
        "rows_of": np.concatenate([np.tile((k[:, None] // Q == q), (1, P)) for q in range(CPT)], 1),
        "hide": np.where(k[None, :] > k[:, None], -1e30, 0.0),
    }
    theta = (1.0 / np.float32(10000.0) ** (np.arange(0, HD, 2, dtype=np.float32) / HD)).astype(np.float32)
    angle = np.arange(L, dtype=np.float32)[:, None] * theta[None, :]
    scale = np.array([HD ** -0.5] * H + [1.0] * HKV)
    for name, pair in (("cos", (np.cos(angle), np.cos(angle))), ("sin", (-np.sin(angle), np.sin(angle)))):
        table = np.stack(pair, -1).reshape(L, 1, HD) * scale[None, :, None]
        tables[name] = chunks(table.reshape(L, QK), TS).reshape(P, -1)
    tables.update({
        "A_log": np.tile(given("attn_a_A_log"), (P, 1)), "D": np.tile(given("attn_a_D"), (P, 1)),
        "dt_bias": np.tile(given("attn_a_dt_bias"), P // HEADS)[:, None],
        "conv_w": given("attn_a_conv_w").reshape(NB, P, TAPS).transpose(1, 0, 2).reshape(P, -1),
        "conv_b": given("attn_a_conv_b").reshape(NB, P).T, "norm_w": given("attn_a_norm_w").reshape(CB_, P).T,
    })

    def packed(fields):
        return np.concatenate([np.asarray(tables[name], np.float32) for name, _ in fields], 1)

    wq = given("attn_b_wq").reshape(G, HALF, REP, HD, D).transpose(0, 2, 1, 3, 4).reshape(H * HD, D)
    shared_up = np.concatenate([given("ffn_shared_gate_w"), given("ffn_shared_up_w")], 1)[None]
    gate_up = np.concatenate([given("ffn_gate_up_proj"), shared_up])
    down = np.concatenate([given("ffn_down_proj"), given("ffn_shared_down_w")[None]])
    arrays = {
        "hidden": chunks(given("attn_a_hidden_states").reshape(TOK, D), NT),
        "ssd_in": chunks(given("attn_a_in_proj_w").T, KD), "ssd_out": chunks(given("attn_a_out_proj_w").T, CB_),
        "qkv": chunks(np.concatenate([wq, given("attn_b_wk"), given("attn_b_wv")]).T, KD), "wo": chunks(given("attn_b_wo").T, KD),
        "gate_up": gate_up.reshape(E + 1, KD, P, 2 * FI).transpose(2, 0, 1, 3),
        "down": down.reshape(E + 1, KF, P, D).transpose(2, 0, 1, 3),
        "router": chunks(given("ffn_router_w").T, KD),
        "common": packed(COMMON), "for_ssd": packed(FOR_SSD), "for_att": packed(FOR_ATT),
    }
    nc = bacc.Bacc("TRN2", target_bir_lowering=False, num_devices=1)
    feed, args = {}, []
    for name, a in arrays.items():
        feed[name] = np.ascontiguousarray(a)
        args.append(nc.dram_tensor(name, feed[name].shape, mybir.dt.from_np(feed[name].dtype), kind="ExternalInput").ap())
    args.append(nc.dram_tensor("out", (P, NT, D), F32, kind="ExternalOutput").ap())
    hybrid_layer(nc, *args)
    r = run_bass_kernel_spmd(nc, [feed], core_ids=[0])
    return r.results[0]["out"].transpose(1, 0, 2).reshape(B, L, D)
```
